# Optimizing a Trainium2 kernel written in Bass

```python
import numpy as np
import jax
import jax.numpy as jnp

def _softmax(x, axis=-1):
    return jax.nn.softmax(x, axis=axis)

def _gelu(x):
    return jax.nn.gelu(x, approximate=True)

def _silu(x):
    return jax.nn.silu(x)

def _sigmoid(x):
    return jax.nn.sigmoid(x)

def _layernorm(x, axis=-1, eps=1e-05):
    m = jnp.mean(x, axis=axis, keepdims=True)
    v = jnp.var(x, axis=axis, keepdims=True)
    return (x - m) / jnp.sqrt(v + eps)

def _scatter_add(tgt, idx, src, axis=0):
    return tgt.at[idx].add(src)

def _segment_sum(src, seg, n):
    return jax.ops.segment_sum(src, seg, n)
kernel_name = 'mk_gnn_resnorm_d4_gnn_r8_2cb5a8'

def setup_inputs(seed: int=0):
    np.random.seed(seed)
    _w = jnp.asarray

    def _rec_inputs():
        import jax
        import jax.numpy as jnp
        _gk = jax.random.key(seed)
        x = -0.000202 + 1 * jax.random.normal(jax.random.fold_in(_gk, 1), (6250, 128), jnp.float32)
        _s = jax.random.randint(jax.random.fold_in(_gk, 2), (100000,), 0, 6250, jnp.int32)
        _d = jax.random.randint(jax.random.fold_in(_gk, 3), (100000,), 0, 6250, jnp.int32)
        _loop = jnp.arange(6250, dtype=jnp.int32)
        src = jnp.concatenate([_s, _d, _loop])
        dst = jnp.concatenate([_d, _s, _loop])
        _o = jnp.argsort(dst, stable=True)
        src = src[_o]
        dst = dst[_o]
        edge_attr_64 = -8.16379e-05 + 0.999858 * jax.random.normal(jax.random.fold_in(_gk, 12), (206250, 64), jnp.float32)
        edge_type_3 = jax.random.randint(jax.random.fold_in(_gk, 14), (206250,), 0, 3, jnp.int32)
        edge_weight = jax.random.uniform(jax.random.fold_in(_gk, 15), (206250,), jnp.float32, 0.0, 1)
        node_type_3 = jax.random.randint(jax.random.fold_in(_gk, 16), (6250,), 0, 3, jnp.int32)
        return (x, src, dst, edge_attr_64, edge_type_3, edge_weight, node_type_3)
    x, src, dst, edge_attr_64, edge_type_3, edge_weight, node_type_3 = _rec_inputs()

    def _L0_gnn_setup():
        import jax, jax.numpy as jnp
        import numpy as np
        N_NODES = 6250
        N_EDGES = 100000
        D = 128
        T = 3
        NODE_IN = D + T * D
        key = jax.random.key(seed)
        ks = jax.random.split(key, 8)
        scale = 0.05
        return {'node_feature': jax.random.normal(ks[0], (N_NODES, D), jnp.float32), 'W_e': jax.random.normal(ks[1], (T, D, D), jnp.float32) * scale, 'b_e': jnp.zeros((T, D), jnp.float32), 'W_n': jax.random.normal(ks[2], (T, D, NODE_IN), jnp.float32) * scale, 'b_n': jnp.zeros((T, D), jnp.float32), 'edge_src': jax.random.randint(ks[3], (N_EDGES,), 0, N_NODES, jnp.int32), 'edge_dst': jax.random.randint(ks[4], (N_EDGES,), 0, N_NODES, jnp.int32), 'edge_type': jax.random.randint(ks[5], (N_EDGES,), 0, T, jnp.int32), 'node_type': jax.random.randint(ks[6], (N_NODES,), 0, T, jnp.int32)}
    _L0_gnn_all = _L0_gnn_setup()
    _L0_gnn_in = {k: v for k, v in _L0_gnn_all.items() if k in ('W_e', 'b_e', 'W_n', 'b_n')}
    del _L0_gnn_all

    def _L1_gnn_setup():
        import jax, jax.numpy as jnp
        import numpy as np
        C = 1.0
        MIN_NORM = 1e-15
        PROJ_EPS = 0.004
        N_NODES = 12500
        D_IN = 128
        D_OUT = 128
        N_EDGES = 400000

        def _artanh(x):
            return jnp.arctanh(jnp.clip(x, -1.0 + 1e-07, 1.0 - 1e-07))

        def logmap0(p, c):
            sqrt_c = c ** 0.5
            p_norm = jnp.maximum(jnp.linalg.norm(p, axis=-1, keepdims=True), MIN_NORM)
            return _artanh(sqrt_c * p_norm) * p / (sqrt_c * p_norm)

        def expmap0(u, c):
            sqrt_c = c ** 0.5
            u_norm = jnp.maximum(jnp.linalg.norm(u, axis=-1, keepdims=True), MIN_NORM)
            return jnp.tanh(sqrt_c * u_norm) * u / (sqrt_c * u_norm)

        def proj(x, c):
            norm = jnp.maximum(jnp.linalg.norm(x, axis=-1, keepdims=True), MIN_NORM)
            maxnorm = (1.0 - PROJ_EPS) / c ** 0.5
            return jnp.where(norm > maxnorm, x / norm * maxnorm, x)

        def mobius_add(x, y, c):
            x2 = jnp.sum(x * x, axis=-1, keepdims=True)
            y2 = jnp.sum(y * y, axis=-1, keepdims=True)
            xy = jnp.sum(x * y, axis=-1, keepdims=True)
            num = (1.0 + 2.0 * c * xy + c * y2) * x + (1.0 - c * x2) * y
            denom = 1.0 + 2.0 * c * xy + c * c * x2 * y2
            return num / jnp.maximum(denom, MIN_NORM)
        key = jax.random.key(seed)
        k1, k2, k3, k4, k5 = jax.random.split(key, 5)
        x = proj(0.05 * jax.random.normal(k1, (N_NODES, D_IN), dtype=jnp.float32), C)
        lim = float(np.sqrt(6.0 / (D_IN + D_OUT)))
        weight = jax.random.uniform(k2, (D_IN, D_OUT), jnp.float32, -lim, lim)
        bias = 0.01 * jax.random.normal(k3, (D_OUT,), dtype=jnp.float32)
        edge_index = jax.random.randint(k4, (2, N_EDGES), 0, N_NODES, dtype=jnp.int64)
        edge_weight = jax.random.uniform(k5, (N_EDGES,), jnp.float32)
        return {'x': x, 'weight': weight, 'bias': bias, 'edge_index': edge_index, 'edge_weight': edge_weight}
    _L1_gnn_all = _L1_gnn_setup()
    _L1_gnn_in = {k: v for k, v in _L1_gnn_all.items() if k in ('weight', 'bias')}
    del _L1_gnn_all

    def _L2_gnn_setup():
        import jax, jax.numpy as jnp
        import numpy as np
        N_NODES = 12500
        EMB_DIM = 128
        N_EDGES = 200000
        key = jax.random.key(seed)
        k1, k2 = jax.random.split(key)
        edge_index = jax.random.randint(k1, (2, N_EDGES), 0, N_NODES, dtype=jnp.int64 if jax.config.read('jax_enable_x64') else jnp.int32)
        embedding = jax.random.normal(k2, (N_NODES, EMB_DIM), dtype=jnp.float32)
        return {'edge_index': edge_index, 'embedding': embedding}
    _L2_gnn_all = _L2_gnn_setup()
    _L2_gnn_in = {k: v for k, v in _L2_gnn_all.items() if k in ()}
    del _L2_gnn_all

    def _L3_gnn_setup():
        import jax, jax.numpy as jnp
        import numpy as np
        N_NODES = 12500
        N_EDGES = 200000
        IN_FEATS = 128
        OUT_FEATS = 128
        EDGE_HIDDEN = 64
        key = jax.random.key(seed)
        ks = jax.random.split(key, 7)
        h = jax.random.normal(ks[0], (N_NODES, IN_FEATS), dtype=jnp.float32)
        edge_feat = jax.random.normal(ks[1], (N_EDGES, EDGE_HIDDEN), dtype=jnp.float32)
        src = jax.random.randint(ks[2], (N_EDGES,), 0, N_NODES)
        dst = jax.random.randint(ks[3], (N_EDGES,), 0, N_NODES)
        stdv = 1.0 / np.sqrt(OUT_FEATS)
        stdv_e = 1.0 / np.sqrt(IN_FEATS)
        weight = jax.random.uniform(ks[4], (IN_FEATS, OUT_FEATS), minval=-stdv, maxval=stdv, dtype=jnp.float32)
        weight_edge = jax.random.uniform(ks[5], (EDGE_HIDDEN, IN_FEATS), minval=-stdv_e, maxval=stdv_e, dtype=jnp.float32)
        bias = jax.random.uniform(ks[6], (OUT_FEATS,), minval=-stdv, maxval=stdv, dtype=jnp.float32)
        return {'h': h, 'edge_feat': edge_feat, 'src': src, 'dst': dst, 'num_nodes': N_NODES, 'weight': weight, 'weight_edge': weight_edge, 'bias': bias}
    _L3_gnn_all = _L3_gnn_setup()
    _L3_gnn_in = {k: v for k, v in _L3_gnn_all.items() if k in ('weight', 'weight_edge', 'bias')}
    del _L3_gnn_all
    return {'x': x, 'src': src, 'dst': dst, 'edge_attr_64': edge_attr_64, 'edge_type_3': edge_type_3, 'edge_weight': edge_weight, 'node_type_3': node_type_3, 'L0_gnn_W_e': _L0_gnn_in['W_e'], 'L0_gnn_b_e': _L0_gnn_in['b_e'], 'L0_gnn_W_n': _L0_gnn_in['W_n'], 'L0_gnn_b_n': _L0_gnn_in['b_n'], 'L1_gnn_weight': _L1_gnn_in['weight'], 'L1_gnn_bias': _L1_gnn_in['bias'], 'L3_gnn_weight': _L3_gnn_in['weight'], 'L3_gnn_weight_edge': _L3_gnn_in['weight_edge'], 'L3_gnn_bias': _L3_gnn_in['bias']}

def reference(x, src, dst, edge_attr_64, edge_type_3, edge_weight, node_type_3, L0_gnn_W_e, L0_gnn_b_e, L0_gnn_W_n, L0_gnn_b_n, L1_gnn_weight, L1_gnn_bias, L3_gnn_weight, L3_gnn_weight_edge, L3_gnn_bias):
    import jax
    import jax.numpy as jnp

    def _L0_gnn_ref(node_feature, W_e, b_e, W_n, b_n, edge_src, edge_dst, edge_type, node_type):
        import jax, jax.numpy as jnp
        import numpy as np
        N_NODES = 6250
        N_EDGES = 100000
        D = 128
        T = 3
        NODE_IN = D + T * D
        N, Din = node_feature.shape
        n_types = W_e.shape[0]
        out_dim = W_e.shape[1]
        src = node_feature[edge_src]
        parts = [jax.nn.relu(node_feature)]
        for t in range(n_types):
            msg = jax.nn.relu(src @ W_e[t].T + b_e[t])
            msg = jnp.where((edge_type == t)[:, None], msg, jnp.zeros((), msg.dtype))
            parts.append(jax.ops.segment_sum(msg, edge_dst, num_segments=N))
        agg = jnp.concatenate(parts, axis=1)
        updated = jnp.zeros((N, out_dim), node_feature.dtype)
        for t in range(n_types):
            o = agg @ W_n[t].T + b_n[t]
            updated = jnp.where((node_type == t)[:, None], o, updated)
        return updated + node_feature

    def _L1_gnn_ref(x, weight, bias, edge_index, edge_weight):
        import jax, jax.numpy as jnp
        import numpy as np
        C = 1.0
        MIN_NORM = 1e-15
        PROJ_EPS = 0.004
        N_NODES = 12500
        D_IN = 128
        D_OUT = 128
        N_EDGES = 400000

        def _artanh(x):
            return jnp.arctanh(jnp.clip(x, -1.0 + 1e-07, 1.0 - 1e-07))

        def logmap0(p, c):
            sqrt_c = c ** 0.5
            p_norm = jnp.maximum(jnp.linalg.norm(p, axis=-1, keepdims=True), MIN_NORM)
            return _artanh(sqrt_c * p_norm) * p / (sqrt_c * p_norm)

        def expmap0(u, c):
            sqrt_c = c ** 0.5
            u_norm = jnp.maximum(jnp.linalg.norm(u, axis=-1, keepdims=True), MIN_NORM)
            return jnp.tanh(sqrt_c * u_norm) * u / (sqrt_c * u_norm)

        def proj(x, c):
            norm = jnp.maximum(jnp.linalg.norm(x, axis=-1, keepdims=True), MIN_NORM)
            maxnorm = (1.0 - PROJ_EPS) / c ** 0.5
            return jnp.where(norm > maxnorm, x / norm * maxnorm, x)

        def mobius_add(x, y, c):
            x2 = jnp.sum(x * x, axis=-1, keepdims=True)
            y2 = jnp.sum(y * y, axis=-1, keepdims=True)
            xy = jnp.sum(x * y, axis=-1, keepdims=True)
            num = (1.0 + 2.0 * c * xy + c * y2) * x + (1.0 - c * x2) * y
            denom = 1.0 + 2.0 * c * xy + c * c * x2 * y2
            return num / jnp.maximum(denom, MIN_NORM)
        c = C
        x_tangent = logmap0(x, c)
        support = x_tangent @ weight
        hyp_bias = proj(expmap0(bias[None, :], c), c)
        support = proj(mobius_add(support, hyp_bias, c), c)
        row, col = (edge_index[0], edge_index[1])
        agg = jax.ops.segment_sum(edge_weight[:, None] * support[col], row, num_segments=x.shape[0])
        return proj(expmap0(agg, c), c)

    def _L2_gnn_ref(edge_index, embedding):
        import jax, jax.numpy as jnp
        import numpy as np
        N_NODES = 12500
        EMB_DIM = 128
        N_EDGES = 200000
        N = embedding.shape[0]
        loop = jnp.arange(N, dtype=edge_index.dtype)
        row = jnp.concatenate([edge_index[0], loop])
        col = jnp.concatenate([edge_index[1], loop])
        deg = jax.ops.segment_sum(jnp.ones_like(row, dtype=embedding.dtype), row, num_segments=N)
        deg_inv_sqrt = jnp.where(deg > 0, jax.lax.rsqrt(jnp.maximum(deg, 1.0)), 0.0)
        norm = deg_inv_sqrt[row] * deg_inv_sqrt[col]
        msgs = norm[:, None] * embedding[row]
        out = jax.ops.segment_sum(msgs, col, num_segments=N)
        return out

    def _L3_gnn_ref(h, edge_feat, src, dst, num_nodes, weight, weight_edge, bias):
        import jax, jax.numpy as jnp
        import numpy as np
        N_NODES = 12500
        N_EDGES = 200000
        IN_FEATS = 128
        OUT_FEATS = 128
        EDGE_HIDDEN = 64
        eh = edge_feat @ weight_edge
        m = eh + h[src]
        agg = jax.ops.segment_sum(m, dst, num_segments=num_nodes)
        deg = jax.ops.segment_sum(jnp.ones((dst.shape[0],), dtype=h.dtype), dst, num_segments=num_nodes)
        norm = jnp.clip(deg, 1.0, None) ** (-0.5)
        agg = agg * norm[:, None]
        out = agg @ weight + bias
        return jax.nn.relu(out)
    edge_index = jnp.stack([src, dst])
    x = _layernorm(x + _L0_gnn_ref(x, L0_gnn_W_e, L0_gnn_b_e, L0_gnn_W_n, L0_gnn_b_n, src, dst, edge_type_3, node_type_3), axis=-1)
    x = _layernorm(x + _L1_gnn_ref(x, L1_gnn_weight, L1_gnn_bias, edge_index, edge_weight), axis=-1)
    x = _layernorm(x + _L2_gnn_ref(edge_index, x), axis=-1)
    x = _layernorm(x + _L3_gnn_ref(x, edge_attr_64, src, dst, 6250, L3_gnn_weight, L3_gnn_weight_edge, L3_gnn_bias), axis=-1)
    return x

_drawn_inputs = setup_inputs


def setup_inputs(seed=0):
    import zlib

    import numpy as np

    out = dict(_drawn_inputs(seed))
    spreads = {'L0_gnn_b_e': (0.0, 0.1), 'L0_gnn_b_n': (0.0, 0.1)}
    factors = {}
    for name, (base, spread) in spreads.items():
        noise = np.random.default_rng([zlib.crc32(name.encode()), seed]).standard_normal(out[name].shape)
        drawn = base * np.exp(spread * noise) if base else spread * noise
        out[name] = jnp.asarray(drawn.astype(out[name].dtype))
    for name, factor in factors.items():
        out[name] = (out[name] * factor).astype(out[name].dtype)
    return out
```

```python
from contextlib import ExitStack

import concourse.bass as bass
from concourse import mybir

F32 = mybir.dt.float32
I32 = mybir.dt.int32
ALU = mybir.AluOpType
ACT = mybir.ActivationFunctionType
AX = mybir.AxisListType

P = 128
N, E, D, T, FE = 6250, 206250, 128, 3, 64
NB = -(-N // P)
NFULL = N // P
NREST = N - NFULL * P
NP = NB * P
NO_NODE = NP

EC = E // P
EREST = E - EC * P
C = EC + 1

U, Q = 4, 4
TP = -(-((E + NB * (P - 1)) // P) // (U * Q)) * U * Q
STEPS = TP // (U * Q)
FIXED = 7
OUTSIDE = 1 << 22

SU, SQ = 13, 4
SSTEPS = C // (SU * SQ)
assert SSTEPS * SU * SQ == C

KEY0, DLOC, WGT, SRCF, SLOC, POS2, IDX0 = range(FE, FE + 7)
RW = FE + 7
NR = 5
R_DLOC, R_WGT, R_SRCF, R_SLOC, R_POS2 = range(NR)
MONE, MLOC = D, D + 1
MW = D + 2
FILL = 16
EPS = 1e-5
MIN_NORM = 1e-15
MAX_NORM = 1.0 - 0.004


def build(nc, x, src, dst, attr, etype, weight, ntype, w_e, b_e, w_n, b_n, w1, b1, w3, w3e, b3, out):
    ctx = ExitStack()
    with ctx:
        ctx.enter_context(nc.allow_non_contiguous_dma(reason="node types, leftover edges"))

        def sb(name, cols, dt=F32, rows=P):
            return ctx.enter_context(nc.sbuf_tensor(name, [rows, cols], dt))

        def sem(name):
            return ctx.enter_context(nc.semaphore(name))

        def sems(name, n):
            return [sem(f"{name}{i}") for i in range(n)]

        sorted_edges = nc.dram_tensor("sorted_edges", (P, TP * RW), F32, kind="Internal").ap()
        sorted_msgs = nc.dram_tensor("sorted_msgs", (P, TP * MW), F32, kind="Internal").ap()
        typed_msgs = nc.dram_tensor("typed_msgs", (NP, T * D), F32, kind="Internal").ap()
        table2 = nc.dram_tensor("table2", (NP, D), F32, kind="Internal").ap()
        table3 = nc.dram_tensor("table3", (NP, D), F32, kind="Internal").ap()

        X = sb("X", NB * D)
        X3 = X[:, :].rearrange("p (b f) -> p b f", b=NB)
        ident = sb("ident", P)
        before = sb("before", P)
        ones = sb("ones", P)
        iota = sb("iota", T * P)
        weT = sb("weT", T * D)
        wnT = sb("wnT", (T + 1) * T * D)
        w1s = sb("w1s", D)
        w3s = sb("w3s", D)
        w3es = sb("w3es", D, rows=FE)
        w3eT = sb("w3eT", FE)
        w3ew = sb("w3ew", D, rows=FE)
        be_row = sb("be_row", T * D, rows=1)
        bn_row = sb("bn_row", T * D, rows=1)
        b1b = sb("b1b", D)
        b3b = sb("b3b", D)
        ntype_i = sb("ntype_i", NB, I32)
        ntype_f = sb("ntype_f", NB)
        nmask = sb("nmask", T * NB)
        bucket_of = [sb(f"bucket_of{i}", TP, I32, rows=1) for i in range(2)]
        R = sb("R", TP * NR)
        small = sb("small", 20 * NB)
        big_words = (nc.sbuf_bytes_remaining // 4) // 16 * 16 - 64
        big = sb("big", big_words)

        def cut(at, n):
            assert at + n <= big_words, (at, n, big_words)
            return big[:, at:at + n], at + n

        ps = [ctx.enter_context(nc.psum_tensor(f"ps{i}", [P, 512], F32)) for i in range(8)]

        at = 0
        cols = []
        for _ in range(15):
            c, at = cut(at, C)
            cols.append(c)
        (dst_c, src_c, typ_c, w_c, dbkt, sbkt, dloc, key0, srcf, idx0, pos1, pos2, mask, scan, sloc) = cols
        dst_i, src_i, typ_i = (c.bitcast(I32) for c in (dst_c, src_c, typ_c))
        pay, at = cut(at, SQ * SU * RW)
        pay4 = pay.rearrange("p (q u r) -> p q u r", q=SQ, u=SU)
        fill1, at = cut(at, FILL * RW)
        sidx, at = cut(at, SQ * SU)
        sidx = sidx.bitcast(I32).rearrange("p (q u) -> p q u", q=SQ)
        iota_t = R[:, 0:TP]
        past = R[:, TP:2 * TP]
        wnat = R[:, 2 * TP:2 * TP + (T + 1) * T * D].rearrange("p (t i) -> p t i", t=T)
        wenat = R[:, 4 * TP - T * D:4 * TP].rearrange("p (t i) -> p t i", t=T)
        xTs = R[:, 4 * TP:4 * TP + D]
        mrow = R[:, 4 * TP + D:4 * TP + D + T * D]
        xst = R[:, 4 * TP + (T + 1) * D:4 * TP + (T + 2) * D]
        Tb = [small[:, i * NB:(i + 1) * NB] for i in range(2)]
        tiles_i = small[:, 2 * NB:3 * NB].bitcast(I32)
        tiles_f = small[:, 3 * NB:4 * NB]
        tends = [small[:, 4 * NB:5 * NB], small[:, 5 * NB:6 * NB]]
        starts = small[:, 6 * NB:7 * NB]
        bases = [small[:, 7 * NB:8 * NB], small[:, 8 * NB:9 * NB]]
        endcol = small[:, 9 * NB:9 * NB + 2]

        s_edges = sem("s_edges")
        s_rest = sem("s_rest")
        s_x = sem("s_x")
        s_w = sem("s_w")
        s_cst = sem("s_cst")
        s_filler = sem("s_filler")
        s_fill1 = sem("s_fill1")
        s_v1 = sem("s_v1")
        s_tot = sem("s_tot")
        s_pref = sem("s_pref")
        s_tend = sem("s_tend")
        s_tendT = sem("s_tendT")
        s_past = sem("s_past")
        s_pastp = sem("s_pastp")
        s_wT = sem("s_wT")
        s_wTe = sem("s_wTe")
        s_xs = sem("s_xs")
        s_xT = sem("s_xT")
        s_xTe = sem("s_xTe")
        s_m = sem("s_m")
        s_me = sem("s_me")
        s_mst = sem("s_mst")
        s_fills = sem("s_fills")

        main = EC * P

        with nc.Block() as block:
            @block.sync
            def _(sp):
                for col, a in ((dst_i, dst), (src_i, src), (typ_i, etype), (w_c, weight)):
                    sp.dma_start(col[:, 0:EC], a[0:main].rearrange("(p c) -> p c", p=P)).then_inc(s_edges, 16)
                sp.dma_start(X3[:, 0:NFULL, :], x[0:NFULL * P, :].rearrange("(b p) f -> p b f", p=P)).then_inc(s_x, 16)
                sp.wait_ge(s_filler, 6)
                for col, a in ((dst_i, dst), (src_i, src), (typ_i, etype), (w_c, weight)):
                    sp.dma_start(col[0:EREST, EC:C], a[main:E].rearrange("(p c) -> p c", c=1)).then_inc(s_rest, 16)
                sp.dma_start(X3[0:NREST, NFULL, :], x[NFULL * P:N, :]).then_inc(s_x, 16)
                sp.dma_start(ntype_i[:, 0:NFULL], ntype[0:NFULL * P].rearrange("(b p) -> p b", p=P)).then_inc(s_rest, 16)
                sp.dma_start(ntype_i[0:NREST, NFULL:NB], ntype[NFULL * P:N].rearrange("(p c) -> p c", c=1)).then_inc(s_rest, 16)
                sp.wait_ge(s_fill1, 4)
                with sp.Fori(0, TP // FILL, 1) as i:
                    sp.dma_start(sorted_edges[:, bass.ds(i * (FILL * RW), FILL * RW)], fill1).then_inc(s_fills, 16)
                with sp.Fori(0, NB, 1) as b:
                    sp.wait_ge(s_me, b + 1)
                    sp.dma_start(typed_msgs[bass.ds(b * P, P), :], mrow).then_inc(s_mst, 16)
                sp.wait_ge(s_mst, 16 * NB)
                sp.wait_ge(s_fills, 16 * (TP // FILL))

            @block.gpsimd
            def _(pool):
                pool.memset(ident[:, :], 0.0).then_inc(s_cst, 1)
                pool.memset(before[:, :], 1.0).then_inc(s_cst, 1)
                pool.memset(ones[:, :], 1.0).then_inc(s_cst, 1)
                pool.iota(iota[:, :], pattern=[[1, T * P]], base=0, channel_multiplier=0,
                          allow_small_or_imprecise_dtypes=True).then_inc(s_cst, 1)
                pool.iota(iota_t, pattern=[[1, TP]], base=0, channel_multiplier=0,
                          allow_small_or_imprecise_dtypes=True).then_inc(s_cst, 1)
                pool.wait_ge(s_cst, 5)
                pool.affine_select(out=ident[:, :], in_=ident[:, :], compare_op=ALU.not_equal, fill=1.0,
                                   base=0, pattern=[[-1, P]], channel_multiplier=1).then_inc(s_cst, 1)
                pool.affine_select(out=before[:, :], in_=before[:, :], compare_op=ALU.is_gt, fill=0.0,
                                   base=0, pattern=[[1, P]], channel_multiplier=-1).then_inc(s_cst, 1)

            @block.scalar
            def _(act):
                act.dma_start(wenat, w_e.rearrange("t o i -> o t i")).then_inc(s_w, 16)
                act.dma_start(wnat, w_n.rearrange("t o i -> o t i")).then_inc(s_w, 16)
                for t, a in ((w1s, w1), (w3s, w3), (w3es, w3e)):
                    act.dma_start(t[:, :], a).then_inc(s_w, 16)
                act.dma_start(be_row[:, :], b_e.rearrange("t (o f) -> o (t f)", o=1)).then_inc(s_w, 16)
                act.dma_start(bn_row[:, :], b_n.rearrange("t (o f) -> o (t f)", o=1)).then_inc(s_w, 16)
                act.dma_start(b1b[:, :], b1.rearrange("(o f) -> o f", o=1).to_broadcast([P, D])).then_inc(s_w, 16)
                act.dma_start(b3b[:, :], b3.rearrange("(o f) -> o f", o=1).to_broadcast([P, D])).then_inc(s_w, 16)
                act.wait_ge(s_wT, T)
                act.copy(weT[:, :], ps[0][:, 0:T * D]).then_inc(s_wTe, 1)
                for c in range(T + 1):
                    act.wait_ge(s_wT, T + T * (c + 1))
                    act.copy(wnT[:, c * T * D:(c + 1) * T * D], ps[1 + c][:, 0:T * D]).then_inc(s_wTe, 1)
                act.wait_ge(s_wT, T + T * (T + 1) + 1)
                act.copy(w3eT[:, :], ps[5][:, 0:FE]).then_inc(s_wTe, 1)
                act.wait_ge(s_wT, T + T * (T + 1) + 2)
                act.copy(w3ew[:, :], ps[6][0:FE, 0:D]).then_inc(s_wTe, 1)
                act.wait_ge(s_x, 32)
                act.wait_ge(s_filler, 6)
                with act.Fori(0, NB, 1) as b:
                    act.wait_ge(s_xT, b)
                    act.copy(xst, X[:, bass.ds(b * D, D)]).then_inc(s_xs, 1)
                    act.wait_ge(s_xT, b + 1)
                    act.copy(xTs, ps[0][:, 0:P]).then_inc(s_xTe, 1)
                    act.wait_ge(s_m, b + 1)
                    act.wait_ge(s_mst, 16 * b)
                    act.activation(mrow, ps[1][:, 0:T * D], ACT.Relu).then_inc(s_me, 1)

            @block.tensor
            def _(pe):
                pe.wait_ge(s_w, 16 * 9)
                pe.wait_ge(s_cst, FIXED)
                for t in range(T):
                    pe.transpose(ps[0][:, t * D:(t + 1) * D], wenat[:, t, :], ident[:, :]).then_inc(s_wT, 1)
                for c in range(T + 1):
                    for t in range(T):
                        pe.transpose(ps[1 + c][:, t * D:(t + 1) * D], wnat[:, t, c * D:(c + 1) * D],
                                     ident[:, :]).then_inc(s_wT, 1)
                pe.transpose(ps[5][:, 0:FE], w3es[:, :], ident[0:FE, 0:FE]).then_inc(s_wT, 1)
                pe.wait_ge(s_wTe, T + 3)
                pe.matmul(ps[6][0:FE, 0:D], w3eT[:, :], w3s[:, :], start=True, stop=True).then_inc(s_wT, 1)
                with pe.Fori(0, NB, 1) as b:
                    pe.wait_ge(s_me, b)
                    pe.wait_ge(s_xs, b + 1)
                    pe.transpose(ps[0][:, 0:P], xst, ident[:, :]).then_inc(s_xT, 1)
                    pe.wait_ge(s_xTe, b + 1)
                    pe.matmul(ps[1][:, 0:T * D], xTs, weT[:, :], start=True, stop=False)
                    pe.matmul(ps[1][:, 0:T * D], ones[0:1, :], be_row[:, :], start=False, stop=True).then_inc(s_m, 1)
                for k in range(2):
                    pe.wait_ge(s_tot, k + 1)
                    pe.matmul(ps[2 + k][:, 0:NB], before[:, :], Tb[k], start=True, stop=True).then_inc(s_pref, 1)
                    pe.matmul(ps[2 + k][:, 64:64 + NB], ones[:, :], Tb[k], start=True, stop=True).then_inc(s_pref, 1)
                    pe.wait_ge(s_tend, k + 1)
                    pe.transpose(ps[4][0:NB, 0:P], tends[k], ident[:, :]).then_inc(s_tendT, 1)
                    pe.wait_ge(s_past, k + 1)
                    for c in range(4):
                        pe.matmul(ps[4 + c][0:1, 0:TP // 4], ones[0:NB, 0:1],
                                  past[0:NB, c * (TP // 4):(c + 1) * (TP // 4)],
                                  start=True, stop=True).then_inc(s_pastp, 1)

            @block.vector
            def _(dve):
                n = [0]

                def link(ins):
                    n[0] += 1
                    ins.then_inc(s_v1, 1)
                    dve.wait_ge(s_v1, n[0])

                dve.memset(dst_i[:, EC:C], NO_NODE).then_inc(s_filler, 1)
                dve.memset(src_i[:, EC:C], NO_NODE).then_inc(s_filler, 1)
                dve.memset(typ_i[:, EC:C], 0).then_inc(s_filler, 1)
                dve.memset(w_c[:, EC:C], 0.0).then_inc(s_filler, 1)
                dve.memset(X3[:, NFULL, :], 0.0).then_inc(s_filler, 1)
                dve.memset(ntype_i[:, NFULL:NB], 0).then_inc(s_filler, 1)
                f3 = fill1.rearrange("p (u r) -> p u r", u=FILL)
                link(dve.memset(fill1, 0.0))
                dve.memset(f3[:, :, KEY0:DLOC + 1], -1.0).then_inc(s_fill1, 1)
                dve.memset(f3[:, :, SLOC:SLOC + 1], -1.0).then_inc(s_fill1, 1)
                dve.memset(f3[:, :, POS2:POS2 + 1].bitcast(I32), OUTSIDE).then_inc(s_fill1, 1)
                dve.memset(pay, 0.0).then_inc(s_fill1, 1)

                dve.wait_ge(s_edges, 64)
                dve.wait_ge(s_rest, 96)
                link(dve.tensor_scalar(mask.bitcast(I32), dst_i, 7, None, ALU.logical_shift_right))
                link(dve.tensor_copy(dbkt, mask.bitcast(I32)))
                link(dve.tensor_scalar(mask.bitcast(I32), src_i, 7, None, ALU.logical_shift_right))
                link(dve.tensor_copy(sbkt, mask.bitcast(I32)))
                link(dve.tensor_copy(srcf, src_i))
                link(dve.tensor_copy(scan, dst_i))
                link(dve.scalar_tensor_tensor(dloc, dbkt, -float(P), scan, ALU.mult, ALU.add))
                link(dve.scalar_tensor_tensor(sloc, sbkt, -float(P), srcf, ALU.mult, ALU.add))
                link(dve.tensor_copy(mask, typ_i))
                link(dve.scalar_tensor_tensor(key0, mask, float(P), dloc, ALU.mult, ALU.add))
                link(dve.scalar_tensor_tensor(idx0.bitcast(I32), srcf, float(T), mask, ALU.mult, ALU.add))
                link(dve.tensor_copy(ntype_f[:, :], ntype_i[:, :]))
                for t in range(T):
                    link(dve.tensor_scalar(nmask[:, t * NB:(t + 1) * NB], ntype_f[:, :], float(t), None, ALU.is_equal))

                for k, (bkt, pos) in enumerate(((dbkt, pos1), (sbkt, pos2))):
                    tot, tend, base = Tb[k], tends[k], bases[k]
                    for b in range(NB):
                        link(dve.tensor_scalar(mask, bkt, float(b), 0.0, ALU.is_equal, ALU.add,
                                               accum_out=tot[:, b:b + 1]))
                    dve.sem_inc(s_tot, 1)
                    dve.wait_ge(s_pref, 2 * k + 2)
                    link(dve.tensor_scalar(tiles_f, ps[2 + k][:, 64:64 + NB], float(P - 1), None, ALU.add))
                    link(dve.tensor_copy(tiles_i, tiles_f))
                    link(dve.tensor_scalar(tiles_i, tiles_i, 7, None, ALU.logical_shift_right))
                    link(dve.tensor_copy(tiles_f, tiles_i))
                    link(dve.tensor_tensor_scan(tend, tiles_f, tiles_f, 0.0, ALU.add, ALU.bypass))
                    dve.sem_inc(s_tend, 1)
                    link(dve.tensor_tensor(starts, tend, tiles_f, ALU.subtract))
                    link(dve.scalar_tensor_tensor(base, starts, float(P), ps[2 + k][:, 0:NB], ALU.mult, ALU.add))
                    dve.wait_ge(s_tendT, k + 1)
                    link(dve.tensor_copy(endcol[0:NB, k:k + 1], ps[4][0:NB, 0:1]))
                    link(dve.tensor_scalar(past[0:NB, :], iota_t[0:NB, :], endcol[0:NB, k:k + 1], None, ALU.is_ge))
                    dve.sem_inc(s_past, 1)
                    dve.wait_ge(s_pastp, 4 * k + 4)
                    for c in range(4):
                        link(dve.tensor_scalar(bucket_of[k][:, c * (TP // 4):(c + 1) * (TP // 4)],
                                               ps[4 + c][0:1, 0:TP // 4], float(NB - 1), None, ALU.min))
                    link(dve.memset(pos, float(OUTSIDE)))
                    for b in range(NB):
                        link(dve.tensor_scalar(mask, bkt, float(b), None, ALU.is_equal))
                        link(dve.tensor_tensor_scan(scan, mask, mask, base[:, b:b + 1], ALU.add, ALU.bypass))
                        link(dve.copy_predicated(pos, mask.bitcast(I32), scan))
                    link(dve.tensor_scalar(mask.bitcast(I32), pos, -1.0, None, ALU.add))
                    link(dve.tensor_scalar(scan.bitcast(I32), mask.bitcast(I32), P - 1, None, ALU.bitwise_and))
                    link(dve.tensor_scalar(mask.bitcast(I32), mask.bitcast(I32), 7, None, ALU.logical_shift_right))
                    link(dve.tensor_copy(pos, scan.bitcast(I32)))
                    link(dve.tensor_copy(scan, mask.bitcast(I32)))
                    link(dve.scalar_tensor_tensor(pos.bitcast(I32), pos, float(TP), scan, ALU.mult, ALU.add))

        s_turn = sem("s_turn")
        s_sattr = sems("s_sattr", SQ)
        s_sextra = sem("s_sextra")
        s_sfield = sems("s_sfield", SQ)
        s_srow = sems("s_srow", SQ)
        NFIELDS = 8
        attr_main = attr[0:main, :].rearrange("(p c) f -> p (c f)", p=P)
        sorted_rows = sorted_edges.rearrange("p (t r) -> (p t) r", r=RW)

        with nc.Block() as block:
            @block.sync
            def _(sp):
                def step(i, last=False):
                    for h in range(SQ):
                        sp.wait_ge(s_srow[h], i * (16 * SU))
                        k = i * SQ + h
                        n = SU - 1 if last and h == SQ - 1 else SU
                        sp.dma_start(pay4[:, h, 0:n, 0:FE],
                                     attr_main[:, bass.ds(k * (SU * FE), n * FE)].rearrange("p (u f) -> p u f", u=n)
                                     ).then_inc(s_sattr[h], 16)
                with sp.Fori(0, SSTEPS - 1, 1) as i:
                    step(i)
                step(SSTEPS - 1, last=True)
                sp.dma_start(pay4[0:EREST, SQ - 1, SU - 1, 0:FE], attr[main:E, :]).then_inc(s_sextra, 16)

            @block.vector
            def _(dve):
                with dve.Fori(0, SSTEPS, 1) as i:
                    for h in range(SQ):
                        c0 = dve.snap(i * (SQ * SU) + h * SU)
                        dve.wait_ge(s_srow[h], i * (16 * SU))
                        for field, col in ((KEY0, key0), (DLOC, dloc), (WGT, w_c), (SRCF, srcf), (SLOC, sloc),
                                           (POS2, pos2), (IDX0, idx0)):
                            dve.tensor_copy(pay4[:, h, :, field], col[:, bass.ds(c0, SU)]).then_inc(s_sfield[h], 1)
                        dve.tensor_copy(sidx[:, h, :], pos1.bitcast(I32)[:, bass.ds(c0, SU)]).then_inc(s_sfield[h], 1)

            @block.gpsimd
            def _(pool):
                beyond = pool.to_reg(P * TP - 1)

                def step(i, last=False):
                    for h in range(SQ):
                        pool.wait_ge(s_sattr[h], i * 16 + 16)
                        pool.wait_ge(s_sfield[h], i * NFIELDS + NFIELDS)
                        if last and h == SQ - 1:
                            pool.wait_ge(s_sextra, 16)
                        pool.sem_inc(s_turn, 1)
                        for u in range(SU):
                            pool.indirect_dma_start(
                                out=sorted_rows,
                                out_offset=bass.IndirectOffsetOnAxis(ap=sidx[:, h, u:u + 1], axis=0),
                                in_=pay4[:, h, u, :], in_offset=None,
                                bounds_check=beyond, oob_is_err=False).then_inc(s_srow[h], 16)
                with pool.Fori(0, SSTEPS - 1, 1) as i:
                    step(i)
                step(SSTEPS - 1, last=True)
                for h in range(SQ):
                    pool.wait_ge(s_srow[h], SSTEPS * 16 * SU)

        s_hot = sems("s_hot", Q)
        s_mm = sems("s_mm", Q)
        s_acc = sems("s_acc", Q)

        def free_of(sem_of, h, i, n, base=0):
            return (sem_of[h - 2], i * n + (n + base)) if h >= 2 else (sem_of[h + 2], i * n + base)

        def prior(sem_of, h, u, i, base=0):
            if u:
                return sem_of[h], i * U + (u + base)
            return (sem_of[h - 1], i * U + (U + base)) if h else (sem_of[Q - 1], i * U + base)

        acc, at = cut(0, NB * T * P)
        rec, at = cut(at, Q * U * RW)
        rec4 = rec.rearrange("p (q u r) -> p q u r", q=Q, u=U)
        rec4i = rec.bitcast(I32).rearrange("p (q u r) -> p q u r", q=Q, u=U)
        got, at = cut(at, Q * U * D)
        got4 = got.rearrange("p (q u f) -> p q u f", q=Q, u=U)
        hot, at = cut(at, 2 * U * T * P)
        hot4 = hot.rearrange("p (q u f) -> p q u f", q=2, u=U)
        fill2, at = cut(at, FILL * MW)
        R3 = R[:, :].rearrange("p (t r) -> p t r", r=NR)

        s_rec = sems("s_rec", Q)
        s_rused = sems("s_rused", Q)
        s_got = sems("s_got", Q)
        s_zero = sem("s_zero")
        s_fill2 = sem("s_fill2")
        s_fills2 = sem("s_fills2")
        typed_rows = typed_msgs.rearrange("n (t f) -> (n t) f", t=T)

        with nc.Block() as block:
            @block.sync
            def _(sp):
                sp.wait_ge(s_fill2, 2)
                with sp.Fori(0, STEPS, 1) as i:
                    for h in range(Q):
                        c0 = sp.snap((i * Q + h) * (U * RW))
                        sp.wait_ge(s_mm[h], i * U)
                        sp.dma_start(rec4[:, h, :, :], sorted_edges[:, bass.ds(c0, U * RW)]
                                     .rearrange("p (u r) -> p u r", u=U)).then_inc(s_rec[h], 16)
                    sp.dma_start(sorted_msgs[:, bass.ds(i * (FILL * MW), FILL * MW)], fill2).then_inc(s_fills2, 16)
                sp.wait_ge(s_fills2, 16 * STEPS)

            @block.gpsimd
            def _(pool):
                with pool.Fori(0, STEPS, 1) as i:
                    for h in range(Q):
                        pool.wait_ge(s_rec[h], i * 16 + 16)
                        pool.wait_ge(s_mm[h], i * U)
                        pool.sem_inc(s_turn, 1)
                        for u in range(U):
                            pool.indirect_dma_start(
                                out=got4[:, h, u, :], out_offset=None, in_=typed_rows,
                                in_offset=bass.IndirectOffsetOnAxis(ap=rec4i[:, h, u, IDX0:IDX0 + 1], axis=0)
                            ).then_inc(s_got[h], 16)

            @block.vector
            def _(dve):
                f2 = fill2.rearrange("p (u r) -> p u r", u=FILL)
                dve.memset(fill2, 0.0).then_inc(s_fill2, 1)
                dve.wait_ge(s_fill2, 1)
                dve.memset(f2[:, :, MLOC:MLOC + 1], -1.0).then_inc(s_fill2, 1)
                dve.memset(acc, 0.0).then_inc(s_zero, 1)
                dve.wait_ge(s_zero, 1)
                with dve.Fori(0, STEPS, 1) as i:
                    at_of = {}

                    def one_hot(h, u):
                        if u == 0:
                            for v in range(U):
                                b = dve.value_load(bucket_of[0][0:1, bass.ds(i * (Q * U) + h * U + v, 1)],
                                                   min_val=0, max_val=NB - 1)
                                at_of[h, v] = dve.snap(b * (T * P))
                            k = dve.snap((i * Q + h) * U)
                            dve.wait_ge(s_rec[h], i * 16 + 16)
                            dve.tensor_copy(R3[:, bass.ds(k, U), :], rec4[:, h, :, DLOC:DLOC + NR]).then_inc(s_rused[h], 1)
                            dve.wait_ge(*free_of(s_mm, h, i, U))
                        dve.tensor_scalar(hot4[:, h % 2, u, :], iota[:, :], rec4[:, h, u, KEY0:KEY0 + 1], None,
                                          ALU.is_equal).then_inc(s_rused[h], 1)

                    def add(h, u):
                        dve.wait_ge(s_mm[h], i * U + u + 1)
                        dve.wait_ge(*prior(s_acc, h, u, i))
                        a = acc[:, bass.ds(at_of[h, u], T * P)]
                        dve.tensor_tensor(a, ps[(h % 2) * U + u][:, 0:T * P], a, ALU.add).then_inc(s_acc[h], 1)

                    tiles = [(h, u) for h in range(Q) for u in range(U)]
                    for j, hu in enumerate(tiles):
                        one_hot(*hu)
                        if j >= 2:
                            add(*tiles[j - 2])
                    add(*tiles[-2])
                    add(*tiles[-1])

            @block.tensor
            def _(pe):
                with pe.Fori(0, STEPS, 1) as i:
                    for h in range(Q):
                        pe.wait_ge(s_got[h], i * (16 * U) + 16 * U)
                        pe.wait_ge(*free_of(s_acc, h, i, U))
                        for u in range(U):
                            pe.wait_ge(s_rused[h], i * (U + 1) + u + 2)
                            pe.matmul(ps[(h % 2) * U + u][:, 0:T * P], got4[:, h, u, :], hot4[:, h % 2, u, :],
                                      start=True, stop=True).then_inc(s_mm[h], 1)

        def sm(i):
            return small[:, i * NB:(i + 1) * NB]

        def along(v):
            return v.unsqueeze(2).to_broadcast([P, NB, D])

        def wide(v):
            return v.rearrange("p (b f) -> p b f", b=NB)

        def sum_of_squares(dve, link, h3, sq3, to):
            link(dve.tensor_tensor(sq3, h3, h3, ALU.mult))
            link(dve.tensor_reduce(out=to, in_=sq3, axis=AX.X, op=ALU.add))

        def layer_norm(dve, link, h3, sq3, ask_sqrt):
            mean, var = sm(0), sm(1)
            link(dve.tensor_reduce(out=mean, in_=h3, axis=AX.X, op=ALU.add))
            link(dve.tensor_scalar(mean, mean, 1.0 / D, None, ALU.mult))
            link(dve.tensor_tensor(h3, h3, along(mean), ALU.subtract))
            sum_of_squares(dve, link, h3, sq3, var)
            link(dve.tensor_scalar(var, var, 1.0 / D, EPS, ALU.mult, ALU.add))
            ask_sqrt(var, sm(2))
            link(dve.reciprocal(sm(2), sm(2)))
            link(dve.tensor_tensor(X3, h3, along(sm(2)), ALU.mult))

        class Chain:

            def __init__(self):
                self.v, self.ask, self.did = sem("s_step"), sem("s_ask"), sem("s_did")
                self.n = self.k = 0
                self.jobs = []

            def on(self, dve):
                self.dve = dve
                self.jobs = []

            def link(self, ins):
                self.n += 1
                ins.then_inc(self.v, 1)
                self.dve.wait_ge(self.v, self.n)

            def func(self, f, i, o, **kw):
                self.k += 1
                self.jobs.append((self.k, f, i, o, kw))
                self.dve.sem_inc(self.ask, 1)
                self.dve.wait_ge(self.did, self.k)

            def sqrt(self, i, o):
                self.func(ACT.Sqrt, i, o)

        h4, sq4, S = (cut(i * NB * D, NB * D)[0] for i in range(3))
        h4 = cut(3 * NB * D, NB * D)[0]
        h43 = wide(h4)
        rest4 = 4 * NB * D
        xTs4, rest4 = cut(rest4, D)
        xst4, rest4 = cut(rest4, D)
        acc_st, rest4 = cut(rest4, T * P)
        sq4 = cut(0, NB * D)[0]
        S = cut(NB * D, NB * D)[0]
        S3, sq43 = wide(S), wide(sq4)
        s_xs4 = sem("s_xs4")
        s_xT4 = sem("s_xT4")
        s_xTe4 = sem("s_xTe4")
        s_o4 = sem("s_o4")
        s_h4 = sem("s_h4")
        chain = Chain()

        with nc.Block() as block:
            @block.tensor
            def _(pe):
                with pe.Fori(0, NB, 1) as b:
                    pe.wait_ge(s_h4, b * T)
                    pe.wait_ge(s_xs4, b * 2 + 2)
                    pe.transpose(ps[0][:, 0:P], xst4, ident[:, :]).then_inc(s_xT4, 1)
                    for t in range(T):
                        pe.matmul(ps[1][:, 0:T * D], acc_st[:, t * P:(t + 1) * P],
                                  wnT[:, (t + 1) * T * D:(t + 2) * T * D], start=(t == 0), stop=False)
                    pe.matmul(ps[1][:, 0:T * D], ones[0:1, :], bn_row[:, :], start=False, stop=False)
                    pe.wait_ge(s_xTe4, b + 1)
                    pe.matmul(ps[1][:, 0:T * D], xTs4, wnT[:, 0:T * D], start=False, stop=True).then_inc(s_o4, 1)

            @block.scalar
            def _(act):
                with act.Fori(0, NB, 1) as b:
                    act.wait_ge(s_o4, b)
                    act.activation(xst4, X[:, bass.ds(b * D, D)], ACT.Relu).then_inc(s_xs4, 1)
                    act.copy(acc_st, acc[:, bass.ds(b * (T * P), T * P)]).then_inc(s_xs4, 1)
                    act.wait_ge(s_xT4, b + 1)
                    act.copy(xTs4, ps[0][:, 0:P]).then_inc(s_xTe4, 1)

            @block.vector
            def _(dve):
                dve.tensor_scalar(h4, X[:, :], 2.0, None, ALU.mult).then_inc(chain.v, 1)
                chain.n = 1
                dve.wait_ge(chain.v, 1)
                with dve.Fori(0, NB, 1) as b:
                    hb = dve.snap(b * D)
                    dve.wait_ge(s_o4, b + 1)
                    for t in range(T):
                        mb = dve.snap(b + t * NB)
                        dve.wait_ge(s_h4, b * T + t)
                        dve.scalar_tensor_tensor(h4[:, bass.ds(hb, D)], ps[1][:, t * D:(t + 1) * D],
                                                 nmask[:, bass.ds(mb, 1)], h4[:, bass.ds(hb, D)],
                                                 ALU.mult, ALU.add).then_inc(s_h4, 1)

        s_x1 = sem("s_x1")
        s_xs5 = sem("s_xs5")
        s_xT5 = sem("s_xT5")
        s_xTe5 = sem("s_xTe5")
        s_o5 = sem("s_o5")
        s_S5 = sem("s_S5")
        hb5 = sq4[:, 0:D]

        with nc.Block() as block:
            @block.vector
            def _(dve):
                chain.on(dve)
                link = chain.link
                dve.wait_ge(s_h4, T * NB)
                layer_norm(dve, link, h43, sq43, chain.sqrt)
                dve.sem_inc(s_x1, 1)
                n2, norm, z, lo, hi, ser, sel, t0 = (sm(i) for i in range(3, 11))
                sum_of_squares(dve, link, X3, sq43, n2)
                chain.sqrt(n2, norm)
                link(dve.tensor_scalar(norm, norm, MIN_NORM, None, ALU.max))
                link(dve.tensor_scalar(z, norm, 1.0 - 1e-7, None, ALU.min))
                link(dve.tensor_scalar(lo, z, -1.0, 1.0, ALU.mult, ALU.add))
                link(dve.tensor_scalar(hi, z, 1.0, None, ALU.add))
                chain.func(ACT.Ln, lo, lo)
                chain.func(ACT.Ln, hi, hi)
                link(dve.tensor_tensor(hi, hi, lo, ALU.subtract))
                link(dve.tensor_scalar(hi, hi, 0.5, None, ALU.mult))
                link(dve.tensor_tensor(t0, z, z, ALU.mult))
                link(dve.tensor_scalar(ser, t0, 1.0 / 11, 1.0 / 9, ALU.mult, ALU.add))
                for c in (1.0 / 7, 1.0 / 5, 1.0 / 3, 1.0):
                    link(dve.tensor_tensor(ser, ser, t0, ALU.mult))
                    link(dve.tensor_scalar(ser, ser, c, None, ALU.add))
                link(dve.tensor_tensor(ser, ser, z, ALU.mult))
                link(dve.tensor_scalar(sel, z, 0.25, None, ALU.is_lt))
                link(dve.copy_predicated(hi, sel.bitcast(I32), ser))
                link(dve.reciprocal(norm, norm))
                link(dve.tensor_tensor(hi, hi, norm, ALU.mult))
                c1 = small[:, 11 * NB:11 * NB + 8]
                link(dve.tensor_tensor(hb5, b1b[:, :], b1b[:, :], ALU.mult))
                link(dve.tensor_reduce(out=c1[:, 0:1], in_=hb5, axis=AX.X, op=ALU.add))
                chain.sqrt(c1[:, 0:1], c1[:, 1:2])
                link(dve.tensor_scalar(c1[:, 1:2], c1[:, 1:2], MIN_NORM, None, ALU.max))
                chain.func(ACT.Tanh, c1[:, 1:2], c1[:, 2:3])
                link(dve.reciprocal(c1[:, 3:4], c1[:, 1:2]))
                link(dve.tensor_tensor(c1[:, 2:3], c1[:, 2:3], c1[:, 3:4], ALU.mult))
                link(dve.tensor_scalar(b1b[:, :], b1b[:, :], c1[:, 2:3], None, ALU.mult))
                link(dve.tensor_tensor(hb5, b1b[:, :], b1b[:, :], ALU.mult))
                link(dve.tensor_reduce(out=c1[:, 0:1], in_=hb5, axis=AX.X, op=ALU.add))
                chain.sqrt(c1[:, 0:1], c1[:, 1:2])
                link(dve.tensor_scalar(c1[:, 1:2], c1[:, 1:2], MIN_NORM, None, ALU.max))
                link(dve.reciprocal(c1[:, 1:2], c1[:, 1:2]))
                link(dve.tensor_scalar(c1[:, 1:2], c1[:, 1:2], MAX_NORM, 1.0, ALU.mult, ALU.min))
                link(dve.tensor_scalar(b1b[:, :], b1b[:, :], c1[:, 1:2], None, ALU.mult))
                link(dve.tensor_tensor(hb5, b1b[:, :], b1b[:, :], ALU.mult))
                link(dve.tensor_reduce(out=c1[:, 0:1], in_=hb5, axis=AX.X, op=ALU.add))
                y2 = c1[:, 0:1]
                dve.wait_ge(s_S5, NB)
                link(dve.tensor_tensor(S3, S3, along(hi), ALU.mult))
                x2, xy, den, a = sm(3), sm(4), sm(5), sm(6)
                sum_of_squares(dve, link, S3, sq43, x2)
                bias3 = b1b[:, :].unsqueeze(1).to_broadcast([P, NB, D])
                link(dve.tensor_tensor(sq43, S3, bias3, ALU.mult))
                link(dve.tensor_reduce(out=xy, in_=sq43, axis=AX.X, op=ALU.add))
                link(dve.tensor_scalar(xy, xy, 2.0, 1.0, ALU.mult, ALU.add))
                link(dve.tensor_scalar(a, xy, y2, None, ALU.add))
                link(dve.tensor_scalar(den, x2, y2, None, ALU.mult))
                link(dve.tensor_tensor(den, den, xy, ALU.add))
                link(dve.tensor_scalar(den, den, MIN_NORM, None, ALU.max))
                link(dve.reciprocal(den, den))
                link(dve.tensor_tensor(a, a, den, ALU.mult))
                link(dve.tensor_scalar(x2, x2, -1.0, 1.0, ALU.mult, ALU.add))
                link(dve.tensor_tensor(x2, x2, den, ALU.mult))
                link(dve.tensor_tensor(S3, S3, along(a), ALU.mult))
                link(dve.tensor_tensor(sq43, bias3, along(x2), ALU.mult))
                link(dve.tensor_tensor(S3, S3, sq43, ALU.add))
                sum_of_squares(dve, link, S3, sq43, den)
                chain.sqrt(den, a)
                link(dve.tensor_scalar(a, a, MIN_NORM, None, ALU.max))
                link(dve.reciprocal(a, a))
                link(dve.tensor_scalar(a, a, MAX_NORM, 1.0, ALU.mult, ALU.min))
                link(dve.tensor_tensor(S3, S3, along(a), ALU.mult))

            @block.scalar
            def _(act):
                for k, f, i, o, kw in chain.jobs:
                    act.wait_ge(chain.ask, k)
                    act.activation(o, i, f, **kw).then_inc(chain.did, 1)
                    if k == 1:
                        act.wait_ge(s_x1, 1)
                        with act.Fori(0, NB, 1) as b:
                            act.wait_ge(s_xT5, b)
                            act.copy(xst4, X[:, bass.ds(b * D, D)]).then_inc(s_xs5, 1)
                            act.wait_ge(s_xT5, b + 1)
                            act.copy(xTs4, ps[0][:, 0:P]).then_inc(s_xTe5, 1)
                            act.wait_ge(s_o5, b + 1)
                            act.copy(S[:, bass.ds(b * D, D)], ps[1][:, 0:D]).then_inc(s_S5, 1)

            @block.tensor
            def _(pe):
                with pe.Fori(0, NB, 1) as b:
                    pe.wait_ge(s_S5, b)
                    pe.wait_ge(s_xs5, b + 1)
                    pe.transpose(ps[0][:, 0:P], xst4, ident[:, :]).then_inc(s_xT5, 1)
                    pe.wait_ge(s_xTe5, b + 1)
                    pe.matmul(ps[1][:, 0:D], xTs4, w1s[:, :], start=True, stop=True).then_inc(s_o5, 1)

        at = 2 * NB * D
        hotw, at = cut(at, 2 * U * P)
        hotw4 = hotw.rearrange("p (q u f) -> p q u f", q=2, u=U)
        hotT, at = cut(at, 2 * U * P)
        hotT4 = hotT.rearrange("p (q u f) -> p q u f", q=2, u=U)
        msg, at = cut(at, Q * U * MW)
        msg4 = msg.rearrange("p (q u r) -> p q u r", q=Q, u=U)
        midx, at = cut(at, Q * U)
        midx3 = midx.bitcast(I32).rearrange("p (q u) -> p q u", q=Q)
        s_one6 = sem("s_one6")
        s_hot6 = sems("s_hot6", Q)
        s_fld6 = sems("s_fld6", Q)
        s_T6 = sems("s_T6", Q)
        s_Te6 = sems("s_Te6", Q)
        s_G6 = sems("s_G6", Q)
        s_Ge6 = sems("s_Ge6", Q)
        s_row6 = sems("s_row6", Q)
        msg_rows = sorted_msgs.rearrange("p (t r) -> (p t) r", r=MW)

        with nc.Block() as block:
            @block.vector
            def _(dve):
                dve.memset(msg4[:, :, :, MONE], 1.0).then_inc(s_one6, 1)
                with dve.Fori(0, STEPS, 1) as i:
                    for h in range(Q):
                        t0 = dve.snap((i * Q + h) * U)
                        at_w = [dve.snap(((i * Q + h) * U + u) * NR) for u in range(U)]
                        dve.wait_ge(*free_of(s_T6, h, i, U))
                        for u in range(U):
                            dve.tensor_scalar(hotw4[:, h % 2, u, :], iota[:, 0:P],
                                              R[:, bass.ds(at_w[u] + R_DLOC, 1)], R[:, bass.ds(at_w[u] + R_WGT, 1)],
                                              ALU.is_equal, ALU.mult).then_inc(s_hot6[h], 1)
                        dve.wait_ge(s_row6[h], i * (16 * U))
                        dve.tensor_copy(msg4[:, h, :, MLOC], R3[:, bass.ds(t0, U), R_SLOC]).then_inc(s_fld6[h], 1)
                        dve.tensor_copy(midx3[:, h, :], R3[:, bass.ds(t0, U), R_POS2].bitcast(I32)).then_inc(s_fld6[h], 1)

            @block.tensor
            def _(pe):
                with pe.Fori(0, STEPS, 1) as i:
                    def turn(h):
                        pe.wait_ge(*free_of(s_Te6, h, i, 1))
                        for u in range(U):
                            pe.wait_ge(s_hot6[h], i * U + u + 1)
                            pe.transpose(ps[h % 2][:, u * P:(u + 1) * P], hotw4[:, h % 2, u, :],
                                         ident[:, :]).then_inc(s_T6[h], 1)

                    def take(h):
                        rows = []
                        for u in range(U):
                            b = pe.value_load(bucket_of[0][0:1, bass.ds(i * (Q * U) + h * U + u, 1)],
                                              min_val=0, max_val=NB - 1)
                            rows.append(pe.snap(b * D))
                        pe.wait_ge(s_Te6[h], i + 1)
                        pe.wait_ge(*free_of(s_Ge6, h, i, 1))
                        for u in range(U):
                            pe.matmul(ps[2 + h % 2][:, u * D:(u + 1) * D], hotT4[:, h % 2, u, :],
                                      S[:, bass.ds(rows[u], D)], start=True, stop=True).then_inc(s_G6[h], 1)

                    turn(0)
                    for h in range(1, Q):
                        turn(h)
                        take(h - 1)
                    take(Q - 1)

            @block.scalar
            def _(act):
                with act.Fori(0, STEPS, 1) as i:
                    def turned(h):
                        act.wait_ge(s_T6[h], i * U + U)
                        act.wait_ge(*free_of(s_G6, h, i, U))
                        act.copy(hotT4[:, h % 2, :, :], ps[h % 2][:, :].rearrange("p (u f) -> p u f", u=U)).then_inc(s_Te6[h], 1)

                    def taken(h):
                        act.wait_ge(s_G6[h], i * U + U)
                        act.wait_ge(s_row6[h], i * (16 * U))
                        act.copy(msg4[:, h, :, 0:D], ps[2 + h % 2][:, :].rearrange("p (u f) -> p u f", u=U)).then_inc(s_Ge6[h], 1)

                    turned(0)
                    for h in range(1, Q):
                        turned(h)
                        taken(h - 1)
                    taken(Q - 1)

            @block.gpsimd
            def _(pool):
                beyond = pool.to_reg(P * TP - 1)
                pool.wait_ge(s_one6, 1)
                with pool.Fori(0, STEPS, 1) as i:
                    for h in range(Q):
                        pool.wait_ge(s_Ge6[h], i + 1)
                        pool.wait_ge(s_fld6[h], i * 2 + 2)
                        pool.sem_inc(s_turn, 1)
                        for u in range(U):
                            pool.indirect_dma_start(
                                out=msg_rows, out_offset=bass.IndirectOffsetOnAxis(ap=midx3[:, h, u:u + 1], axis=0),
                                in_=msg4[:, h, u, :], in_offset=None,
                                bounds_check=beyond, oob_is_err=False).then_inc(s_row6[h], 16)
                for h in range(Q):
                    pool.wait_ge(s_row6[h], STEPS * 16 * U)

        AW = D + 1
        acc7, at = cut(0, NB * AW)
        rec7, at = cut(at, Q * U * MW)
        rec74 = rec7.rearrange("p (q u r) -> p q u r", q=Q, u=U)
        hot7, at = cut(at, 2 * U * P)
        hot74 = hot7.rearrange("p (q u f) -> p q u f", q=2, u=U)
        s_zero7 = sem("s_zero7")
        s_rec7 = sems("s_rec7", Q)

        def tile_sums(ps_at, h, u, w, rows=P):
            return ps[(h % 2) * U + u][0:rows, ps_at:ps_at + w]

        with nc.Block() as block:
            @block.sync
            def _(sp):
                with sp.Fori(0, STEPS, 1) as i:
                    for h in range(Q):
                        c0 = sp.snap((i * Q + h) * (U * MW))
                        sp.wait_ge(s_mm[h], i * U + STEPS * U)
                        sp.dma_start(rec74[:, h, :, :], sorted_msgs[:, bass.ds(c0, U * MW)]
                                     .rearrange("p (u r) -> p u r", u=U)).then_inc(s_rec7[h], 16)

            @block.vector
            def _(dve):
                dve.memset(acc7, 0.0).then_inc(s_zero7, 1)
                dve.wait_ge(s_zero7, 1)
                with dve.Fori(0, STEPS, 1) as i:
                    at_of = {}

                    def one_hot(h, u):
                        if u == 0:
                            for v in range(U):
                                b = dve.value_load(bucket_of[1][0:1, bass.ds(i * (Q * U) + h * U + v, 1)],
                                                   min_val=0, max_val=NB - 1)
                                at_of[h, v] = dve.snap(b * AW)
                            dve.wait_ge(s_rec7[h], i * 16 + 16)
                            dve.wait_ge(*free_of(s_mm, h, i, U, STEPS * U))
                        dve.tensor_scalar(hot74[:, h % 2, u, :], iota[:, 0:P], rec74[:, h, u, MLOC:MLOC + 1], None,
                                          ALU.is_equal).then_inc(s_hot[h], 1)

                    def add(h, u):
                        dve.wait_ge(s_mm[h], i * U + u + 1 + STEPS * U)
                        dve.wait_ge(*prior(s_acc, h, u, i, STEPS * U))
                        a = acc7[:, bass.ds(at_of[h, u], AW)]
                        dve.tensor_tensor(a, tile_sums(0, h, u, AW), a, ALU.add).then_inc(s_acc[h], 1)

                    tiles = [(h, u) for h in range(Q) for u in range(U)]
                    for j, hu in enumerate(tiles):
                        one_hot(*hu)
                        if j >= 3:
                            add(*tiles[j - 3])
                    for hu in tiles[-3:]:
                        add(*hu)

            @block.tensor
            def _(pe):
                with pe.Fori(0, STEPS, 1) as i:
                    for h in range(Q):
                        pe.wait_ge(*free_of(s_acc, h, i, U, STEPS * U))
                        for u in range(U):
                            pe.wait_ge(s_hot[h], i * U + u + 1)
                            pe.matmul(tile_sums(0, h, u, AW), hot74[:, h % 2, u, :], rec74[:, h, u, 0:AW],
                                      start=True, stop=True).then_inc(s_mm[h], 1)

        top = big_words - 2 * NB * D
        sq8 = cut(top, NB * D)[0]
        h8 = cut(top + NB * D, NB * D)[0]
        sq83, h83 = wide(sq8), wide(h8)
        agg7 = acc7.rearrange("p (b f) -> p b f", b=NB)
        y = h8
        dinv = small[:, 12 * NB:13 * NB]
        s_st8 = sem("s_st8")
        s_y8 = sem("s_y8")
        with nc.Block() as block:
            @block.vector
            def _(dve):
                chain.on(dve)
                link = chain.link
                raw, norm, th, f, ne = (sm(i) for i in range(3, 8))
                g = agg7[:, :, 0:D]
                sum_of_squares(dve, link, g, sq83, raw)
                chain.sqrt(raw, raw)
                link(dve.tensor_scalar(norm, raw, MIN_NORM, None, ALU.max))
                chain.func(ACT.Tanh, norm, th)
                link(dve.reciprocal(norm, norm))
                link(dve.tensor_tensor(f, th, norm, ALU.mult))
                link(dve.tensor_tensor(ne, f, raw, ALU.mult))
                link(dve.tensor_scalar(ne, ne, MIN_NORM, None, ALU.max))
                link(dve.reciprocal(ne, ne))
                link(dve.tensor_scalar(ne, ne, MAX_NORM, 1.0, ALU.mult, ALU.min))
                link(dve.tensor_tensor(f, f, ne, ALU.mult))
                link(dve.tensor_tensor(h83, g, along(f), ALU.mult))
                link(dve.tensor_tensor(h83, h83, X3, ALU.add))
                layer_norm(dve, link, h83, sq83, chain.sqrt)
                link(dve.tensor_scalar(dinv, agg7[:, :, D], 1.0, None, ALU.add))
                chain.sqrt(dinv, dinv)
                link(dve.reciprocal(dinv, dinv))
                link(dve.tensor_tensor(wide(y), X3, along(dinv), ALU.mult))
                dve.sem_inc(s_y8, 1)

            @block.scalar
            def _(act):
                for k, f, i, o, kw in chain.jobs:
                    act.wait_ge(chain.ask, k)
                    act.activation(o, i, f, **kw).then_inc(chain.did, 1)

            @block.sync
            def _(sp):
                sp.wait_ge(s_y8, 1)
                sp.dma_start(table2.rearrange("(b p) f -> p b f", p=P), wide(y)).then_inc(s_st8, 16)
                sp.wait_ge(s_st8, 16)

        AW9 = D + 1
        acc9, at = cut(0, NB * AW9)
        got9, at = cut(at, Q * U * AW9)
        got94 = got9.rearrange("p (q u f) -> p q u f", q=Q, u=U)
        hot9, at = cut(at, 2 * U * P)
        hot94 = hot9.rearrange("p (q u f) -> p q u f", q=2, u=U)
        gidx, at = cut(at, Q * U)
        gidx3 = gidx.bitcast(I32).rearrange("p (q u) -> p q u", q=Q)
        assert at <= top
        s_zero9 = sem("s_zero9")
        s_idx9 = sems("s_idx9", Q)
        s_got9 = sems("s_got9", Q)
        with nc.Block() as block:
            @block.gpsimd
            def _(pool):
                pool.wait_ge(s_zero9, 2)
                with pool.Fori(0, STEPS, 1) as i:
                    for h in range(Q):
                        pool.wait_ge(s_idx9[h], i + 1)
                        pool.wait_ge(s_mm[h], i * U + 2 * STEPS * U)
                        pool.sem_inc(s_turn, 1)
                        for u in range(U):
                            pool.indirect_dma_start(
                                out=got94[:, h, u, 0:D], out_offset=None, in_=table2,
                                in_offset=bass.IndirectOffsetOnAxis(ap=gidx3[:, h, u:u + 1], axis=0)
                            ).then_inc(s_got9[h], 16)

            @block.vector
            def _(dve):
                dve.memset(acc9, 0.0).then_inc(s_zero9, 1)
                dve.memset(got94[:, :, :, D], 1.0).then_inc(s_zero9, 1)
                dve.wait_ge(s_zero9, 2)
                with dve.Fori(0, STEPS, 1) as i:
                    at_of = {}

                    def one_hot(h, u):
                        if u == 0:
                            t0 = dve.snap((i * Q + h) * U)
                            for v in range(U):
                                b = dve.value_load(bucket_of[0][0:1, bass.ds(i * (Q * U) + h * U + v, 1)],
                                                   min_val=0, max_val=NB - 1)
                                at_of[h, v] = dve.snap(b * AW9)
                            dve.wait_ge(s_got9[h], i * (16 * U))
                            dve.tensor_copy(gidx3[:, h, :], R3[:, bass.ds(t0, U), R_SRCF]).then_inc(s_idx9[h], 1)
                            dve.wait_ge(*free_of(s_mm, h, i, U, 2 * STEPS * U))
                        dve.tensor_scalar(hot94[:, h % 2, u, :], iota[:, 0:P],
                                          R[:, bass.ds(((i * Q + h) * U + u) * NR + R_DLOC, 1)], None,
                                          ALU.is_equal).then_inc(s_hot[h], 1)

                    def add(h, u):
                        dve.wait_ge(s_mm[h], i * U + u + 1 + 2 * STEPS * U)
                        dve.wait_ge(*prior(s_acc, h, u, i, 2 * STEPS * U))
                        a = acc9[:, bass.ds(at_of[h, u], AW9)]
                        dve.tensor_tensor(a, tile_sums(0, h, u, AW9), a, ALU.add).then_inc(s_acc[h], 1)

                    for h in range(Q):
                        for u in range(U):
                            one_hot(h, u)
                        if h:
                            for u in range(U):
                                add(h - 1, u)
                    for u in range(U):
                        add(Q - 1, u)

            @block.tensor
            def _(pe):
                with pe.Fori(0, STEPS, 1) as i:
                    for h in range(Q):
                        pe.wait_ge(s_got9[h], i * (16 * U) + 16 * U)
                        pe.wait_ge(*free_of(s_acc, h, i, U, 2 * STEPS * U))
                        for u in range(U):
                            pe.wait_ge(s_hot[h], i * U + u + 1 + STEPS * U)
                            pe.matmul(tile_sums(0, h, u, AW9), hot94[:, h % 2, u, :], got94[:, h, u, :],
                                      start=True, stop=True).then_inc(s_mm[h], 1)

        agg9 = acc9.rearrange("p (b f) -> p b f", b=NB)
        degn = small[:, 13 * NB:14 * NB]
        s_st10 = sem("s_st10")
        s_x3 = sem("s_x3")
        with nc.Block() as block:
            @block.vector
            def _(dve):
                chain.on(dve)
                link = chain.link
                link(dve.tensor_tensor(h83, agg9[:, :, 0:D], h83, ALU.add))
                link(dve.tensor_tensor(h83, h83, along(dinv), ALU.mult))
                link(dve.tensor_tensor(h83, h83, X3, ALU.add))
                layer_norm(dve, link, h83, sq83, chain.sqrt)
                dve.sem_inc(s_x3, 1)
                link(dve.tensor_scalar(degn, agg9[:, :, D], 1.0, None, ALU.max))
                chain.sqrt(degn, degn)
                link(dve.reciprocal(degn, degn))

            @block.scalar
            def _(act):
                for k, f, i, o, kw in chain.jobs:
                    act.wait_ge(chain.ask, k)
                    act.activation(o, i, f, **kw).then_inc(chain.did, 1)

            @block.sync
            def _(sp):
                sp.wait_ge(s_x3, 1)
                sp.dma_start(table3.rearrange("(b p) f -> p b f", p=P), X3).then_inc(s_st10, 16)
                sp.wait_ge(s_st10, 16)

        accN, at = cut(0, NB * P)
        accE, at = cut(at, NB * P)
        got11, at = cut(at, Q * U * D)
        got114 = got11.rearrange("p (q u f) -> p q u f", q=Q, u=U)
        hot11, at = cut(at, 2 * U * P)
        hot114 = hot11.rearrange("p (q u f) -> p q u f", q=2, u=U)
        rec11, at = cut(at, Q * U * RW)
        rec114 = rec11.rearrange("p (q u r) -> p q u r", q=Q, u=U)
        gidx11, at = cut(at, Q * U)
        gidx113 = gidx11.bitcast(I32).rearrange("p (q u) -> p q u", q=Q)
        s_zero11 = sem("s_zero11")
        s_rec11 = sems("s_rec11", Q)
        s_idx11 = sems("s_idx11", Q)
        s_got11 = sems("s_got11", Q)
        s_accE11 = sems("s_accE11", Q)
        with nc.Block() as block:
            @block.sync
            def _(sp):
                with sp.Fori(0, STEPS, 1) as i:
                    for h in range(Q):
                        c0 = sp.snap((i * Q + h) * (U * RW))
                        sp.wait_ge(s_mm[h], i * (2 * U) + 3 * STEPS * U)
                        sp.dma_start(rec114[:, h, :, :], sorted_edges[:, bass.ds(c0, U * RW)]
                                     .rearrange("p (u r) -> p u r", u=U)).then_inc(s_rec11[h], 16)

            @block.gpsimd
            def _(pool):
                with pool.Fori(0, STEPS, 1) as i:
                    for h in range(Q):
                        pool.wait_ge(s_idx11[h], i + 1)
                        pool.wait_ge(s_mm[h], i * (2 * U) + 3 * STEPS * U)
                        pool.sem_inc(s_turn, 1)
                        for u in range(U):
                            pool.indirect_dma_start(
                                out=got114[:, h, u, :], out_offset=None, in_=table3,
                                in_offset=bass.IndirectOffsetOnAxis(ap=gidx113[:, h, u:u + 1], axis=0)
                            ).then_inc(s_got11[h], 16)

            @block.vector
            def _(dve):
                dve.memset(accN, 0.0).then_inc(s_zero11, 1)
                dve.memset(accE[0:FE, :], 0.0).then_inc(s_zero11, 1)
                dve.wait_ge(s_zero11, 2)
                with dve.Fori(0, STEPS, 1) as i:
                    at_of = {}

                    def one_hot(h, u):
                        if u == 0:
                            t0 = dve.snap((i * Q + h) * U)
                            for v in range(U):
                                b = dve.value_load(bucket_of[0][0:1, bass.ds(i * (Q * U) + h * U + v, 1)],
                                                   min_val=0, max_val=NB - 1)
                                at_of[h, v] = dve.snap(b * P)
                            dve.wait_ge(s_got11[h], i * (16 * U))
                            dve.tensor_copy(gidx113[:, h, :], R3[:, bass.ds(t0, U), R_SRCF]).then_inc(s_idx11[h], 1)
                            dve.wait_ge(*free_of(s_mm, h, i, 2 * U, 3 * STEPS * U))
                        dve.tensor_scalar(hot114[:, h % 2, u, :], iota[:, 0:P],
                                          R[:, bass.ds(((i * Q + h) * U + u) * NR + R_DLOC, 1)], None,
                                          ALU.is_equal).then_inc(s_hot[h], 1)

                    def add(h, u):
                        dve.wait_ge(s_mm[h], i * (2 * U) + 2 * u + 2 + 3 * STEPS * U)
                        dve.wait_ge(*prior(s_acc, h, u, i, 3 * STEPS * U))
                        a = accN[:, bass.ds(at_of[h, u], P)]
                        dve.tensor_tensor(a, tile_sums(0, h, u, P), a, ALU.add).then_inc(s_acc[h], 1)
                        dve.wait_ge(*prior(s_accE11, h, u, i))
                        e = accE[0:FE, bass.ds(at_of[h, u], P)]
                        dve.tensor_tensor(e, tile_sums(P, h, u, P, FE), e, ALU.add).then_inc(s_accE11[h], 1)

                    for h in range(Q):
                        for u in range(U):
                            one_hot(h, u)
                        if h:
                            for u in range(U):
                                add(h - 1, u)
                    for u in range(U):
                        add(Q - 1, u)

            @block.tensor
            def _(pe):
                with pe.Fori(0, STEPS, 1) as i:
                    for h in range(Q):
                        pe.wait_ge(s_got11[h], i * (16 * U) + 16 * U)
                        pe.wait_ge(s_rec11[h], i * 16 + 16)
                        pe.wait_ge(*free_of(s_accE11, h, i, U))
                        for u in range(U):
                            pe.wait_ge(s_hot[h], i * U + u + 1 + 2 * STEPS * U)
                            pe.matmul(tile_sums(0, h, u, P), got114[:, h, u, :], hot114[:, h % 2, u, :],
                                      start=True, stop=True).then_inc(s_mm[h], 1)
                            pe.matmul(tile_sums(P, h, u, P, FE), rec114[:, h, u, 0:FE], hot114[:, h % 2, u, :],
                                      start=True, stop=True).then_inc(s_mm[h], 1)

        h12 = cut(2 * NB * P, NB * D)[0]
        sq12 = cut(3 * NB * P, NB * D)[0]
        h123, sq123 = wide(h12), wide(sq12)
        n_st = cut(4 * NB * P, P)[0]
        e_st = cut(4 * NB * P + P, P)[0]
        s_st12 = sem("s_st12")
        s_o12 = sem("s_o12")
        s_h12 = sem("s_h12")
        s_out = sem("s_out")
        s_x4 = sem("s_x4")
        with nc.Block() as block:
            @block.tensor
            def _(pe):
                with pe.Fori(0, NB, 1) as b:
                    pe.wait_ge(s_h12, b)
                    pe.wait_ge(s_st12, b * 2 + 2)
                    pe.matmul(ps[0][:, 0:D], n_st, w3s[:, :], start=True, stop=False)
                    pe.matmul(ps[0][:, 0:D], e_st[0:FE, :], w3ew[:, :],
                              start=False, stop=True).then_inc(s_o12, 1)

            @block.vector
            def _(dve):
                chain.on(dve)
                link = chain.link
                with dve.Fori(0, NB, 1) as b:
                    dve.wait_ge(s_o12, b + 1)
                    dve.scalar_tensor_tensor(h12[:, bass.ds(b * D, D)], ps[0][:, 0:D], degn[:, bass.ds(b, 1)],
                                             b3b[:, :], ALU.mult, ALU.add).then_inc(s_h12, 1)
                dve.wait_ge(s_h12, NB)
                link(dve.scalar_tensor_tensor(h12, h12, 0.0, X[:, :], ALU.max, ALU.add))
                layer_norm(dve, link, h123, sq123, chain.sqrt)
                dve.sem_inc(s_x4, 1)

            @block.scalar
            def _(act):
                with act.Fori(0, NB, 1) as b:
                    act.wait_ge(s_o12, b)
                    act.copy(n_st, accN[:, bass.ds(b * P, P)]).then_inc(s_st12, 1)
                    act.copy(e_st[0:FE, :], accE[0:FE, bass.ds(b * P, P)]).then_inc(s_st12, 1)
                for k, f, i, o, kw in chain.jobs:
                    act.wait_ge(chain.ask, k)
                    act.activation(o, i, f, **kw).then_inc(chain.did, 1)

            @block.sync
            def _(sp):
                sp.wait_ge(s_x4, 1)
                sp.dma_start(out[0:NFULL * P, :].rearrange("(b p) f -> p b f", p=P), X3[:, 0:NFULL, :]).then_inc(s_out, 16)
                sp.dma_start(out[NFULL * P:N, :], X3[0:NREST, NFULL, :]).then_inc(s_out, 16)
                sp.wait_ge(s_out, 32)


_INS = ["x", "src", "dst", "edge_attr_64", "edge_type_3", "edge_weight", "node_type_3", "L0_gnn_W_e", "L0_gnn_b_e",
        "L0_gnn_W_n", "L0_gnn_b_n", "L1_gnn_weight", "L1_gnn_bias", "L3_gnn_weight", "L3_gnn_weight_edge", "L3_gnn_bias"]


def kernel(**inputs):
    import numpy as np
    import concourse.bacc as bacc
    from concourse.bass_utils import run_bass_kernel_spmd as run

    nc = bacc.Bacc("TRN2", target_bir_lowering=False, num_devices=1)
    arrays, args = {}, []
    for name in _INS:
        a = np.ascontiguousarray(inputs[name])
        arrays[f"in_{name}"] = a
        args.append(nc.dram_tensor(f"in_{name}", a.shape, mybir.dt.from_np(a.dtype), kind="ExternalInput").ap())
    out = nc.dram_tensor("out", (N, D), F32, kind="ExternalOutput").ap()
    build(nc, *args, out)
    return run(nc, [arrays], core_ids=[0]).results[0]["out"]
```

```python
from contextlib import ExitStack

import concourse.bass as bass
from concourse import mybir

F32 = mybir.dt.float32
I32 = mybir.dt.int32
I16 = mybir.dt.int16
BF16 = mybir.dt.bfloat16
ALU = mybir.AluOpType
ACT = mybir.ActivationFunctionType
AX = mybir.AxisListType

P = 128
N, E, D, T, FE = 6250, 206250, 128, 3, 64
NB = -(-N // P)
NFULL = N // P
NREST = N - NFULL * P
NP = NB * P
NO_NODE = NP

EC = E // P
MAIN = EC * P
EREST = E - MAIN
C = EC + 1

U, Q = 4, 4
GE = U * P
NG = -(-((E + NB * (GE - 1)) // GE) // Q) * Q
TP = NG * U
STEPS = NG // Q
EPAD = E + GE
OUTSIDE = 1 << 22

SU, SQ = 13, 4
SSTEPS = C // (SU * SQ)
assert SSTEPS * SU * SQ == C

KEY, DST, WGT, SRCF, SLOC, POS2, IDX0 = range(7)
NF = 7
KT = 8192
assert KT > NP + P
R_DLOC, R_WGT, R_SRCF, R_SLOC, R_POS2 = range(5)
NR = 5
MONE, MLOC = D, D + 1
MW = D + 2
FILL = 16
assert TP % FILL == 0 and TP // FILL == STEPS
EPS = 1e-5
MIN_NORM = 1e-15
MAX_NORM = 1.0 - 0.004


def at_least(eng, sem, value):
    if not isinstance(value, int) or value > 0:
        eng.wait_ge(sem, value)


def in_steps(eng, n, body):
    body(0)
    with eng.Fori(1, n, 1) as i:
        body(i)


def build(nc, x, src, dst, attr, etype, weight, ntype, w_e, b_e, w_n, b_n, w1, b1, w3, w3e, b3, out):
    ctx = ExitStack()
    with ctx:
        ctx.enter_context(nc.allow_non_contiguous_dma(reason="node types, leftover edges"))

        def sb(name, cols, dt=F32, rows=P):
            return ctx.enter_context(nc.sbuf_tensor(name, [rows, cols], dt))

        def sem(name):
            return ctx.enter_context(nc.semaphore(name))

        def sems(name, n):
            return [sem(f"{name}{i}") for i in range(n)]

        edge_fields = nc.dram_tensor("edge_fields", (EPAD, NF), F32, kind="Internal").ap()
        edge_feats = nc.dram_tensor("edge_feats", (EPAD, FE), F32, kind="Internal").ap()
        sorted_msgs = nc.dram_tensor("sorted_msgs", (P, TP * MW), F32, kind="Internal").ap()
        typed_msgs = nc.dram_tensor("typed_msgs", (NP, T * D), F32, kind="Internal").ap()
        table2 = nc.dram_tensor("table2", (NP, D), F32, kind="Internal").ap()
        table3 = nc.dram_tensor("table3", (NP, D), F32, kind="Internal").ap()

        X = sb("X", NB * D)
        X3 = X[:, :].rearrange("p (b f) -> p b f", b=NB)
        ident = sb("ident", P)
        before = sb("before", P)
        ones = sb("ones", P)
        iota = sb("iota", T * P)
        weT = sb("weT", T * D)
        wnT = sb("wnT", (T + 1) * T * D)
        w1s = sb("w1s", D)
        w3s = sb("w3s", D)
        w3es = sb("w3es", D, rows=FE)
        w3eT = sb("w3eT", FE)
        w3ew = sb("w3ew", D, rows=FE)
        be_row = sb("be_row", T * D, rows=1)
        bn_row = sb("bn_row", T * D, rows=1)
        b1b = sb("b1b", D)
        b3b = sb("b3b", D)
        ntype_i = sb("ntype_i", NB, I32)
        ntype_f = sb("ntype_f", NB)
        nmask = sb("nmask", T * NB)
        bucket_of = [sb(f"bucket_of{i}", NG, I32, rows=1) for i in range(2)]
        start_of = sb("start_of", NG, I32, rows=1)
        node0 = sb("node0", NG)
        is_sorted = sb("is_sorted", 2, I32, rows=1)
        R = sb("R", TP * NR)
        R3 = R[:, :].rearrange("p (t r) -> p t r", r=NR)
        small = sb("small", 20 * NB)
        big_words = (nc.sbuf_bytes_remaining // 4) // 16 * 16 - 64
        big = sb("big", big_words)

        def cut(at, n):
            assert at + n <= big_words, (at, n, big_words)
            return big[:, at:at + n], at + n

        def cut4(at, width):
            c, at = cut(at, Q * U * width)
            return c.rearrange("p (q u r) -> p q u r", q=Q, u=U), at

        ps = [ctx.enter_context(nc.psum_tensor(f"ps{i}", [P, 512], F32)) for i in range(8)]

        Fc, at = cut(0, C * NF)
        F3 = Fc.rearrange("p (c r) -> p c r", r=NF)
        cols = []
        for _ in range(4):
            c, at = cut(at, C)
            cols.append(c)
        dst_i, src_i, typ_i = (c.bitcast(I32) for c in cols[:3])
        w_c = cols[3]
        next_c, at = cut(at, C)
        next_i = next_c.bitcast(I32)
        buckets = []
        for _ in range(2):
            c, at = cut(at, C // 2)
            buckets.append(c.bitcast(BF16))
        dbkt, sbkt = buckets
        masks = []
        for _ in range(2):
            c, at = cut(at, C // 2)
            masks.append(c.bitcast(I16))
        scans = []
        for _ in range(2):
            c, at = cut(at, C)
            scans.append(c)
        pos, at = cut(at, C)
        tmp = scans[0]
        sfeat, _ = cut(C * NF, SQ * SU * FE)
        sfeat4 = sfeat.rearrange("p (q u r) -> p q u r", q=SQ, u=SU)
        sfield, _ = cut(C * NF + SQ * SU * FE, SQ * SU * NF)
        sfield4 = sfield.rearrange("p (q u r) -> p q u r", q=SQ, u=SU)
        sidx, _ = cut(C * NF + SQ * SU * (FE + NF), SQ * SU)
        sidx3 = sidx.bitcast(I32).rearrange("p (q u) -> p q u", q=SQ)
        assert SQ * SU * (FE + NF + 1) <= 4 * C
        r_at = [0]

        def room(n):
            r_at[0] += n
            assert r_at[0] <= TP * NR
            return R[:, r_at[0] - n:r_at[0]]

        iota_g = room(NG)
        past = room(NG)
        wnat = room((T + 1) * T * D).rearrange("p (t i) -> p t i", t=T)
        wenat = room(T * D).rearrange("p (t i) -> p t i", t=T)
        xsts, xTs, mrows = ([room(D) for _ in range(2)], [room(D) for _ in range(2)], [room(T * D) for _ in range(2)])
        fillf = room(U * NF)
        fille = room(U * FE)
        e0f = room(NG)
        Tb = [small[:, i * NB:(i + 1) * NB] for i in range(2)]
        groups_i = small[:, 2 * NB:3 * NB].bitcast(I32)
        groups_f = small[:, 3 * NB:4 * NB]
        ends = [small[:, 4 * NB:5 * NB], small[:, 5 * NB:6 * NB]]
        starts = small[:, 6 * NB:7 * NB]
        bases = [small[:, 7 * NB:8 * NB], small[:, 8 * NB:9 * NB]]
        ahead = small[:, 9 * NB:10 * NB]
        steps_ = small[:, 10 * NB:11 * NB]
        endcol = small[:, 11 * NB:11 * NB + 4]
        viol = small[:, 12 * NB:12 * NB + 4]

        s_edges = sem("s_edges")
        s_rest = sem("s_rest")
        s_x = sem("s_x")
        s_w = sem("s_w")
        s_cst = sem("s_cst")
        s_filler = sem("s_filler")
        s_fillf = sem("s_fillf")
        s_v1 = sem("s_v1")
        s_tot = sem("s_tot")
        s_pref = sem("s_pref")
        s_end = sem("s_end")
        s_endT = sem("s_endT")
        s_past = sem("s_past")
        s_pastp = sem("s_pastp")
        s_viol = sem("s_viol")
        s_violp = sem("s_violp")
        s_wT = sem("s_wT")
        s_wTe = sem("s_wTe")
        s_xs = sem("s_xs")
        s_xT = sem("s_xT")
        s_xTe = sem("s_xTe")
        s_m = sem("s_m")
        s_me = sem("s_me")
        s_mst = sems("s_mst", 2)
        s_pads = sem("s_pads")

        with nc.Block() as block:
            @block.sync
            def _(sp):
                for col, a in ((src_i, src), (dst_i, dst), (typ_i, etype), (w_c, weight)):
                    sp.dma_start(col[:, 0:EC], a[0:MAIN].rearrange("(p c) -> p c", p=P)).then_inc(s_edges, 16)
                sp.dma_start(next_i[:, 0:EC], dst[1:MAIN + 1].rearrange("(p c) -> p c", p=P)).then_inc(s_edges, 16)
                sp.wait_ge(s_filler, 7)
                for col, a in ((dst_i, dst), (src_i, src), (typ_i, etype), (w_c, weight)):
                    sp.dma_start(col[0:EREST, EC:C], a[MAIN:E].rearrange("(p c) -> p c", c=1)).then_inc(s_rest, 16)
                sp.dma_start(next_i[0:EREST - 1, EC:C], dst[MAIN + 1:E].rearrange("(p c) -> p c", c=1)).then_inc(s_rest, 16)
                sp.dma_start(ntype_i[:, 0:NFULL], ntype[0:NFULL * P].rearrange("(b p) -> p b", p=P)).then_inc(s_rest, 16)
                sp.dma_start(ntype_i[0:NREST, NFULL:NB], ntype[NFULL * P:N].rearrange("(p c) -> p c", c=1)).then_inc(s_rest, 16)
                sp.wait_ge(s_fillf, 6)
                sp.dma_start(edge_fields[E:EPAD, :].rearrange("(p u) r -> p (u r)", u=U), fillf).then_inc(s_pads, 16)
                sp.dma_start(edge_feats[E:EPAD, :].rearrange("(p u) r -> p (u r)", u=U), fille).then_inc(s_pads, 16)
                sp.wait_ge(s_pads, 32)

                def pair(i, n=2):
                    for k in range(n):
                        sp.wait_ge(s_me, i * 2 + (k + 1))
                        sp.dma_start(typed_msgs[bass.ds(i * (2 * P) + k * P, P), :], mrows[k]).then_inc(s_mst[k], 16)
                in_steps(sp, NB // 2, pair)
                pair(NB // 2, 1)
                sp.wait_ge(s_mst[0], 16 * (NB // 2 + 1))
                sp.wait_ge(s_mst[1], 16 * (NB // 2))

            @block.gpsimd
            def _(pool):
                pool.memset(ident[:, :], 0.0).then_inc(s_cst, 1)
                pool.memset(before[:, :], 1.0).then_inc(s_cst, 1)
                pool.memset(ones[:, :], 1.0).then_inc(s_cst, 1)
                pool.iota(iota[:, :], pattern=[[KT, T], [1, P]], base=0, channel_multiplier=0,
                          allow_small_or_imprecise_dtypes=True).then_inc(s_cst, 1)
                pool.iota(iota_g, pattern=[[1, NG]], base=0, channel_multiplier=0,
                          allow_small_or_imprecise_dtypes=True).then_inc(s_cst, 1)
                pool.wait_ge(s_cst, 5)
                pool.affine_select(out=ident[:, :], in_=ident[:, :], compare_op=ALU.not_equal, fill=1.0,
                                   base=0, pattern=[[-1, P]], channel_multiplier=1).then_inc(s_cst, 1)
                pool.affine_select(out=before[:, :], in_=before[:, :], compare_op=ALU.is_gt, fill=0.0,
                                   base=0, pattern=[[1, P]], channel_multiplier=-1).then_inc(s_cst, 1)

            @block.scalar
            def _(act):
                act.dma_start(wenat, w_e.rearrange("t o i -> o t i")).then_inc(s_w, 16)
                act.dma_start(wnat, w_n.rearrange("t o i -> o t i")).then_inc(s_w, 16)
                for t, a in ((w1s, w1), (w3s, w3), (w3es, w3e)):
                    act.dma_start(t[:, :], a).then_inc(s_w, 16)
                act.dma_start(be_row[:, :], b_e.rearrange("t (o f) -> o (t f)", o=1)).then_inc(s_w, 16)
                act.dma_start(bn_row[:, :], b_n.rearrange("t (o f) -> o (t f)", o=1)).then_inc(s_w, 16)
                act.dma_start(b1b[:, :], b1.rearrange("(o f) -> o f", o=1).to_broadcast([P, D])).then_inc(s_w, 16)
                act.dma_start(b3b[:, :], b3.rearrange("(o f) -> o f", o=1).to_broadcast([P, D])).then_inc(s_w, 16)
                act.dma_start(X3[:, 0:NFULL, :], x[0:NFULL * P, :].rearrange("(b p) f -> p b f", p=P)).then_inc(s_x, 16)
                act.wait_ge(s_filler, 7)
                act.dma_start(X3[0:NREST, NFULL, :], x[NFULL * P:N, :]).then_inc(s_x, 16)
                act.wait_ge(s_wT, T)
                act.copy(weT[:, :], ps[0][:, 0:T * D]).then_inc(s_wTe, 1)
                for c in range(T + 1):
                    act.wait_ge(s_wT, T + T * (c + 1))
                    act.copy(wnT[:, c * T * D:(c + 1) * T * D], ps[1 + c][:, 0:T * D]).then_inc(s_wTe, 1)
                act.wait_ge(s_wT, T + T * (T + 1) + 1)
                act.copy(w3eT[:, :], ps[5][:, 0:FE]).then_inc(s_wTe, 1)
                act.wait_ge(s_wT, T + T * (T + 1) + 2)
                act.copy(w3ew[:, :], ps[6][0:FE, 0:D]).then_inc(s_wTe, 1)
                act.wait_ge(s_x, 32)

                def pair(i, n=2):
                    for k in range(n):
                        at_least(act, s_xT, i * 2 + (k - 1))
                        act.copy(xsts[k], X[:, bass.ds(i * (2 * D) + k * D, D)]).then_inc(s_xs, 1)
                    for k in range(n):
                        act.wait_ge(s_xT, i * 2 + (k + 1))
                        act.copy(xTs[k], ps[k][:, 0:P]).then_inc(s_xTe, 1)
                    for k in range(n):
                        act.wait_ge(s_m, i * 2 + (k + 1))
                        at_least(act, s_mst[k], i * 16)
                        act.activation(mrows[k], ps[6 + k][:, 0:T * D], ACT.Relu).then_inc(s_me, 1)
                in_steps(act, NB // 2, pair)
                pair(NB // 2, 1)

            @block.tensor
            def _(pe):
                pe.wait_ge(s_w, 16 * 9)
                pe.wait_ge(s_cst, 7)
                for t in range(T):
                    pe.transpose(ps[0][:, t * D:(t + 1) * D], wenat[:, t, :], ident[:, :]).then_inc(s_wT, 1)
                for c in range(T + 1):
                    for t in range(T):
                        pe.transpose(ps[1 + c][:, t * D:(t + 1) * D], wnat[:, t, c * D:(c + 1) * D],
                                     ident[:, :]).then_inc(s_wT, 1)
                pe.transpose(ps[5][:, 0:FE], w3es[:, :], ident[0:FE, 0:FE]).then_inc(s_wT, 1)
                pe.wait_ge(s_wTe, T + 3)
                pe.matmul(ps[6][0:FE, 0:D], w3eT[:, :], w3s[:, :], start=True, stop=True).then_inc(s_wT, 1)
                pe.wait_ge(s_wTe, T + 4)

                def pair(i, n=2):
                    for k in range(n):
                        pe.wait_ge(s_xs, i * 2 + (k + 1))
                        pe.transpose(ps[k][:, 0:P], xsts[k], ident[:, :]).then_inc(s_xT, 1)
                    for k in range(n):
                        pe.wait_ge(s_xTe, i * 2 + (k + 1))
                        at_least(pe, s_me, i * 2)
                        pe.matmul(ps[6 + k][:, 0:T * D], xTs[k], weT[:, :], start=True, stop=False)
                        pe.matmul(ps[6 + k][:, 0:T * D], ones[0:1, :], be_row[:, :], start=False, stop=True).then_inc(s_m, 1)
                in_steps(pe, NB // 2, pair)
                pair(NB // 2, 1)

                for k in range(2):
                    pe.wait_ge(s_tot, k + 1)
                    pe.matmul(ps[2 + k][:, 0:NB], before[:, :], Tb[k], start=True, stop=True).then_inc(s_pref, 1)
                    pe.matmul(ps[2 + k][:, 64:64 + NB], ones[:, :], Tb[k], start=True, stop=True).then_inc(s_pref, 1)
                    pe.wait_ge(s_end, k + 1)
                    pe.transpose(ps[4][0:NB, 0:P], ends[k], ident[:, :]).then_inc(s_endT, 1)
                    pe.transpose(ps[4][0:NB, P:2 * P], steps_, ident[:, :]).then_inc(s_endT, 1)
                    pe.wait_ge(s_past, k + 1)
                    pe.matmul(ps[5][:, 0:NG], ones[0:NB, :], past[0:NB, :], start=True, stop=True).then_inc(s_pastp, 1)
                    pe.matmul(ps[2 + k][0:1, 0:NG], endcol[0:NB, 2:3], past[0:NB, :], start=True, stop=True).then_inc(s_pastp, 1)
                pe.wait_ge(s_viol, 1)
                pe.matmul(ps[4][0:1, 0:1], viol[:, 0:1], ones[:, 0:1], start=True, stop=True).then_inc(s_violp, 1)

            def count_on(dve, start=0):
                n = [start]

                def do(ins):
                    n[0] += 1
                    ins.then_inc(s_v1, 1)
                    return n[0]

                def link(ins):
                    dve.wait_ge(s_v1, do(ins))
                return n, do, link

            def place(dve, do, link, bkt, base):
                link(dve.memset(pos, float(OUTSIDE)))
                masked, scanned, picked = {}, {}, {}
                for b in range(NB + 2):
                    if b < NB:
                        if b >= 2:
                            dve.wait_ge(s_v1, picked[b - 2])
                        masked[b] = do(dve.tensor_scalar(masks[b % 2], bkt, float(b), None, ALU.is_equal))
                    if 1 <= b <= NB:
                        dve.wait_ge(s_v1, masked[b - 1])
                        scanned[b - 1] = do(dve.tensor_tensor_scan(scans[(b - 1) % 2], masks[(b - 1) % 2], masks[(b - 1) % 2],
                                                                   base[:, b - 1:b], ALU.add, ALU.bypass))
                        dve.wait_ge(s_v1, scanned[b - 1])
                        picked[b - 1] = do(dve.copy_predicated(pos, masks[(b - 1) % 2], scans[(b - 1) % 2]))
                dve.wait_ge(s_v1, picked[NB - 1])

            steps_done = [0]

            @block.vector
            def _(dve):
                n, do, link = count_on(dve)
                dve.memset(dst_i[:, EC:C], NO_NODE).then_inc(s_filler, 1)
                dve.memset(src_i[:, EC:C], NO_NODE).then_inc(s_filler, 1)
                dve.memset(typ_i[:, EC:C], 0).then_inc(s_filler, 1)
                dve.memset(w_c[:, EC:C], 0.0).then_inc(s_filler, 1)
                dve.memset(next_i[:, EC:C], NO_NODE).then_inc(s_filler, 1)
                dve.memset(X3[:, NFULL, :], 0.0).then_inc(s_filler, 1)
                dve.memset(ntype_i[:, NFULL:NB], 0).then_inc(s_filler, 1)
                f3 = fillf.rearrange("p (u r) -> p u r", u=U)
                dve.memset(f3[:, :, KEY:DST + 1], float(NO_NODE)).then_inc(s_fillf, 1)
                dve.memset(f3[:, :, WGT:SRCF + 1], 0.0).then_inc(s_fillf, 1)
                dve.memset(f3[:, :, SLOC:SLOC + 1], -1.0).then_inc(s_fillf, 1)
                dve.memset(f3[:, :, POS2:POS2 + 1], float(OUTSIDE)).then_inc(s_fillf, 1)
                dve.memset(f3[:, :, IDX0:IDX0 + 1].bitcast(I32), 0).then_inc(s_fillf, 1)
                dve.memset(fille, 0.0).then_inc(s_fillf, 1)

                dve.wait_ge(s_edges, 16 * 5)
                dve.wait_ge(s_rest, 16 * 7)
                tmp_i = tmp.bitcast(I32)
                a = do(dve.tensor_copy(F3[:, :, DST], dst_i))
                a = do(dve.tensor_copy(F3[:, :, SRCF], src_i))
                do(dve.tensor_copy(F3[:, :, WGT], w_c))
                link(dve.tensor_scalar(tmp_i, dst_i, 7, None, ALU.logical_shift_right))
                link(dve.tensor_copy(dbkt, tmp_i))
                link(dve.tensor_scalar(tmp_i, src_i, 7, None, ALU.logical_shift_right))
                link(dve.tensor_copy(sbkt, tmp_i))
                link(dve.tensor_copy(tmp, typ_i))
                do(dve.scalar_tensor_tensor(F3[:, :, SLOC], sbkt, -float(P), F3[:, :, SRCF], ALU.mult, ALU.add))
                do(dve.scalar_tensor_tensor(F3[:, :, KEY], tmp, float(KT), F3[:, :, DST], ALU.mult, ALU.add))
                do(dve.scalar_tensor_tensor(F3[:, :, IDX0].bitcast(I32), F3[:, :, SRCF], float(T), tmp, ALU.mult, ALU.add))
                link(dve.tensor_copy(ntype_f[:, :], ntype_i[:, :]))
                for t in range(T):
                    do(dve.tensor_scalar(nmask[:, t * NB:(t + 1) * NB], ntype_f[:, :], float(t), None, ALU.is_equal))
                link(dve.tensor_tensor(scans[1], dst_i, next_i, ALU.is_gt))
                link(dve.tensor_reduce(out=viol[:, 0:1], in_=scans[1], axis=AX.X, op=ALU.add))
                dve.sem_inc(s_viol, 1)

                for k, bkt in enumerate((dbkt, sbkt)):
                    tot, end, base = Tb[k], ends[k], bases[k]
                    last = [0, 0]
                    for b in range(NB):
                        at_least(dve, s_v1, last[b % 2])
                        last[b % 2] = do(dve.tensor_scalar(masks[b % 2], bkt, float(b), 0.0, ALU.is_equal, ALU.add,
                                                           accum_out=tot[:, b:b + 1]))
                    dve.wait_ge(s_v1, n[0])
                    dve.sem_inc(s_tot, 1)
                    dve.wait_ge(s_pref, 2 * k + 2)
                    total = ps[2 + k][:, 64:64 + NB]
                    link(dve.tensor_scalar(groups_f, total, float(GE - 1), None, ALU.add))
                    link(dve.tensor_copy(groups_i, groups_f))
                    link(dve.tensor_scalar(groups_i, groups_i, 9, None, ALU.logical_shift_right))
                    link(dve.tensor_copy(groups_f, groups_i))
                    link(dve.tensor_tensor_scan(end, groups_f, groups_f, 0.0, ALU.add, ALU.bypass))
                    link(dve.tensor_tensor(starts, end, groups_f, ALU.subtract))
                    if k:
                        link(dve.scalar_tensor_tensor(base, starts, float(GE), ps[2 + k][:, 0:NB], ALU.mult, ALU.add))
                    else:
                        link(dve.tensor_copy(viol[:, 2:3], total[:, 0:1]))
                        link(dve.tensor_copy(groups_f, total))
                        link(dve.tensor_tensor_scan(base, groups_f, groups_f, 0.0, ALU.add, ALU.bypass))
                        link(dve.tensor_tensor(base, base, groups_f, ALU.subtract))
                        link(dve.scalar_tensor_tensor(ahead, starts, -float(GE), base, ALU.mult, ALU.add))
                        link(dve.memset(steps_[:, NB - 1:NB], 0.0))
                        link(dve.tensor_tensor(steps_[:, 0:NB - 1], ahead[:, 1:NB], ahead[:, 0:NB - 1], ALU.subtract))
                        link(dve.tensor_tensor(base, base, ps[2 + k][:, 0:NB], ALU.add))
                    dve.sem_inc(s_end, 1)
                    dve.wait_ge(s_endT, 2 * k + 2)
                    do(dve.tensor_copy(endcol[0:NB, k:k + 1], ps[4][0:NB, 0:1]))
                    link(dve.tensor_copy(endcol[0:NB, 2:3], ps[4][0:NB, P:P + 1]))
                    link(dve.tensor_scalar(past[0:NB, :], iota_g[0:NB, :], endcol[0:NB, k:k + 1], None, ALU.is_ge))
                    dve.sem_inc(s_past, 1)
                    dve.wait_ge(s_pastp, 2 * k + 2)
                    do(dve.tensor_scalar(bucket_of[k][:, :], ps[5][0:1, 0:NG], float(NB - 1), None, ALU.min))
                    if not k:
                        do(dve.tensor_scalar(node0[:, :], ps[5][:, 0:NG], float(NB - 1), float(P), ALU.min, ALU.mult))
                        link(dve.scalar_tensor_tensor(e0f[0:1, :], iota_g[0:1, :], float(GE), ps[2][0:1, 0:NG],
                                                      ALU.mult, ALU.add))
                        link(dve.tensor_scalar(start_of[:, :], e0f[0:1, :], float(E), None, ALU.min))
                    else:
                        dve.wait_ge(s_v1, n[0])
                place(dve, do, link, sbkt, bases[1])
                t_i, u_i = tmp.bitcast(I32), scans[1].bitcast(I32)
                link(dve.tensor_scalar(t_i, pos, -1.0, None, ALU.add))
                link(dve.tensor_scalar(u_i, t_i, P - 1, None, ALU.bitwise_and))
                link(dve.tensor_scalar(t_i, t_i, 7, None, ALU.logical_shift_right))
                link(dve.tensor_copy(pos, u_i))
                link(dve.tensor_copy(scans[1], t_i))
                link(dve.scalar_tensor_tensor(F3[:, :, POS2], pos, float(TP), scans[1], ALU.mult, ALU.add))
                dve.wait_ge(s_violp, 1)
                link(dve.tensor_scalar(is_sorted[:, 0:1], ps[4][0:1, 0:1], 0.0, None, ALU.is_equal))
                steps_done[0] = n[0]

        s_turn = sem("s_turn")
        s_placed = sem("s_placed")
        s_fields = sem("s_fields")
        s_sfeat = sems("s_sfeat", SQ)
        s_sextra = sem("s_sextra")
        s_sfield = sems("s_sfield", SQ)
        s_srow = sems("s_srow", SQ)
        attr_main = attr[0:MAIN, :].rearrange("(p c) f -> p (c f)", p=P)

        with nc.Block() as block:
            @block.sync
            def _(sp):
                given = sp.value_load(is_sorted[0:1, 0:1], min_val=0, max_val=1)
                with sp.If(given == 1):
                    sp.dma_start(edge_fields[0:MAIN, :].rearrange("(p c) r -> p (c r)", p=P),
                                 Fc[:, 0:EC * NF]).then_inc(s_fields, 16)
                    sp.dma_start(edge_fields[MAIN:E, :], F3[0:EREST, EC, :]).then_inc(s_fields, 16)
                    sp.wait_ge(s_fields, 32)
                with sp.If(given == 0):
                    def step(i, last=False):
                        for h in range(SQ):
                            at_least(sp, s_srow[h], i * (2 * 16 * SU))
                            n = SU - 1 if last and h == SQ - 1 else SU
                            sp.dma_start(sfeat4[:, h, 0:n, :],
                                         attr_main[:, bass.ds(i * (SQ * SU * FE) + h * (SU * FE), n * FE)]
                                         .rearrange("p (u f) -> p u f", u=n)).then_inc(s_sfeat[h], 16)
                    sp.wait_ge(s_placed, 1)
                    step(0)
                    with sp.Fori(1, SSTEPS - 1, 1) as i:
                        step(i)
                    step(SSTEPS - 1, last=True)
                    sp.dma_start(sfeat4[0:EREST, SQ - 1, SU - 1, :], attr[MAIN:E, :]).then_inc(s_sextra, 16)

            @block.vector
            def _(dve):
                given = dve.value_load(is_sorted[0:1, 0:1], min_val=0, max_val=1)
                with dve.If(given == 0):
                    n, do, link = count_on(dve, steps_done[0])
                    place(dve, do, link, dbkt, bases[0])
                    link(dve.tensor_scalar(pos.bitcast(I32), pos, -1.0, None, ALU.add))
                    link(dve.memset(sfeat, 0.0))
                    dve.sem_inc(s_placed, 1)

                    def step(i):
                        for h in range(SQ):
                            at_least(dve, s_srow[h], i * (2 * 16 * SU))
                            dve.tensor_copy(sfield4[:, h, :, :], F3[:, bass.ds(i * (SQ * SU) + h * SU, SU), :]).then_inc(s_sfield[h], 1)
                            dve.tensor_copy(sidx3[:, h, :], pos.bitcast(I32)[:, bass.ds(i * (SQ * SU) + h * SU, SU)]).then_inc(s_sfield[h], 1)
                    in_steps(dve, SSTEPS, step)

            @block.gpsimd
            def _(pool):
                given = pool.value_load(is_sorted[0:1, 0:1], min_val=0, max_val=1)
                with pool.If(given == 0):
                    beyond = pool.to_reg(E - 1)

                    def step(i, last=False):
                        for h in range(SQ):
                            pool.wait_ge(s_sfeat[h], i * 16 + 16)
                            pool.wait_ge(s_sfield[h], i * 2 + 2)
                            if last and h == SQ - 1:
                                pool.wait_ge(s_sextra, 16)
                            pool.sem_inc(s_turn, 1)
                            for u in range(SU):
                                for table, ring in ((edge_feats, sfeat4), (edge_fields, sfield4)):
                                    pool.indirect_dma_start(
                                        out=table, out_offset=bass.IndirectOffsetOnAxis(ap=sidx3[:, h, u:u + 1], axis=0),
                                        in_=ring[:, h, u, :], in_offset=None,
                                        bounds_check=beyond, oob_is_err=False).then_inc(s_srow[h], 16)
                    step(0)
                    with pool.Fori(1, SSTEPS - 1, 1) as i:
                        step(i)
                    step(SSTEPS - 1, last=True)
                    for h in range(SQ):
                        pool.wait_ge(s_srow[h], SSTEPS * 2 * 16 * SU)

        acc, at = cut(0, NB * T * P)
        fld4, at = cut4(at, NF)
        fld4i = fld4.bitcast(I32)
        rel, at = cut(at, Q * U)
        rel3 = rel.rearrange("p (q u) -> p q u", q=Q)
        got4, at = cut4(at, D)
        hot4, at = cut4(at, T * P)
        FILL2 = 8
        fill2, at = cut(at, FILL2 * MW)

        s_hot = sems("s_hot", Q)
        s_mm = sems("s_mm", Q)
        s_acc = sems("s_acc", Q)
        s_fld = sems("s_fld", Q)
        s_kept = sems("s_kept", Q)
        s_got = sems("s_got", Q)
        s_rel = sems("s_rel", Q)
        s_zero = sem("s_zero")
        s_fill2 = sem("s_fill2")
        s_fills2 = sem("s_fills2")
        s_feats = sem("s_feats")
        s_feats2 = sem("s_feats2")
        typed_rows = typed_msgs.rearrange("n (t f) -> (n t) f", t=T)

        def sums_up(dve, k, h, i, acc_at, part_of, base):
            b = dve.value_load(bucket_of[k][0:1, bass.ds(i * Q + h, 1)], min_val=0, max_val=NB - 1)
            dve.wait_ge(s_mm[h], i + (1 + base))
            at_least(dve, s_acc[h - 1] if h else s_acc[Q - 1], i + (1 + base) if h else i + base)
            last = None
            for a, part in zip(acc_at(b), part_of(h)):
                last = dve.tensor_tensor(a, part, a, ALU.add)
            last.then_inc(s_acc[h], 1)

        LAG = 2

        def hot_then_add(dve, one_hot, add):
            def step(i):
                for h in range(Q):
                    one_hot(i, h)
                    if h >= LAG:
                        add(i, h - LAG)
                    elif not isinstance(i, int) or i > 0:
                        add(i - 1, h + Q - LAG)
            in_steps(dve, STEPS, step)
            for h in range(Q - LAG, Q):
                add(STEPS - 1, h)

        with nc.Block() as block:
            @block.sync
            def _(sp):
                given = sp.value_load(is_sorted[0:1, 0:1], min_val=0, max_val=1)
                sp.dma_start(edge_feats[0:MAIN, :].rearrange("(p c) f -> p (c f)", p=P), attr_main,
                             cond=given).then_inc(s_feats, 16)
                sp.dma_start(edge_feats[MAIN:E, :], attr[MAIN:E, :], cond=given).then_inc(s_feats2, 16)
                sp.wait_ge(s_fill2, 2)

                def step(i):
                    for h in range(Q):
                        e0 = sp.value_load(start_of[0:1, bass.ds(i * Q + h, 1)], min_val=0, max_val=E)
                        at_least(sp, s_mm[h], i)
                        at_least(sp, s_kept[h], i)
                        sp.dma_start(fld4[:, h, :, :], edge_fields[bass.ds(e0, GE), :]
                                     .rearrange("(p u) r -> p u r", u=U)).then_inc(s_fld[h], 16)
                    for k in range(2):
                        sp.dma_start(sorted_msgs[:, bass.ds(i * (2 * FILL2 * MW) + k * FILL2 * MW, FILL2 * MW)],
                                     fill2).then_inc(s_fills2, 16)
                in_steps(sp, STEPS, step)
                sp.wait_ge(s_fills2, 32 * STEPS)

            @block.gpsimd
            def _(pool):
                def step(i):
                    for h in range(Q):
                        pool.wait_ge(s_fld[h], i * 16 + 16)
                        at_least(pool, s_mm[h], i)
                        pool.sem_inc(s_turn, 1)
                        for u in range(U):
                            pool.indirect_dma_start(
                                out=got4[:, h, u, :], out_offset=None, in_=typed_rows,
                                in_offset=bass.IndirectOffsetOnAxis(ap=fld4i[:, h, u, IDX0:IDX0 + 1], axis=0)
                            ).then_inc(s_got[h], 16)
                in_steps(pool, STEPS, step)

            @block.scalar
            def _(act):
                def step(i):
                    for h in range(Q):
                        act.wait_ge(s_fld[h], i * 16 + 16)
                        act.copy(R3[:, bass.ds(i * (Q * U) + h * U, U), R_WGT:NR], fld4[:, h, :, WGT:POS2 + 1]).then_inc(s_kept[h], 1)
                in_steps(act, STEPS, step)

            @block.vector
            def _(dve):
                f2 = fill2.rearrange("p (u r) -> p u r", u=FILL2)
                dve.memset(fill2, 0.0).then_inc(s_fill2, 1)
                dve.wait_ge(s_fill2, 1)
                dve.memset(f2[:, :, MLOC:MLOC + 1], -1.0).then_inc(s_fill2, 1)
                dve.memset(acc, 0.0).then_inc(s_zero, 1)
                dve.wait_ge(s_zero, 1)

                def one_hot(i, h):
                    dve.wait_ge(s_fld[h], i * 16 + 16)
                    at_least(dve, s_mm[h], i)
                    first = node0[:, bass.ds(i * Q + h, 1)]
                    dve.tensor_scalar(R3[:, bass.ds(i * (Q * U) + h * U, U), R_DLOC], fld4[:, h, :, DST], first, None, ALU.subtract)
                    dve.tensor_scalar(rel3[:, h, :], fld4[:, h, :, KEY], first, None, ALU.subtract).then_inc(s_rel[h], 1)
                    dve.wait_ge(s_rel[h], i + 1)
                    for u in range(U):
                        last = dve.tensor_scalar(hot4[:, h, u, :], iota[:, :], rel3[:, h, u:u + 1], None, ALU.is_equal)
                    last.then_inc(s_hot[h], 1)

                def add(i, h):
                    sums_up(dve, 0, h, i, lambda b: [acc[:, bass.ds(b * (T * P), T * P)]],
                            lambda h: [ps[h][:, 0:T * P]], 0)

                hot_then_add(dve, one_hot, add)

            @block.tensor
            def _(pe):
                def step(i):
                    for h in range(Q):
                        pe.wait_ge(s_hot[h], i + 1)
                        pe.wait_ge(s_got[h], i * (16 * U) + 16 * U)
                        at_least(pe, s_acc[h], i)
                        for u in range(U):
                            last = pe.matmul(ps[h][:, 0:T * P], got4[:, h, u, :], hot4[:, h, u, :],
                                             start=(u == 0), stop=(u == U - 1))
                        last.then_inc(s_mm[h], 1)
                in_steps(pe, STEPS, step)

        def sm(i):
            return small[:, i * NB:(i + 1) * NB]

        def along(v):
            return v.unsqueeze(2).to_broadcast([P, NB, D])

        def wide(v):
            return v.rearrange("p (b f) -> p b f", b=NB)

        def sum_of_squares(dve, link, h3, sq3, to):
            link(dve.tensor_tensor(sq3, h3, h3, ALU.mult))
            link(dve.tensor_reduce(out=to, in_=sq3, axis=AX.X, op=ALU.add))

        def layer_norm(dve, link, h3, sq3, ask_sqrt):
            mean, var = sm(0), sm(1)
            link(dve.tensor_reduce(out=mean, in_=h3, axis=AX.X, op=ALU.add))
            link(dve.tensor_scalar(mean, mean, 1.0 / D, None, ALU.mult))
            link(dve.tensor_tensor(h3, h3, along(mean), ALU.subtract))
            sum_of_squares(dve, link, h3, sq3, var)
            link(dve.tensor_scalar(var, var, 1.0 / D, EPS, ALU.mult, ALU.add))
            ask_sqrt(var, sm(2))
            link(dve.reciprocal(sm(2), sm(2)))
            link(dve.tensor_tensor(X3, h3, along(sm(2)), ALU.mult))

        class Chain:

            def __init__(self):
                self.v, self.ask, self.did = sem("s_step"), sem("s_ask"), sem("s_did")
                self.n = self.k = 0
                self.jobs = []

            def on(self, dve):
                self.dve = dve
                self.jobs = []

            def link(self, ins):
                self.n += 1
                ins.then_inc(self.v, 1)
                self.dve.wait_ge(self.v, self.n)

            def func(self, f, i, o, **kw):
                self.k += 1
                self.jobs.append((self.k, f, i, o, kw))
                self.dve.sem_inc(self.ask, 1)
                self.dve.wait_ge(self.did, self.k)

            def sqrt(self, i, o):
                self.func(ACT.Sqrt, i, o)

        h4, sq4, S = (cut(i * NB * D, NB * D)[0] for i in range(3))
        h4 = cut(3 * NB * D, NB * D)[0]
        h43 = wide(h4)
        rest4 = 4 * NB * D
        xTs4, rest4 = cut(rest4, D)
        xst4, rest4 = cut(rest4, D)
        acc_st, rest4 = cut(rest4, T * P)
        sq4 = cut(0, NB * D)[0]
        S = cut(NB * D, NB * D)[0]
        S3, sq43 = wide(S), wide(sq4)
        s_xs4 = sem("s_xs4")
        s_xT4 = sem("s_xT4")
        s_xTe4 = sem("s_xTe4")
        s_o4 = sem("s_o4")
        s_h4 = sem("s_h4")
        chain = Chain()

        with nc.Block() as block:
            @block.tensor
            def _(pe):
                def bucket(b):
                    at_least(pe, s_h4, b * T)
                    pe.wait_ge(s_xs4, b * 2 + 2)
                    pe.transpose(ps[0][:, 0:P], xst4, ident[:, :]).then_inc(s_xT4, 1)
                    for t in range(T):
                        pe.matmul(ps[1][:, 0:T * D], acc_st[:, t * P:(t + 1) * P],
                                  wnT[:, (t + 1) * T * D:(t + 2) * T * D], start=(t == 0), stop=False)
                    pe.matmul(ps[1][:, 0:T * D], ones[0:1, :], bn_row[:, :], start=False, stop=False)
                    pe.wait_ge(s_xTe4, b + 1)
                    pe.matmul(ps[1][:, 0:T * D], xTs4, wnT[:, 0:T * D], start=False, stop=True).then_inc(s_o4, 1)
                in_steps(pe, NB, bucket)

            @block.scalar
            def _(act):
                def bucket(b):
                    at_least(act, s_o4, b)
                    act.activation(xst4, X[:, bass.ds(b * D, D)], ACT.Relu).then_inc(s_xs4, 1)
                    act.copy(acc_st, acc[:, bass.ds(b * (T * P), T * P)]).then_inc(s_xs4, 1)
                    act.wait_ge(s_xT4, b + 1)
                    act.copy(xTs4, ps[0][:, 0:P]).then_inc(s_xTe4, 1)
                in_steps(act, NB, bucket)

            @block.vector
            def _(dve):
                dve.tensor_scalar(h4, X[:, :], 2.0, None, ALU.mult).then_inc(chain.v, 1)
                chain.n = 1
                dve.wait_ge(chain.v, 1)
                def bucket(b):
                    dve.wait_ge(s_o4, b + 1)
                    for t in range(T):
                        at_least(dve, s_h4, b * T + t)
                        dve.scalar_tensor_tensor(h4[:, bass.ds(b * D, D)], ps[1][:, t * D:(t + 1) * D],
                                                 nmask[:, bass.ds(b + t * NB, 1)], h4[:, bass.ds(b * D, D)],
                                                 ALU.mult, ALU.add).then_inc(s_h4, 1)
                in_steps(dve, NB, bucket)

        s_x1 = sem("s_x1")
        s_xs5 = sem("s_xs5")
        s_xT5 = sem("s_xT5")
        s_xTe5 = sem("s_xTe5")
        s_o5 = sem("s_o5")
        s_S5 = sem("s_S5")
        hb5 = sq4[:, 0:D]

        with nc.Block() as block:
            @block.vector
            def _(dve):
                chain.on(dve)
                link = chain.link
                dve.wait_ge(s_h4, T * NB)
                layer_norm(dve, link, h43, sq43, chain.sqrt)
                dve.sem_inc(s_x1, 1)
                n2, norm, z, lo, hi, ser, sel, t0 = (sm(i) for i in range(3, 11))
                sum_of_squares(dve, link, X3, sq43, n2)
                chain.sqrt(n2, norm)
                link(dve.tensor_scalar(norm, norm, MIN_NORM, None, ALU.max))
                link(dve.tensor_scalar(z, norm, 1.0 - 1e-7, None, ALU.min))
                link(dve.tensor_scalar(lo, z, -1.0, 1.0, ALU.mult, ALU.add))
                link(dve.tensor_scalar(hi, z, 1.0, None, ALU.add))
                chain.func(ACT.Ln, lo, lo)
                chain.func(ACT.Ln, hi, hi)
                link(dve.tensor_tensor(hi, hi, lo, ALU.subtract))
                link(dve.tensor_scalar(hi, hi, 0.5, None, ALU.mult))
                link(dve.tensor_tensor(t0, z, z, ALU.mult))
                link(dve.tensor_scalar(ser, t0, 1.0 / 11, 1.0 / 9, ALU.mult, ALU.add))
                for c in (1.0 / 7, 1.0 / 5, 1.0 / 3, 1.0):
                    link(dve.tensor_tensor(ser, ser, t0, ALU.mult))
                    link(dve.tensor_scalar(ser, ser, c, None, ALU.add))
                link(dve.tensor_tensor(ser, ser, z, ALU.mult))
                link(dve.tensor_scalar(sel, z, 0.25, None, ALU.is_lt))
                link(dve.copy_predicated(hi, sel.bitcast(I32), ser))
                link(dve.reciprocal(norm, norm))
                link(dve.tensor_tensor(hi, hi, norm, ALU.mult))
                c1 = small[:, 11 * NB:11 * NB + 8]
                link(dve.tensor_tensor(hb5, b1b[:, :], b1b[:, :], ALU.mult))
                link(dve.tensor_reduce(out=c1[:, 0:1], in_=hb5, axis=AX.X, op=ALU.add))
                chain.sqrt(c1[:, 0:1], c1[:, 1:2])
                link(dve.tensor_scalar(c1[:, 1:2], c1[:, 1:2], MIN_NORM, None, ALU.max))
                chain.func(ACT.Tanh, c1[:, 1:2], c1[:, 2:3])
                link(dve.reciprocal(c1[:, 3:4], c1[:, 1:2]))
                link(dve.tensor_tensor(c1[:, 2:3], c1[:, 2:3], c1[:, 3:4], ALU.mult))
                link(dve.tensor_scalar(b1b[:, :], b1b[:, :], c1[:, 2:3], None, ALU.mult))
                link(dve.tensor_tensor(hb5, b1b[:, :], b1b[:, :], ALU.mult))
                link(dve.tensor_reduce(out=c1[:, 0:1], in_=hb5, axis=AX.X, op=ALU.add))
                chain.sqrt(c1[:, 0:1], c1[:, 1:2])
                link(dve.tensor_scalar(c1[:, 1:2], c1[:, 1:2], MIN_NORM, None, ALU.max))
                link(dve.reciprocal(c1[:, 1:2], c1[:, 1:2]))
                link(dve.tensor_scalar(c1[:, 1:2], c1[:, 1:2], MAX_NORM, 1.0, ALU.mult, ALU.min))
                link(dve.tensor_scalar(b1b[:, :], b1b[:, :], c1[:, 1:2], None, ALU.mult))
                link(dve.tensor_tensor(hb5, b1b[:, :], b1b[:, :], ALU.mult))
                link(dve.tensor_reduce(out=c1[:, 0:1], in_=hb5, axis=AX.X, op=ALU.add))
                y2 = c1[:, 0:1]
                dve.wait_ge(s_S5, NB)
                link(dve.tensor_tensor(S3, S3, along(hi), ALU.mult))
                x2, xy, den, a = sm(3), sm(4), sm(5), sm(6)
                sum_of_squares(dve, link, S3, sq43, x2)
                bias3 = b1b[:, :].unsqueeze(1).to_broadcast([P, NB, D])
                link(dve.tensor_tensor(sq43, S3, bias3, ALU.mult))
                link(dve.tensor_reduce(out=xy, in_=sq43, axis=AX.X, op=ALU.add))
                link(dve.tensor_scalar(xy, xy, 2.0, 1.0, ALU.mult, ALU.add))
                link(dve.tensor_scalar(a, xy, y2, None, ALU.add))
                link(dve.tensor_scalar(den, x2, y2, None, ALU.mult))
                link(dve.tensor_tensor(den, den, xy, ALU.add))
                link(dve.tensor_scalar(den, den, MIN_NORM, None, ALU.max))
                link(dve.reciprocal(den, den))
                link(dve.tensor_tensor(a, a, den, ALU.mult))
                link(dve.tensor_scalar(x2, x2, -1.0, 1.0, ALU.mult, ALU.add))
                link(dve.tensor_tensor(x2, x2, den, ALU.mult))
                link(dve.tensor_tensor(S3, S3, along(a), ALU.mult))
                link(dve.tensor_tensor(sq43, bias3, along(x2), ALU.mult))
                link(dve.tensor_tensor(S3, S3, sq43, ALU.add))
                sum_of_squares(dve, link, S3, sq43, den)
                chain.sqrt(den, a)
                link(dve.tensor_scalar(a, a, MIN_NORM, None, ALU.max))
                link(dve.reciprocal(a, a))
                link(dve.tensor_scalar(a, a, MAX_NORM, 1.0, ALU.mult, ALU.min))
                link(dve.tensor_tensor(S3, S3, along(a), ALU.mult))

            @block.scalar
            def _(act):
                for k, f, i, o, kw in chain.jobs:
                    act.wait_ge(chain.ask, k)
                    act.activation(o, i, f, **kw).then_inc(chain.did, 1)
                    if k == 1:
                        act.wait_ge(s_x1, 1)

                        def bucket(b):
                            at_least(act, s_xT5, b)
                            act.copy(xst4, X[:, bass.ds(b * D, D)]).then_inc(s_xs5, 1)
                            act.wait_ge(s_xT5, b + 1)
                            act.copy(xTs4, ps[0][:, 0:P]).then_inc(s_xTe5, 1)
                            act.wait_ge(s_o5, b + 1)
                            act.copy(S[:, bass.ds(b * D, D)], ps[1][:, 0:D]).then_inc(s_S5, 1)
                        in_steps(act, NB, bucket)

            @block.tensor
            def _(pe):
                def bucket(b):
                    at_least(pe, s_S5, b)
                    pe.wait_ge(s_xs5, b + 1)
                    pe.transpose(ps[0][:, 0:P], xst4, ident[:, :]).then_inc(s_xT5, 1)
                    pe.wait_ge(s_xTe5, b + 1)
                    pe.matmul(ps[1][:, 0:D], xTs4, w1s[:, :], start=True, stop=True).then_inc(s_o5, 1)
                in_steps(pe, NB, bucket)

        kept4, at = cut4(2 * NB * D, NR)
        hotw4, at = cut4(at, P)
        hotT4, at = cut4(at, P)
        msg4, at = cut4(at, MW)
        mrow, at = cut(at, Q * U)
        mrow3 = mrow.rearrange("p (q u) -> p q u", q=Q)
        midx, at = cut(at, Q * U)
        midx3 = midx.bitcast(I32).rearrange("p (q u) -> p q u", q=Q)
        s_one6 = sem("s_one6")
        s_keep6 = sems("s_keep6", Q)
        s_hot6 = sems("s_hot6", Q)
        s_fld6 = sems("s_fld6", Q)
        s_T6 = sems("s_T6", Q)
        s_Te6 = sems("s_Te6", Q)
        s_G6 = sems("s_G6", Q)
        s_Ge6 = sems("s_Ge6", Q)
        s_row6 = sems("s_row6", Q)
        msg_rows = sorted_msgs.rearrange("p (t r) -> (p t) r", r=MW)

        with nc.Block() as block:
            @block.vector
            def _(dve):
                dve.memset(msg4[:, :, :, MONE], 1.0).then_inc(s_one6, 1)

                def step(i):
                    for h in range(Q):
                        at_least(dve, s_T6[h], i)
                        at_least(dve, s_row6[h], i * (16 * U))
                        dve.tensor_copy(kept4[:, h, :, :], R3[:, bass.ds(i * (Q * U) + h * U, U), :]).then_inc(s_keep6[h], 1)
                        dve.wait_ge(s_keep6[h], i * 2 + 1)
                        dve.tensor_scalar(mrow3[:, h, :], kept4[:, h, :, R_DLOC], P - 0.5, float(OUTSIDE),
                                          ALU.is_gt, ALU.mult).then_inc(s_keep6[h], 1)
                        for u in range(U):
                            last = dve.tensor_scalar(hotw4[:, h, u, :], iota[:, 0:P], kept4[:, h, u, R_DLOC:R_DLOC + 1],
                                                     kept4[:, h, u, R_WGT:R_WGT + 1], ALU.is_equal, ALU.mult)
                        last.then_inc(s_hot6[h], 1)
                        dve.wait_ge(s_keep6[h], i * 2 + 2)
                        dve.tensor_tensor(midx3[:, h, :], mrow3[:, h, :], kept4[:, h, :, R_POS2], ALU.add)
                        dve.tensor_copy(msg4[:, h, :, MLOC], kept4[:, h, :, R_SLOC]).then_inc(s_fld6[h], 1)
                in_steps(dve, STEPS, step)

            def turn_then_take(eng, turn, take):
                def step(i):
                    for h in range(Q):
                        turn(i, h)
                        if h:
                            take(i, h - 1)
                        elif not isinstance(i, int) or i > 0:
                            take(i - 1, Q - 1)
                in_steps(eng, STEPS, step)
                take(STEPS - 1, Q - 1)

            @block.tensor
            def _(pe):
                def turn(i, h):
                    pe.wait_ge(s_hot6[h], i + 1)
                    at_least(pe, s_Te6[h], i)
                    for u in range(U):
                        last = pe.transpose(ps[h][:, u * P:(u + 1) * P], hotw4[:, h, u, :], ident[:, :])
                    last.then_inc(s_T6[h], 1)

                def take(i, h):
                    b = pe.value_load(bucket_of[0][0:1, bass.ds(i * Q + h, 1)], min_val=0, max_val=NB - 1)
                    pe.wait_ge(s_Te6[h], i + 1)
                    at_least(pe, s_Ge6[h], i)
                    for u in range(U):
                        last = pe.matmul(ps[4 + h][:, u * D:(u + 1) * D], hotT4[:, h, u, :],
                                         S[:, bass.ds(b * D, D)], start=True, stop=True)
                    last.then_inc(s_G6[h], 1)

                turn_then_take(pe, turn, take)

            @block.scalar
            def _(act):
                def turned(i, h):
                    act.wait_ge(s_T6[h], i + 1)
                    at_least(act, s_G6[h], i)
                    act.copy(hotT4[:, h, :, :], ps[h][:, :].rearrange("p (u f) -> p u f", u=U)).then_inc(s_Te6[h], 1)

                def taken(i, h):
                    act.wait_ge(s_G6[h], i + 1)
                    at_least(act, s_row6[h], i * (16 * U))
                    act.copy(msg4[:, h, :, 0:D], ps[4 + h][:, :].rearrange("p (u f) -> p u f", u=U)).then_inc(s_Ge6[h], 1)

                turn_then_take(act, turned, taken)

            @block.gpsimd
            def _(pool):
                beyond = pool.to_reg(P * TP - 1)
                pool.wait_ge(s_one6, 1)

                def step(i):
                    for h in range(Q):
                        pool.wait_ge(s_Ge6[h], i + 1)
                        pool.wait_ge(s_fld6[h], i + 1)
                        pool.sem_inc(s_turn, 1)
                        for u in range(U):
                            pool.indirect_dma_start(
                                out=msg_rows, out_offset=bass.IndirectOffsetOnAxis(ap=midx3[:, h, u:u + 1], axis=0),
                                in_=msg4[:, h, u, :], in_offset=None,
                                bounds_check=beyond, oob_is_err=False).then_inc(s_row6[h], 16)
                in_steps(pool, STEPS, step)
                for h in range(Q):
                    pool.wait_ge(s_row6[h], STEPS * 16 * U)

        AW = D + 1
        acc7, at = cut(0, NB * AW)
        rec74, at = cut4(at, MW)
        hot74, at = cut4(at, P)
        s_zero7 = sem("s_zero7")
        s_rec7 = sems("s_rec7", Q)
        iota_u = iota[:, 0:P].unsqueeze(1).to_broadcast([P, U, P])

        def hot_of(col):
            return col.unsqueeze(2).to_broadcast([P, U, P])

        with nc.Block() as block:
            @block.sync
            def _(sp):
                def step(i):
                    for h in range(Q):
                        at_least(sp, s_mm[h], i + STEPS)
                        sp.dma_start(rec74[:, h, :, :], sorted_msgs[:, bass.ds(i * (Q * U * MW) + h * (U * MW), U * MW)]
                                     .rearrange("p (u r) -> p u r", u=U)).then_inc(s_rec7[h], 16)
                in_steps(sp, STEPS, step)

            @block.vector
            def _(dve):
                dve.memset(acc7, 0.0).then_inc(s_zero7, 1)
                dve.wait_ge(s_zero7, 1)

                def one_hot(i, h):
                    dve.wait_ge(s_rec7[h], i * 16 + 16)
                    at_least(dve, s_mm[h], i + STEPS)
                    dve.tensor_tensor(hot74[:, h, :, :], iota_u, hot_of(rec74[:, h, :, MLOC]), ALU.is_equal).then_inc(s_hot[h], 1)

                def add(i, h):
                    sums_up(dve, 1, h, i, lambda b: [acc7[:, bass.ds(b * AW, AW)]], lambda h: [ps[h][:, 0:AW]], STEPS)

                hot_then_add(dve, one_hot, add)

            @block.tensor
            def _(pe):
                def step(i):
                    for h in range(Q):
                        pe.wait_ge(s_hot[h], i + (1 + STEPS))
                        at_least(pe, s_acc[h], i + STEPS)
                        for u in range(U):
                            last = pe.matmul(ps[h][:, 0:AW], hot74[:, h, u, :], rec74[:, h, u, 0:AW],
                                             start=(u == 0), stop=(u == U - 1))
                        last.then_inc(s_mm[h], 1)
                in_steps(pe, STEPS, step)

        top = big_words - 2 * NB * D
        sq8 = cut(top, NB * D)[0]
        h8 = cut(top + NB * D, NB * D)[0]
        sq83, h83 = wide(sq8), wide(h8)
        agg7 = acc7.rearrange("p (b f) -> p b f", b=NB)
        y = h8
        dinv = small[:, 12 * NB:13 * NB]
        s_st8 = sem("s_st8")
        s_y8 = sem("s_y8")
        with nc.Block() as block:
            @block.vector
            def _(dve):
                chain.on(dve)
                link = chain.link
                raw, norm, th, f, ne = (sm(i) for i in range(3, 8))
                g = agg7[:, :, 0:D]
                sum_of_squares(dve, link, g, sq83, raw)
                chain.sqrt(raw, raw)
                link(dve.tensor_scalar(norm, raw, MIN_NORM, None, ALU.max))
                chain.func(ACT.Tanh, norm, th)
                link(dve.reciprocal(norm, norm))
                link(dve.tensor_tensor(f, th, norm, ALU.mult))
                link(dve.tensor_tensor(ne, f, raw, ALU.mult))
                link(dve.tensor_scalar(ne, ne, MIN_NORM, None, ALU.max))
                link(dve.reciprocal(ne, ne))
                link(dve.tensor_scalar(ne, ne, MAX_NORM, 1.0, ALU.mult, ALU.min))
                link(dve.tensor_tensor(f, f, ne, ALU.mult))
                link(dve.tensor_tensor(h83, g, along(f), ALU.mult))
                link(dve.tensor_tensor(h83, h83, X3, ALU.add))
                layer_norm(dve, link, h83, sq83, chain.sqrt)
                link(dve.tensor_scalar(dinv, agg7[:, :, D], 1.0, None, ALU.add))
                chain.sqrt(dinv, dinv)
                link(dve.reciprocal(dinv, dinv))
                link(dve.tensor_tensor(wide(y), X3, along(dinv), ALU.mult))
                dve.sem_inc(s_y8, 1)

            @block.scalar
            def _(act):
                for k, f, i, o, kw in chain.jobs:
                    act.wait_ge(chain.ask, k)
                    act.activation(o, i, f, **kw).then_inc(chain.did, 1)

            @block.sync
            def _(sp):
                sp.wait_ge(s_y8, 1)
                sp.dma_start(table2.rearrange("(b p) f -> p b f", p=P), wide(y)).then_inc(s_st8, 16)
                sp.wait_ge(s_st8, 16)

        AW9 = D + 1
        acc9, at = cut(0, NB * AW9)
        got94, at = cut4(at, AW9)
        hot94, at = cut4(at, P)
        gidx, at = cut(at, Q * U)
        gidx3 = gidx.bitcast(I32).rearrange("p (q u) -> p q u", q=Q)
        assert at <= top
        s_zero9 = sem("s_zero9")
        s_idx = sems("s_idx", Q)

        def gather_step(pool, table, to, base):
            def step(i):
                for h in range(Q):
                    pool.wait_ge(s_idx[h], i + (1 + base))
                    at_least(pool, s_mm[h], i + (2 * STEPS + base))
                    pool.sem_inc(s_turn, 1)
                    for u in range(U):
                        pool.indirect_dma_start(
                            out=to[:, h, u, 0:D], out_offset=None, in_=table,
                            in_offset=bass.IndirectOffsetOnAxis(ap=gidx3[:, h, u:u + 1], axis=0)
                        ).then_inc(s_got[h], 16)
            return step

        def index_and_hot(dve, hot, base):
            def one_hot(i, h):
                at_least(dve, s_mm[h], i + (2 * STEPS + base))
                dve.tensor_copy(gidx3[:, h, :], R3[:, bass.ds(i * (Q * U) + h * U, U), R_SRCF]).then_inc(s_idx[h], 1)
                dve.tensor_tensor(hot[:, h, :, :], iota_u, hot_of(R3[:, bass.ds(i * (Q * U) + h * U, U), R_DLOC]),
                                  ALU.is_equal).then_inc(s_hot[h], 1)
            return one_hot

        with nc.Block() as block:
            @block.gpsimd
            def _(pool):
                pool.wait_ge(s_zero9, 2)
                in_steps(pool, STEPS, gather_step(pool, table2, got94, 0))

            @block.vector
            def _(dve):
                dve.memset(acc9, 0.0).then_inc(s_zero9, 1)
                dve.memset(got94[:, :, :, D], 1.0).then_inc(s_zero9, 1)
                dve.wait_ge(s_zero9, 2)

                def add(i, h):
                    sums_up(dve, 0, h, i, lambda b: [acc9[:, bass.ds(b * AW9, AW9)]], lambda h: [ps[h][:, 0:AW9]],
                            2 * STEPS)

                hot_then_add(dve, index_and_hot(dve, hot94, 0), add)

            @block.tensor
            def _(pe):
                def step(i):
                    for h in range(Q):
                        pe.wait_ge(s_hot[h], i + (1 + 2 * STEPS))
                        pe.wait_ge(s_got[h], i * (16 * U) + 16 * U * (1 + STEPS))
                        at_least(pe, s_acc[h], i + 2 * STEPS)
                        for u in range(U):
                            last = pe.matmul(ps[h][:, 0:AW9], hot94[:, h, u, :], got94[:, h, u, :],
                                             start=(u == 0), stop=(u == U - 1))
                        last.then_inc(s_mm[h], 1)
                in_steps(pe, STEPS, step)

        agg9 = acc9.rearrange("p (b f) -> p b f", b=NB)
        degn = small[:, 13 * NB:14 * NB]
        s_st10 = sem("s_st10")
        s_x3 = sem("s_x3")
        with nc.Block() as block:
            @block.vector
            def _(dve):
                chain.on(dve)
                link = chain.link
                link(dve.tensor_tensor(h83, agg9[:, :, 0:D], h83, ALU.add))
                link(dve.tensor_tensor(h83, h83, along(dinv), ALU.mult))
                link(dve.tensor_tensor(h83, h83, X3, ALU.add))
                layer_norm(dve, link, h83, sq83, chain.sqrt)
                dve.sem_inc(s_x3, 1)
                link(dve.tensor_scalar(degn, agg9[:, :, D], 1.0, None, ALU.max))
                chain.sqrt(degn, degn)
                link(dve.reciprocal(degn, degn))

            @block.scalar
            def _(act):
                for k, f, i, o, kw in chain.jobs:
                    act.wait_ge(chain.ask, k)
                    act.activation(o, i, f, **kw).then_inc(chain.did, 1)

            @block.sync
            def _(sp):
                sp.wait_ge(s_x3, 1)
                sp.dma_start(table3.rearrange("(b p) f -> p b f", p=P), X3).then_inc(s_st10, 16)
                sp.wait_ge(s_st10, 16)

        accN, at = cut(0, NB * P)
        accE, at = cut(at, NB * P)
        got114, at = cut4(at, D)
        hot114, at = cut4(at, P)
        feat4, at = cut4(at, FE)
        gidx, at = cut(at, Q * U)
        gidx3 = gidx.bitcast(I32).rearrange("p (q u) -> p q u", q=Q)
        s_zero11 = sem("s_zero11")
        s_feat11 = sems("s_feat11", Q)
        with nc.Block() as block:
            @block.sync
            def _(sp):
                sp.wait_ge(s_feats, 16)
                sp.wait_ge(s_feats2, 16)

                def step(i):
                    for h in range(Q):
                        e0 = sp.value_load(start_of[0:1, bass.ds(i * Q + h, 1)], min_val=0, max_val=E)
                        at_least(sp, s_mm[h], i + 3 * STEPS)
                        sp.dma_start(feat4[:, h, :, :], edge_feats[bass.ds(e0, GE), :]
                                     .rearrange("(p u) r -> p u r", u=U)).then_inc(s_feat11[h], 16)
                in_steps(sp, STEPS, step)

            @block.gpsimd
            def _(pool):
                in_steps(pool, STEPS, gather_step(pool, table3, got114, STEPS))

            @block.vector
            def _(dve):
                dve.memset(accN, 0.0).then_inc(s_zero11, 1)
                dve.memset(accE[0:FE, :], 0.0).then_inc(s_zero11, 1)
                dve.wait_ge(s_zero11, 2)

                def add(i, h):
                    sums_up(dve, 0, h, i, lambda b: [accN[:, bass.ds(b * P, P)], accE[0:FE, bass.ds(b * P, P)]],
                            lambda h: [ps[h][:, 0:P], ps[h][0:FE, P:2 * P]], 3 * STEPS)

                hot_then_add(dve, index_and_hot(dve, hot114, STEPS), add)

            @block.tensor
            def _(pe):
                def step(i):
                    for h in range(Q):
                        pe.wait_ge(s_hot[h], i + (1 + 3 * STEPS))
                        pe.wait_ge(s_feat11[h], i * 16 + 16)
                        at_least(pe, s_acc[h], i + 3 * STEPS)
                        for u in range(U):
                            pe.matmul(ps[h][0:FE, P:2 * P], feat4[:, h, u, :], hot114[:, h, u, :],
                                      start=(u == 0), stop=(u == U - 1))
                        pe.wait_ge(s_got[h], i * (16 * U) + 16 * U * (1 + 2 * STEPS))
                        for u in range(U):
                            last = pe.matmul(ps[h][:, 0:P], got114[:, h, u, :], hot114[:, h, u, :],
                                             start=(u == 0), stop=(u == U - 1))
                        last.then_inc(s_mm[h], 1)
                in_steps(pe, STEPS, step)

        h12 = cut(2 * NB * P, NB * D)[0]
        sq12 = cut(3 * NB * P, NB * D)[0]
        h123, sq123 = wide(h12), wide(sq12)
        n_st = cut(4 * NB * P, P)[0]
        e_st = cut(4 * NB * P + P, P)[0]
        s_st12 = sem("s_st12")
        s_o12 = sem("s_o12")
        s_h12 = sem("s_h12")
        s_out = sem("s_out")
        s_x4 = sem("s_x4")
        with nc.Block() as block:
            @block.tensor
            def _(pe):
                def bucket(b):
                    at_least(pe, s_h12, b)
                    pe.wait_ge(s_st12, b * 2 + 2)
                    pe.matmul(ps[0][:, 0:D], n_st, w3s[:, :], start=True, stop=False)
                    pe.matmul(ps[0][:, 0:D], e_st[0:FE, :], w3ew[:, :],
                              start=False, stop=True).then_inc(s_o12, 1)
                in_steps(pe, NB, bucket)

            @block.vector
            def _(dve):
                chain.on(dve)
                link = chain.link
                def bucket(b):
                    dve.wait_ge(s_o12, b + 1)
                    dve.scalar_tensor_tensor(h12[:, bass.ds(b * D, D)], ps[0][:, 0:D], degn[:, bass.ds(b, 1)],
                                             b3b[:, :], ALU.mult, ALU.add).then_inc(s_h12, 1)
                in_steps(dve, NB, bucket)
                dve.wait_ge(s_h12, NB)
                link(dve.scalar_tensor_tensor(h12, h12, 0.0, X[:, :], ALU.max, ALU.add))
                layer_norm(dve, link, h123, sq123, chain.sqrt)
                dve.sem_inc(s_x4, 1)

            @block.scalar
            def _(act):
                def bucket(b):
                    at_least(act, s_o12, b)
                    act.copy(n_st, accN[:, bass.ds(b * P, P)]).then_inc(s_st12, 1)
                    act.copy(e_st[0:FE, :], accE[0:FE, bass.ds(b * P, P)]).then_inc(s_st12, 1)
                in_steps(act, NB, bucket)
                for k, f, i, o, kw in chain.jobs:
                    act.wait_ge(chain.ask, k)
                    act.activation(o, i, f, **kw).then_inc(chain.did, 1)

            @block.sync
            def _(sp):
                sp.wait_ge(s_x4, 1)
                sp.dma_start(out[0:NFULL * P, :].rearrange("(b p) f -> p b f", p=P), X3[:, 0:NFULL, :]).then_inc(s_out, 16)
                sp.dma_start(out[NFULL * P:N, :], X3[0:NREST, NFULL, :]).then_inc(s_out, 16)
                sp.wait_ge(s_out, 32)


_INS = ["x", "src", "dst", "edge_attr_64", "edge_type_3", "edge_weight", "node_type_3", "L0_gnn_W_e", "L0_gnn_b_e",
        "L0_gnn_W_n", "L0_gnn_b_n", "L1_gnn_weight", "L1_gnn_bias", "L3_gnn_weight", "L3_gnn_weight_edge", "L3_gnn_bias"]


def kernel(**inputs):
    import numpy as np
    import concourse.bacc as bacc
    from concourse.bass_utils import run_bass_kernel_spmd as run

    nc = bacc.Bacc("TRN2", target_bir_lowering=False, num_devices=1)
    arrays, args = {}, []
    for name in _INS:
        a = np.ascontiguousarray(inputs[name])
        arrays[f"in_{name}"] = a
        args.append(nc.dram_tensor(f"in_{name}", a.shape, mybir.dt.from_np(a.dtype), kind="ExternalInput").ap())
    out = nc.dram_tensor("out", (N, D), F32, kind="ExternalOutput").ap()
    build(nc, *args, out)
    return run(nc, [arrays], core_ids=[0]).results[0]["out"]
```

```python
from contextlib import ExitStack

import concourse.bass as bass
from concourse import mybir

F32 = mybir.dt.float32
I32 = mybir.dt.int32
I16 = mybir.dt.int16
BF16 = mybir.dt.bfloat16
ALU = mybir.AluOpType
ACT = mybir.ActivationFunctionType
AX = mybir.AxisListType

P = 128
N, E, D, T, FE = 6250, 206250, 128, 3, 64
NB = -(-N // P)
NFULL = N // P
NREST = N - NFULL * P
NP = NB * P
NO_NODE = NP

EC = E // P
MAIN = EC * P
EREST = E - MAIN
C = EC + 1

U, Q = 2, 8
GE = U * P
NG = -(-((E + NB * (GE - 1)) // GE) // Q) * Q
TP = NG * U
STEPS = NG // Q
MU, MQ = 4, 8
MGE = MU * P
MNG = -(-((E + NB * (MGE - 1)) // MGE) // MQ) * MQ
MTP = MNG * MU
MSTEPS = MNG // MQ
EPAD = E + GE
OUTSIDE = 1 << 22

SU, SQ = 13, 4
SSTEPS = C // (SU * SQ)
assert SSTEPS * SU * SQ == C

KEY, DST, WGT, SRCF, SLOC, POS2, IDX0 = range(7)
NF = 7
KT = 8192
assert KT > NP + P
R_DLOC, R_WGT, R_SRCF, R_SLOC, R_POS2 = range(5)
NR = 5
MONE, MLOC = D, D + 1
MW = D + 2
EPS = 1e-5
MIN_NORM = 1e-15
MAX_NORM = 1.0 - 0.004


def at_least(eng, sem, value):
    if not isinstance(value, int) or value > 0:
        eng.wait_ge(sem, value)


def in_steps(eng, n, body):
    body(0)
    with eng.Fori(1, n, 1) as i:
        body(i)


BB = 4
SHARE = 18


def in_batches(eng, body):
    in_steps(eng, NB // BB, lambda i: body(i, BB))
    if NB % BB:
        body(NB // BB, NB % BB)


def in_groups(eng, step):
    step(0)
    with eng.Fori(Q, NG - Q + 1, Q) as g0:
        step(g0)


def build(nc, x, src, dst, attr, etype, weight, ntype, w_e, b_e, w_n, b_n, w1, b1, w3, w3e, b3, out):
    ctx = ExitStack()
    with ctx:
        ctx.enter_context(nc.allow_non_contiguous_dma(reason="node types, leftover edges"))

        def sb(name, cols, dt=F32, rows=P):
            return ctx.enter_context(nc.sbuf_tensor(name, [rows, cols], dt))

        def sem(name):
            return ctx.enter_context(nc.semaphore(name))

        def sems(name, n):
            return [sem(f"{name}{i}") for i in range(n)]

        edge_fields = nc.dram_tensor("edge_fields", (EPAD, NF), F32, kind="Internal").ap()
        edge_feats = nc.dram_tensor("edge_feats", (EPAD, FE), F32, kind="Internal").ap()
        sorted_msgs = nc.dram_tensor("sorted_msgs", (P, MTP * MW), F32, kind="Internal").ap()
        typed_msgs = nc.dram_tensor("typed_msgs", (NP, T * D), F32, kind="Internal").ap()
        table2 = nc.dram_tensor("table2", (NP, D), F32, kind="Internal").ap()
        table3 = nc.dram_tensor("table3", (NP, D), F32, kind="Internal").ap()

        X = sb("X", NB * D)
        X3 = X[:, :].rearrange("p (b f) -> p b f", b=NB)
        ident = sb("ident", P)
        before = sb("before", P)
        ones = sb("ones", P)
        iota = sb("iota", T * P)
        weT = sb("weT", T * D)
        wnT = sb("wnT", (T + 1) * T * D)
        w1s = sb("w1s", D)
        w3s = sb("w3s", D)
        w3es = sb("w3es", D, rows=FE)
        w3eT = sb("w3eT", FE)
        w3ew = sb("w3ew", D, rows=FE)
        be_row = sb("be_row", T * D, rows=1)
        bnb = sb("bnb", T * D)
        b1b = sb("b1b", D)
        b3b = sb("b3b", D)
        ntype_i = sb("ntype_i", NB, I32)
        ntype_f = sb("ntype_f", NB)
        nmask = sb("nmask", T * NB)
        bucket_of = [sb(f"bucket_of{i}", n, I32, rows=1) for i, n in enumerate((NG, MNG))]
        start_of = sb("start_of", NG, I32, rows=1)
        as_given = sb("as_given", NG, I32, rows=1)
        given_from = sb("given_from", NG, I32, rows=1)
        node0 = sb("node0", NG)
        is_sorted = sb("is_sorted", 2, I32, rows=1)
        R = sb("R", TP * NR)
        R3 = R[:, :].rearrange("p (t r) -> p t r", r=NR)
        small = sb("small", 20 * NB)
        big_words = (nc.sbuf_bytes_remaining // 4) // 16 * 16 - 64
        big = sb("big", big_words)

        def cut(at, n):
            assert at + n <= big_words, (at, n, big_words)
            return big[:, at:at + n], at + n

        def cut4(at, width):
            c, at = cut(at, Q * U * width)
            return c.rearrange("p (q u r) -> p q u r", q=Q, u=U), at

        ps = [ctx.enter_context(nc.psum_tensor(f"ps{i}", [P, 512], F32)) for i in range(8)]

        Fc, at = cut(0, C * NF)
        F3 = Fc.rearrange("p (c r) -> p c r", r=NF)
        cols = []
        for _ in range(4):
            c, at = cut(at, C)
            cols.append(c)
        dst_i, src_i, typ_i = (c.bitcast(I32) for c in cols[:3])
        w_c = cols[3]
        next_c, at = cut(at, C)
        next_i = next_c.bitcast(I32)
        buckets = []
        for _ in range(2):
            c, at = cut(at, C // 2)
            buckets.append(c.bitcast(BF16))
        dbkt, sbkt = buckets
        masks = []
        for _ in range(2):
            c, at = cut(at, C // 2)
            masks.append(c.bitcast(I16))
        scans = []
        for _ in range(2):
            c, at = cut(at, C)
            scans.append(c)
        pos = next_c
        tmp = scans[0]
        sfeat, _ = cut(C * NF, SQ * SU * FE)
        sfeat4 = sfeat.rearrange("p (q u r) -> p q u r", q=SQ, u=SU)
        sfield, _ = cut(C * NF + SQ * SU * FE, SQ * SU * NF)
        sfield4 = sfield.rearrange("p (q u r) -> p q u r", q=SQ, u=SU)
        sidx, _ = cut(C * NF + SQ * SU * (FE + NF), SQ * SU)
        sidx3 = sidx.bitcast(I32).rearrange("p (q u) -> p q u", q=SQ)
        assert SQ * SU * (FE + NF + 1) <= 4 * C
        r_at = [0]

        def room(n):
            r_at[0] += n
            assert r_at[0] <= TP * NR
            return R[:, r_at[0] - n:r_at[0]]

        iota_g = room(NG)
        past = room(NG)
        wnat = room((T + 1) * T * D).rearrange("p (t i) -> p t i", t=T)
        wenat = room(T * D).rearrange("p (t i) -> p t i", t=T)
        xsts, xTs, mrows = ([room(D) for _ in range(2)], [room(D) for _ in range(2)], [room(T * D) for _ in range(2)])
        fillf = room(U * NF)
        fille = room(U * FE)
        e0f = room(NG)
        e0f_ok = room(NG)
        Tb = [small[:, i * NB:(i + 1) * NB] for i in range(2)]
        groups_i = small[:, 2 * NB:3 * NB].bitcast(I32)
        groups_f = small[:, 3 * NB:4 * NB]
        ends = [small[:, 4 * NB:5 * NB], small[:, 5 * NB:6 * NB]]
        starts = small[:, 6 * NB:7 * NB]
        bases = [small[:, 7 * NB:8 * NB], small[:, 8 * NB:9 * NB]]
        ahead = small[:, 9 * NB:10 * NB]
        steps_ = small[:, 10 * NB:11 * NB]
        endcol = small[:, 11 * NB:11 * NB + 4]
        viol = small[:, 12 * NB:12 * NB + 4]
        sorted_f = small[0:1, 13 * NB:13 * NB + 1]

        parts_of = (((0, NG // 2), (NG // 2, NG)), ((0, MNG),))
        assert max(NG - NG // 2, MNG) <= 512

        s_edges = sem("s_edges")
        s_rest = sem("s_rest")
        s_x = sem("s_x")
        s_w = sem("s_w")
        s_cst = sem("s_cst")
        s_filler = sem("s_filler")
        s_fillf = sem("s_fillf")
        s_v1 = sem("s_v1")
        s_tot = sem("s_tot")
        s_pref = sem("s_pref")
        s_end = sem("s_end")
        s_endT = sem("s_endT")
        s_past = sem("s_past")
        s_pastp = sem("s_pastp")
        s_viol = sem("s_viol")
        s_violp = sem("s_violp")
        s_wT = sem("s_wT")
        s_wTe = sem("s_wTe")
        s_xs = sem("s_xs")
        s_xT = sem("s_xT")
        s_xTe = sem("s_xTe")
        s_m = sem("s_m")
        s_me = sem("s_me")
        s_mst = sems("s_mst", 2)
        s_pads = sem("s_pads")

        with nc.Block() as block:
            @block.sync
            def _(sp):
                for col, a in ((src_i, src), (dst_i, dst), (typ_i, etype), (w_c, weight)):
                    sp.dma_start(col[:, 0:EC], a[0:MAIN].rearrange("(p c) -> p c", p=P)).then_inc(s_edges, 16)
                sp.dma_start(next_i[:, 0:EC], dst[1:MAIN + 1].rearrange("(p c) -> p c", p=P)).then_inc(s_edges, 16)
                sp.wait_ge(s_filler, 7)
                for col, a in ((dst_i, dst), (src_i, src), (typ_i, etype), (w_c, weight)):
                    sp.dma_start(col[0:EREST, EC:C], a[MAIN:E].rearrange("(p c) -> p c", c=1)).then_inc(s_rest, 16)
                sp.dma_start(next_i[0:EREST - 1, EC:C], dst[MAIN + 1:E].rearrange("(p c) -> p c", c=1)).then_inc(s_rest, 16)
                sp.dma_start(ntype_i[:, 0:NFULL], ntype[0:NFULL * P].rearrange("(b p) -> p b", p=P)).then_inc(s_rest, 16)
                sp.dma_start(ntype_i[0:NREST, NFULL:NB], ntype[NFULL * P:N].rearrange("(p c) -> p c", c=1)).then_inc(s_rest, 16)
                sp.wait_ge(s_fillf, 6)
                sp.dma_start(edge_fields[E:EPAD, :].rearrange("(p u) r -> p (u r)", u=U), fillf).then_inc(s_pads, 16)
                sp.dma_start(edge_feats[E:EPAD, :].rearrange("(p u) r -> p (u r)", u=U), fille).then_inc(s_pads, 16)
                sp.wait_ge(s_pads, 32)

                def pair(i, n=2):
                    for k in range(n):
                        sp.wait_ge(s_me, i * 2 + (k + 1))
                        sp.dma_start(typed_msgs[bass.ds(i * (2 * P) + k * P, P), :], mrows[k]).then_inc(s_mst[k], 16)
                in_steps(sp, NB // 2, pair)
                pair(NB // 2, 1)
                sp.wait_ge(s_mst[0], 16 * (NB // 2 + 1))
                sp.wait_ge(s_mst[1], 16 * (NB // 2))

            @block.gpsimd
            def _(pool):
                pool.memset(ident[:, :], 0.0).then_inc(s_cst, 1)
                pool.memset(before[:, :], 1.0).then_inc(s_cst, 1)
                pool.memset(ones[:, :], 1.0).then_inc(s_cst, 1)
                pool.iota(iota[:, :], pattern=[[KT, T], [1, P]], base=0, channel_multiplier=0,
                          allow_small_or_imprecise_dtypes=True).then_inc(s_cst, 1)
                pool.iota(iota_g, pattern=[[1, NG]], base=0, channel_multiplier=0,
                          allow_small_or_imprecise_dtypes=True).then_inc(s_cst, 1)
                pool.wait_ge(s_cst, 5)
                pool.affine_select(out=ident[:, :], in_=ident[:, :], compare_op=ALU.not_equal, fill=1.0,
                                   base=0, pattern=[[-1, P]], channel_multiplier=1).then_inc(s_cst, 1)
                pool.affine_select(out=before[:, :], in_=before[:, :], compare_op=ALU.is_gt, fill=0.0,
                                   base=0, pattern=[[1, P]], channel_multiplier=-1).then_inc(s_cst, 1)

            @block.scalar
            def _(act):
                act.dma_start(wenat, w_e.rearrange("t o i -> o t i")).then_inc(s_w, 16)
                act.dma_start(wnat, w_n.rearrange("t o i -> o t i")).then_inc(s_w, 16)
                for t, a in ((w1s, w1), (w3s, w3), (w3es, w3e)):
                    act.dma_start(t[:, :], a).then_inc(s_w, 16)
                act.dma_start(be_row[:, :], b_e.rearrange("t (o f) -> o (t f)", o=1)).then_inc(s_w, 16)
                act.dma_start(bnb[:, :], b_n.rearrange("t (o f) -> o (t f)", o=1).to_broadcast([P, T * D])).then_inc(s_w, 16)
                act.dma_start(b1b[:, :], b1.rearrange("(o f) -> o f", o=1).to_broadcast([P, D])).then_inc(s_w, 16)
                act.dma_start(b3b[:, :], b3.rearrange("(o f) -> o f", o=1).to_broadcast([P, D])).then_inc(s_w, 16)
                act.dma_start(X3[:, 0:NFULL, :], x[0:NFULL * P, :].rearrange("(b p) f -> p b f", p=P)).then_inc(s_x, 16)
                act.wait_ge(s_filler, 7)
                act.dma_start(X3[0:NREST, NFULL, :], x[NFULL * P:N, :]).then_inc(s_x, 16)
                act.wait_ge(s_wT, T)
                act.copy(weT[:, :], ps[0][:, 0:T * D]).then_inc(s_wTe, 1)
                for c in range(T + 1):
                    act.wait_ge(s_wT, T + T * (c + 1))
                    act.copy(wnT[:, c * T * D:(c + 1) * T * D], ps[1 + c][:, 0:T * D]).then_inc(s_wTe, 1)
                act.wait_ge(s_wT, T + T * (T + 1) + 1)
                act.copy(w3eT[:, :], ps[5][:, 0:FE]).then_inc(s_wTe, 1)
                act.wait_ge(s_wT, T + T * (T + 1) + 2)
                act.copy(w3ew[:, :], ps[6][0:FE, 0:D]).then_inc(s_wTe, 1)
                act.wait_ge(s_x, 32)

                def pair(i, n=2):
                    for k in range(n):
                        at_least(act, s_xT, i * 2 + (k - 1))
                        act.copy(xsts[k], X[:, bass.ds(i * (2 * D) + k * D, D)]).then_inc(s_xs, 1)
                    for k in range(n):
                        act.wait_ge(s_xT, i * 2 + (k + 1))
                        act.copy(xTs[k], ps[k][:, 0:P]).then_inc(s_xTe, 1)
                    for k in range(n):
                        act.wait_ge(s_m, i * 2 + (k + 1))
                        at_least(act, s_mst[k], i * 16)
                        act.activation(mrows[k], ps[6 + k][:, 0:T * D], ACT.Relu).then_inc(s_me, 1)
                in_steps(act, NB // 2, pair)
                pair(NB // 2, 1)

            @block.tensor
            def _(pe):
                pe.wait_ge(s_w, 16 * 9)
                pe.wait_ge(s_cst, 7)
                for t in range(T):
                    pe.transpose(ps[0][:, t * D:(t + 1) * D], wenat[:, t, :], ident[:, :]).then_inc(s_wT, 1)
                for c in range(T + 1):
                    for t in range(T):
                        pe.transpose(ps[1 + c][:, t * D:(t + 1) * D], wnat[:, t, c * D:(c + 1) * D],
                                     ident[:, :]).then_inc(s_wT, 1)
                pe.transpose(ps[5][:, 0:FE], w3es[:, :], ident[0:FE, 0:FE]).then_inc(s_wT, 1)
                pe.wait_ge(s_wTe, T + 3)
                pe.matmul(ps[6][0:FE, 0:D], w3eT[:, :], w3s[:, :], start=True, stop=True).then_inc(s_wT, 1)
                pe.wait_ge(s_wTe, T + 4)

                for k in range(2):
                    pe.wait_ge(s_tot, k + 1)
                    pe.matmul(ps[2 + k][:, 0:NB], before[:, :], Tb[k], start=True, stop=True).then_inc(s_pref, 1)
                    pe.matmul(ps[2 + k][:, 64:64 + NB], ones[:, :], Tb[k], start=True, stop=True).then_inc(s_pref, 1)
                    pe.wait_ge(s_end, k + 1)
                    pe.transpose(ps[4][0:NB, 0:P], ends[k], ident[:, :]).then_inc(s_endT, 1)
                    pe.transpose(ps[4][0:NB, P:2 * P], steps_, ident[:, :]).then_inc(s_endT, 1)
                    pe.wait_ge(s_past, k + 1)
                    for j, (g0, g1) in enumerate(parts_of[k]):
                        half = past[0:NB, g0:g1]
                        pe.matmul(ps[4 + j][:, 0:g1 - g0], ones[0:NB, :], half, start=True, stop=True).then_inc(s_pastp, 1)
                        if not k:
                            pe.matmul(ps[2 + j][0:1, 0:g1 - g0], endcol[0:NB, 2:3], half, start=True, stop=True).then_inc(s_pastp, 1)
                pe.wait_ge(s_viol, 1)
                pe.matmul(ps[3][0:1, 0:1], viol[:, 0:1], ones[:, 0:1], start=True, stop=True).then_inc(s_violp, 1)

                def pair(i, n=2):
                    for k in range(n):
                        pe.wait_ge(s_xs, i * 2 + (k + 1))
                        pe.transpose(ps[k][:, 0:P], xsts[k], ident[:, :]).then_inc(s_xT, 1)
                    for k in range(n):
                        pe.wait_ge(s_xTe, i * 2 + (k + 1))
                        at_least(pe, s_me, i * 2)
                        pe.matmul(ps[6 + k][:, 0:T * D], xTs[k], weT[:, :], start=True, stop=False)
                        pe.matmul(ps[6 + k][:, 0:T * D], ones[0:1, :], be_row[:, :], start=False, stop=True).then_inc(s_m, 1)
                in_steps(pe, NB // 2, pair)
                pair(NB // 2, 1)

            def count_on(dve, start=0):
                n = [start]

                def do(ins):
                    n[0] += 1
                    ins.then_inc(s_v1, 1)
                    return n[0]

                def link(ins):
                    dve.wait_ge(s_v1, do(ins))
                return n, do, link

            def place(dve, do, link, bkt, base):
                link(dve.memset(pos, float(OUTSIDE)))
                masked, scanned, picked = {}, {}, {}
                for b in range(NB + 2):
                    if b < NB:
                        if b >= 2:
                            dve.wait_ge(s_v1, picked[b - 2])
                        masked[b] = do(dve.tensor_scalar(masks[b % 2], bkt, float(b), None, ALU.is_equal))
                    if 1 <= b <= NB:
                        dve.wait_ge(s_v1, masked[b - 1])
                        scanned[b - 1] = do(dve.tensor_tensor_scan(scans[(b - 1) % 2], masks[(b - 1) % 2], masks[(b - 1) % 2],
                                                                   base[:, b - 1:b], ALU.add, ALU.bypass))
                        dve.wait_ge(s_v1, scanned[b - 1])
                        picked[b - 1] = do(dve.copy_predicated(pos, masks[(b - 1) % 2], scans[(b - 1) % 2]))
                dve.wait_ge(s_v1, picked[NB - 1])

            steps_done = [0]

            @block.vector
            def _(dve):
                n, do, link = count_on(dve)
                dve.memset(dst_i[:, EC:C], NO_NODE).then_inc(s_filler, 1)
                dve.memset(src_i[:, EC:C], NO_NODE).then_inc(s_filler, 1)
                dve.memset(typ_i[:, EC:C], 0).then_inc(s_filler, 1)
                dve.memset(w_c[:, EC:C], 0.0).then_inc(s_filler, 1)
                dve.memset(next_i[:, EC:C], NO_NODE).then_inc(s_filler, 1)
                dve.memset(X3[:, NFULL, :], 0.0).then_inc(s_filler, 1)
                dve.memset(ntype_i[:, NFULL:NB], 0).then_inc(s_filler, 1)
                f3 = fillf.rearrange("p (u r) -> p u r", u=U)
                dve.memset(f3[:, :, KEY:DST + 1], float(NO_NODE)).then_inc(s_fillf, 1)
                dve.memset(f3[:, :, WGT:SRCF + 1], 0.0).then_inc(s_fillf, 1)
                dve.memset(f3[:, :, SLOC:SLOC + 1], -1.0).then_inc(s_fillf, 1)
                dve.memset(f3[:, :, POS2:POS2 + 1], float(OUTSIDE)).then_inc(s_fillf, 1)
                dve.memset(f3[:, :, IDX0:IDX0 + 1].bitcast(I32), 0).then_inc(s_fillf, 1)
                dve.memset(fille, 0.0).then_inc(s_fillf, 1)

                dve.wait_ge(s_edges, 16 * 5)
                dve.wait_ge(s_rest, 16 * 7)
                tmp_i = tmp.bitcast(I32)
                do(dve.tensor_copy(F3[:, :, DST], dst_i))
                do(dve.tensor_copy(F3[:, :, SRCF], src_i))
                do(dve.tensor_copy(F3[:, :, WGT], w_c))
                link(dve.tensor_scalar(tmp_i, dst_i, 7, None, ALU.logical_shift_right))
                link(dve.tensor_copy(dbkt, tmp_i))
                link(dve.tensor_scalar(tmp_i, src_i, 7, None, ALU.logical_shift_right))
                link(dve.tensor_copy(sbkt, tmp_i))
                link(dve.tensor_copy(tmp, typ_i))
                do(dve.scalar_tensor_tensor(F3[:, :, SLOC], sbkt, -float(P), F3[:, :, SRCF], ALU.mult, ALU.add))
                do(dve.scalar_tensor_tensor(F3[:, :, KEY], tmp, float(KT), F3[:, :, DST], ALU.mult, ALU.add))
                do(dve.scalar_tensor_tensor(F3[:, :, IDX0].bitcast(I32), F3[:, :, SRCF], float(T), tmp, ALU.mult, ALU.add))
                link(dve.tensor_copy(ntype_f[:, :], ntype_i[:, :]))
                for t in range(T):
                    do(dve.tensor_scalar(nmask[:, t * NB:(t + 1) * NB], ntype_f[:, :], float(t), None, ALU.is_equal))
                link(dve.tensor_tensor(scans[1], dst_i, next_i, ALU.is_gt))
                link(dve.tensor_reduce(out=viol[:, 0:1], in_=scans[1], axis=AX.X, op=ALU.add))
                dve.sem_inc(s_viol, 1)

                for k, bkt in enumerate((dbkt, sbkt)):
                    tot, end, base = Tb[k], ends[k], bases[k]
                    size = (GE, MGE)[k]
                    last = [0, 0]
                    for b in range(NB):
                        at_least(dve, s_v1, last[b % 2])
                        last[b % 2] = do(dve.tensor_scalar(masks[b % 2], bkt, float(b), 0.0, ALU.is_equal, ALU.add,
                                                           accum_out=tot[:, b:b + 1]))
                    dve.wait_ge(s_v1, n[0])
                    dve.sem_inc(s_tot, 1)
                    dve.wait_ge(s_pref, 2 * k + 2)
                    total = ps[2 + k][:, 64:64 + NB]
                    link(dve.tensor_scalar(groups_f, total, float(size - 1), None, ALU.add))
                    link(dve.tensor_copy(groups_i, groups_f))
                    link(dve.tensor_scalar(groups_i, groups_i, size.bit_length() - 1, None, ALU.logical_shift_right))
                    link(dve.tensor_copy(groups_f, groups_i))
                    link(dve.tensor_tensor_scan(end, groups_f, groups_f, 0.0, ALU.add, ALU.bypass))
                    link(dve.tensor_tensor(starts, end, groups_f, ALU.subtract))
                    if k:
                        link(dve.scalar_tensor_tensor(base, starts, float(size), ps[2 + k][:, 0:NB], ALU.mult, ALU.add))
                    else:
                        link(dve.tensor_copy(viol[:, 2:3], total[:, 0:1]))
                        link(dve.tensor_copy(groups_f, total))
                        link(dve.tensor_tensor_scan(base, groups_f, groups_f, 0.0, ALU.add, ALU.bypass))
                        link(dve.tensor_tensor(base, base, groups_f, ALU.subtract))
                        link(dve.scalar_tensor_tensor(ahead, starts, -float(GE), base, ALU.mult, ALU.add))
                        link(dve.memset(steps_[:, NB - 1:NB], 0.0))
                        link(dve.tensor_tensor(steps_[:, 0:NB - 1], ahead[:, 1:NB], ahead[:, 0:NB - 1], ALU.subtract))
                        link(dve.tensor_tensor(base, base, ps[2 + k][:, 0:NB], ALU.add))
                    dve.sem_inc(s_end, 1)
                    dve.wait_ge(s_endT, 2 * k + 2)
                    do(dve.tensor_copy(endcol[0:NB, k:k + 1], ps[4][0:NB, 0:1]))
                    link(dve.tensor_copy(endcol[0:NB, 2:3], ps[4][0:NB, P:P + 1]))
                    link(dve.tensor_scalar(past[0:NB, :], iota_g[0:NB, :], endcol[0:NB, k:k + 1], None, ALU.is_ge))
                    dve.sem_inc(s_past, 1)
                    dve.wait_ge(s_pastp, 4 + k)
                    for j, (g0, g1) in enumerate(parts_of[k]):
                        part, w = slice(g0, g1), g1 - g0
                        do(dve.tensor_scalar(bucket_of[k][:, part], ps[4 + j][0:1, 0:w], float(NB - 1), None, ALU.min))
                        if not k:
                            do(dve.tensor_scalar(node0[:, part], ps[4 + j][:, 0:w], float(NB - 1), float(P), ALU.min, ALU.mult))
                            link(dve.scalar_tensor_tensor(e0f[0:1, part], iota_g[0:1, part], float(GE), ps[2 + j][0:1, 0:w],
                                                          ALU.mult, ALU.add))
                            link(dve.tensor_scalar(start_of[:, part], e0f[0:1, part], float(E), None, ALU.min))
                    dve.wait_ge(s_v1, n[0])
                place(dve, do, link, sbkt, bases[1])
                t_i, u_i = tmp.bitcast(I32), scans[1].bitcast(I32)
                link(dve.tensor_scalar(t_i, pos, -1.0, None, ALU.add))
                link(dve.tensor_scalar(u_i, t_i, P - 1, None, ALU.bitwise_and))
                link(dve.tensor_scalar(t_i, t_i, 7, None, ALU.logical_shift_right))
                link(dve.tensor_copy(pos, u_i))
                link(dve.tensor_copy(scans[1], t_i))
                link(dve.scalar_tensor_tensor(F3[:, :, POS2], pos, float(MTP), scans[1], ALU.mult, ALU.add))
                dve.wait_ge(s_violp, 1)
                link(dve.tensor_scalar(sorted_f[:, 0:1], ps[3][0:1, 0:1], 0.0, None, ALU.is_equal))
                do(dve.tensor_copy(is_sorted[:, 0:1], sorted_f[:, 0:1]))
                ok_f = e0f_ok[0:1, :]
                link(dve.tensor_scalar(ok_f, e0f[0:1, :], float(E - GE), None, ALU.is_le))
                link(dve.tensor_scalar(ok_f, ok_f, sorted_f[:, 0:1], None, ALU.mult))
                do(dve.tensor_copy(as_given[:, :], ok_f))
                link(dve.tensor_scalar(given_from[:, :], e0f[0:1, :], float(E - GE), None, ALU.min))
                steps_done[0] = n[0]

        def sm(i):
            return small[:, i * NB:(i + 1) * NB]

        def along(v):
            return v.unsqueeze(2).to_broadcast([P, NB, D])

        def wide(v):
            return v.rearrange("p (b f) -> p b f", b=NB)

        def sum_of_squares(dve, link, h3, sq3, to):
            asked = chain.squares(h3, sq3, to)
            link(dve.tensor_tensor(sq3[:, SHARE:, :], h3[:, SHARE:, :], h3[:, SHARE:, :], ALU.mult))
            link(dve.tensor_reduce(out=to[:, SHARE:], in_=sq3[:, SHARE:, :], axis=AX.X, op=ALU.add))
            dve.wait_ge(chain.did, asked)

        def layer_norm(dve, link, h3, sq3, ask_sqrt, before_x=lambda: None, summed=False):
            mean, var = sm(0), sm(1)
            if not summed:
                link(dve.tensor_reduce(out=mean, in_=h3, axis=AX.X, op=ALU.add))
            link(dve.tensor_scalar(mean, mean, 1.0 / D, None, ALU.mult))
            link(dve.tensor_tensor(h3, h3, along(mean), ALU.subtract))
            sum_of_squares(dve, link, h3, sq3, var)
            link(dve.tensor_scalar(sm(2), var, 1.0 / D, EPS, ALU.mult, ALU.add))
            ask_sqrt(sm(2), sm(2))
            link(dve.reciprocal(sm(2), sm(2)))
            before_x()
            link(dve.tensor_tensor(X3, h3, along(sm(2)), ALU.mult))

        class Chain:

            def __init__(self):
                self.v, self.ask, self.did = sem("s_step"), sem("s_ask"), sem("s_did")
                self.n = self.k = 0
                self.jobs = []

            def on(self, dve):
                self.dve = dve
                self.jobs = []

            def link(self, ins):
                self.n += 1
                ins.then_inc(self.v, 1)
                self.dve.wait_ge(self.v, self.n)

            def func(self, f, i, o):
                self.k += 1
                self.jobs.append((self.k, f, i, o, None))
                self.dve.sem_inc(self.ask, 1)
                self.dve.wait_ge(self.did, self.k)

            def sqrt(self, i, o):
                self.func(ACT.Sqrt, i, o)

            def squares(self, h3, sq3, to):
                self.k += 1
                self.jobs.append((self.k, None, h3, sq3, to))
                self.dve.sem_inc(self.ask, 1)
                return self.k

            def answer(self, act, first=0, last=None):
                for k, f, i, o, to in self.jobs[first:last]:
                    act.wait_ge(self.ask, k)
                    if f is not None:
                        act.activation(o, i, f).then_inc(self.did, 1)
                    else:
                        for b in range(SHARE):
                            made = act.activation(o[:, b, :], i[:, b, :], ACT.Square, accum_out=to[:, b:b + 1])
                        made.then_inc(self.did, 1)

        s_turn = sem("s_turn")
        s_placed = sem("s_placed")
        s_fields = sem("s_fields")
        s_sfeat = sems("s_sfeat", SQ)
        s_sextra = sem("s_sextra")
        s_sfield = sems("s_sfield", SQ)
        s_srow = sems("s_srow", SQ)
        chain = Chain()
        bias_sq = R[:, 0:D]
        c1 = small[:, 11 * NB:11 * NB + 8]
        y2 = c1[:, 0:1]
        attr_main = attr[0:MAIN, :].rearrange("(p c) f -> p (c f)", p=P)

        with nc.Block() as block:
            @block.sync
            def _(sp):
                given = sp.value_load(is_sorted[0:1, 0:1], min_val=0, max_val=1)
                with sp.If(given == 1):
                    sp.dma_start(edge_fields[0:MAIN, :].rearrange("(p c) r -> p (c r)", p=P),
                                 Fc[:, 0:EC * NF]).then_inc(s_fields, 16)
                    sp.dma_start(edge_fields[MAIN:E, :], F3[0:EREST, EC, :]).then_inc(s_fields, 16)
                    sp.wait_ge(s_fields, 32)
                with sp.If(given == 0):
                    def step(i, last=False):
                        for h in range(SQ):
                            at_least(sp, s_srow[h], i * (2 * 16 * SU))
                            n = SU - 1 if last and h == SQ - 1 else SU
                            sp.dma_start(sfeat4[:, h, 0:n, :],
                                         attr_main[:, bass.ds(i * (SQ * SU * FE) + h * (SU * FE), n * FE)]
                                         .rearrange("p (u f) -> p u f", u=n)).then_inc(s_sfeat[h], 16)
                    sp.wait_ge(s_placed, 1)
                    step(0)
                    with sp.Fori(1, SSTEPS - 1, 1) as i:
                        step(i)
                    step(SSTEPS - 1, last=True)
                    sp.dma_start(sfeat4[0:EREST, SQ - 1, SU - 1, :], attr[MAIN:E, :]).then_inc(s_sextra, 16)

            @block.vector
            def _(dve):
                chain.on(dve)
                link = chain.link
                link(dve.tensor_tensor(bias_sq, b1b[:, :], b1b[:, :], ALU.mult))
                link(dve.tensor_reduce(out=c1[:, 0:1], in_=bias_sq, axis=AX.X, op=ALU.add))
                chain.sqrt(c1[:, 0:1], c1[:, 1:2])
                link(dve.tensor_scalar(c1[:, 1:2], c1[:, 1:2], MIN_NORM, None, ALU.max))
                chain.func(ACT.Tanh, c1[:, 1:2], c1[:, 2:3])
                link(dve.reciprocal(c1[:, 3:4], c1[:, 1:2]))
                link(dve.tensor_tensor(c1[:, 2:3], c1[:, 2:3], c1[:, 3:4], ALU.mult))
                link(dve.tensor_scalar(b1b[:, :], b1b[:, :], c1[:, 2:3], None, ALU.mult))
                link(dve.tensor_tensor(bias_sq, b1b[:, :], b1b[:, :], ALU.mult))
                link(dve.tensor_reduce(out=c1[:, 0:1], in_=bias_sq, axis=AX.X, op=ALU.add))
                chain.sqrt(c1[:, 0:1], c1[:, 1:2])
                link(dve.tensor_scalar(c1[:, 1:2], c1[:, 1:2], MIN_NORM, None, ALU.max))
                link(dve.reciprocal(c1[:, 1:2], c1[:, 1:2]))
                link(dve.tensor_scalar(c1[:, 1:2], c1[:, 1:2], MAX_NORM, 1.0, ALU.mult, ALU.min))
                link(dve.tensor_scalar(b1b[:, :], b1b[:, :], c1[:, 1:2], None, ALU.mult))
                link(dve.tensor_tensor(bias_sq, b1b[:, :], b1b[:, :], ALU.mult))
                link(dve.tensor_reduce(out=c1[:, 0:1], in_=bias_sq, axis=AX.X, op=ALU.add))
                given = dve.value_load(is_sorted[0:1, 0:1], min_val=0, max_val=1)
                with dve.If(given == 0):
                    n, do, link = count_on(dve, steps_done[0])
                    place(dve, do, link, dbkt, bases[0])
                    link(dve.tensor_scalar(pos.bitcast(I32), pos, -1.0, None, ALU.add))
                    link(dve.memset(sfeat, 0.0))
                    dve.sem_inc(s_placed, 1)

                    def step(i):
                        for h in range(SQ):
                            at_least(dve, s_srow[h], i * (2 * 16 * SU))
                            dve.tensor_copy(sfield4[:, h, :, :], F3[:, bass.ds(i * (SQ * SU) + h * SU, SU), :]).then_inc(s_sfield[h], 1)
                            dve.tensor_copy(sidx3[:, h, :], pos.bitcast(I32)[:, bass.ds(i * (SQ * SU) + h * SU, SU)]).then_inc(s_sfield[h], 1)
                    in_steps(dve, SSTEPS, step)

            @block.scalar
            def _(act):
                chain.answer(act)

            @block.gpsimd
            def _(pool):
                given = pool.value_load(is_sorted[0:1, 0:1], min_val=0, max_val=1)
                with pool.If(given == 0):
                    beyond = pool.to_reg(E - 1)

                    def step(i, last=False):
                        for h in range(SQ):
                            pool.wait_ge(s_sfeat[h], i * 16 + 16)
                            pool.wait_ge(s_sfield[h], i * 2 + 2)
                            if last and h == SQ - 1:
                                pool.wait_ge(s_sextra, 16)
                            pool.sem_inc(s_turn, 1)
                            for u in range(SU):
                                for table, ring in ((edge_feats, sfeat4), (edge_fields, sfield4)):
                                    pool.indirect_dma_start(
                                        out=table, out_offset=bass.IndirectOffsetOnAxis(ap=sidx3[:, h, u:u + 1], axis=0),
                                        in_=ring[:, h, u, :], in_offset=None,
                                        bounds_check=beyond, oob_is_err=False).then_inc(s_srow[h], 16)
                    step(0)
                    with pool.Fori(1, SSTEPS - 1, 1) as i:
                        step(i)
                    step(SSTEPS - 1, last=True)
                    for h in range(SQ):
                        pool.wait_ge(s_srow[h], SSTEPS * 2 * 16 * SU)

        acc, at = cut(0, NB * T * P)
        fld4, at = cut4(at, NF)
        fld4i = fld4.bitcast(I32)
        rel, at = cut(at, Q * U)
        rel3 = rel.rearrange("p (q u) -> p q u", q=Q)
        got4, at = cut4(at, D)
        hot4, at = cut4(at, T * P)
        FILL2 = 4
        FILLS = Q * U // FILL2
        assert FILLS * FILL2 == Q * U and MTP % FILL2 == 0 and MTP >= TP
        fill2, at = cut(at, FILL2 * MW)

        s_hot = sem("s_hot")
        s_mm = sem("s_mm")
        s_acc = sem("s_acc")
        s_kept = sem("s_kept")
        s_rel = sem("s_rel")
        s_fld = sems("s_fld", Q)
        s_got = sems("s_got", Q)
        s_zero = sem("s_zero")
        s_fill2 = sem("s_fill2")
        s_fills2 = sem("s_fills2")
        s_feats = sem("s_feats")
        typed_rows = typed_msgs.rearrange("n (t f) -> (n t) f", t=T)

        def arrived(g0, per=16, base=0):
            return g0 * (per // Q) + (per + base * STEPS * per)

        def slot_free(eng, done, g, base=0):
            at_least(eng, done, g + (1 - Q + base))

        def registers(engine, table, first, n, most):
            _, values = nc.values_load_multi_w_load_instructions(table[0:1, bass.ds(first, n)], engines=(engine,),
                                                                 min_val=0, max_val=most)
            return values

        def buckets_at(engine, table, first, n):
            return registers(engine, table, first, n, NB - 1)

        LAG = Q // 2

        def two_steps(eng, engine, table, first, second):
            def step(g0):
                peeled = isinstance(g0, int)
                buckets = None
                if table is not None:
                    buckets = buckets_at(engine, table, 0 if peeled else g0 - LAG, LAG if peeled else Q)
                    if peeled:
                        buckets = [None] * LAG + list(buckets)
                for h in range(Q):
                    first(g0 + h, g0, h)
                    if h >= LAG or not peeled:
                        second(g0 + (h - LAG), (h - LAG) % Q, buckets[h] if buckets else None)
            in_groups(eng, step)
            buckets = buckets_at(engine, table, NG - LAG, LAG) if table is not None else [None] * LAG
            for h in range(LAG):
                second(NG - LAG + h, Q - LAG + h, buckets[h])

        def hot_then_add(dve, table, one_hot, parts, base):
            def add(g, h, b):
                dve.wait_ge(s_mm, g + (1 + base))
                at_least(dve, s_acc, g + base)
                last = None
                for a, part in parts(b, h):
                    last = dve.tensor_tensor(a, part, a, ALU.add)
                last.then_inc(s_acc, 1)
            two_steps(dve, mybir.EngineType.DVE, table, one_hot, add)

        with nc.Block() as block:
            @block.sync
            def _(sp):
                given = sp.value_load(is_sorted[0:1, 0:1], min_val=0, max_val=1)
                sp.dma_start(edge_feats[E - GE:E, :], attr[E - GE:E, :], cond=given).then_inc(s_feats, 16)
                sp.wait_ge(s_fill2, 2)

                def step(g0):
                    first = registers(mybir.EngineType.SP, start_of, g0, Q, E)
                    for h in range(Q):
                        slot_free(sp, s_mm, g0 + h)
                        slot_free(sp, s_kept, g0 + h)
                        sp.dma_start(fld4[:, h, :, :], edge_fields[bass.ds(first[h], GE), :]
                                     .rearrange("(p u) r -> p u r", u=U)).then_inc(s_fld[h], 16)
                    for k in range(FILLS):
                        sp.dma_start(sorted_msgs[:, bass.ds(g0 * (U * MW) + k * FILL2 * MW, FILL2 * MW)],
                                     fill2).then_inc(s_fills2, 16)
                in_groups(sp, step)
                rest = range(TP, MTP, FILL2)
                for tile in rest:
                    sp.dma_start(sorted_msgs[:, tile * MW:(tile + FILL2) * MW], fill2).then_inc(s_fills2, 16)
                sp.wait_ge(s_fills2, 16 * (MTP // FILL2))

            @block.gpsimd
            def _(pool):
                def step(g0):
                    for h in range(Q):
                        pool.wait_ge(s_fld[h], arrived(g0))
                        slot_free(pool, s_mm, g0 + h)
                        pool.sem_inc(s_turn, 1)
                        for u in range(U):
                            pool.indirect_dma_start(
                                out=got4[:, h, u, :], out_offset=None, in_=typed_rows,
                                in_offset=bass.IndirectOffsetOnAxis(ap=fld4i[:, h, u, IDX0:IDX0 + 1], axis=0)
                            ).then_inc(s_got[h], 16)
                in_groups(pool, step)

            @block.scalar
            def _(act):
                def step(g0):
                    for h in range(Q):
                        act.wait_ge(s_fld[h], arrived(g0))
                        act.copy(R3[:, bass.ds(g0 * U + h * U, U), R_WGT:NR], fld4[:, h, :, WGT:POS2 + 1]).then_inc(s_kept, 1)
                in_groups(act, step)

            @block.vector
            def _(dve):
                f2 = fill2.rearrange("p (u r) -> p u r", u=FILL2)
                dve.memset(fill2, 0.0).then_inc(s_fill2, 1)
                dve.wait_ge(s_fill2, 1)
                dve.memset(f2[:, :, MLOC:MLOC + 1], -1.0).then_inc(s_fill2, 1)
                dve.memset(acc, 0.0).then_inc(s_zero, 1)
                dve.wait_ge(s_zero, 1)

                def one_hot(g, g0, h):
                    dve.wait_ge(s_fld[h], arrived(g0))
                    slot_free(dve, s_mm, g)
                    first = node0[:, bass.ds(g, 1)]
                    dve.tensor_scalar(rel3[:, h, :], fld4[:, h, :, KEY], first, None, ALU.subtract).then_inc(s_rel, 1)
                    dve.tensor_scalar(R3[:, bass.ds(g0 * U + h * U, U), R_DLOC], fld4[:, h, :, DST], first, None, ALU.subtract)
                    dve.wait_ge(s_rel, g + 1)
                    for u in range(U):
                        last = dve.tensor_scalar(hot4[:, h, u, :], iota[:, :], rel3[:, h, u:u + 1], None, ALU.is_equal)
                    last.then_inc(s_hot, 1)

                def parts(b, h):
                    return [(acc[:, bass.ds(b * (T * P), T * P)], ps[h][:, 0:T * P])]

                hot_then_add(dve, bucket_of[0], one_hot, parts, 0)

            @block.tensor
            def _(pe):
                def step(g0):
                    for h in range(Q):
                        pe.wait_ge(s_hot, g0 + (h + 1))
                        pe.wait_ge(s_got[h], arrived(g0, 16 * U))
                        slot_free(pe, s_acc, g0 + h)
                        for u in range(U):
                            last = pe.matmul(ps[h][:, 0:T * P], got4[:, h, u, :], hot4[:, h, u, :],
                                             start=(u == 0), stop=(u == U - 1))
                        last.then_inc(s_mm, 1)
                in_groups(pe, step)

        sq4, S = (cut(i * NB * D, NB * D)[0] for i in range(2))
        h4, rest4 = cut(3 * NB * D, NB * D)
        h43, S3, sq43 = wide(h4), wide(S), wide(sq4)

        def staged(n, width):
            nonlocal rest4
            c, rest4 = cut(rest4, n * width)
            return [c[:, k * width:(k + 1) * width] for k in range(n)]

        xst4, xTs4, acc_st = staged(BB, D), staged(BB, D), staged(BB, T * P)
        s_xs4 = sem("s_xs4")
        s_as4 = sem("s_as4")
        s_xT4 = sem("s_xT4")
        s_xTe4 = sem("s_xTe4")
        s_o4 = sem("s_o4")
        s_h4 = sem("s_h4")

        with nc.Block() as block:
            @block.tensor
            def _(pe):
                def batch(i, n):
                    for k in range(n):
                        pe.wait_ge(s_xs4, i * BB + (k + 1))
                        pe.transpose(ps[k][:, 0:P], xst4[k], ident[:, :]).then_inc(s_xT4, 1)
                    for k in range(n):
                        o = ps[BB + k][:, 0:T * D]
                        pe.wait_ge(s_as4, i * BB + (k + 1))
                        at_least(pe, s_h4, (i * BB + (k + 1 - BB)) * (2 * T))
                        for t in range(T):
                            pe.matmul(o, acc_st[k][:, t * P:(t + 1) * P], wnT[:, (t + 1) * T * D:(t + 2) * T * D],
                                      start=(t == 0), stop=False)
                        pe.wait_ge(s_xTe4, i * BB + (k + 1))
                        pe.matmul(o, xTs4[k], wnT[:, 0:T * D], start=False, stop=True).then_inc(s_o4, 1)
                in_batches(pe, batch)

            @block.scalar
            def _(act):
                def batch(i, n):
                    for k in range(n):
                        at_least(act, s_xT4, i * BB + (k + 1 - BB))
                        act.activation(xst4[k], X[:, bass.ds(i * (BB * D) + k * D, D)], ACT.Relu).then_inc(s_xs4, 1)
                    for k in range(n):
                        at_least(act, s_o4, i * BB + (k + 1 - BB))
                        act.copy(acc_st[k], acc[:, bass.ds(i * (BB * T * P) + k * (T * P), T * P)]).then_inc(s_as4, 1)
                    for k in range(n):
                        act.wait_ge(s_xT4, i * BB + (k + 1))
                        act.copy(xTs4[k], ps[k][:, 0:P]).then_inc(s_xTe4, 1)
                in_batches(act, batch)

            @block.vector
            def _(dve):
                chain.on(dve)
                chain.link(dve.tensor_scalar(h4, X[:, :], 2.0, None, ALU.mult))

                def batch(i, n):
                    for k in range(n):
                        h_b = h4[:, bass.ds(i * (BB * D) + k * D, D)]
                        for t in range(2 * T):
                            if t == T:
                                dve.wait_ge(s_o4, i * BB + (k + 1))
                            at_least(dve, s_h4, i * (BB * 2 * T) + (k * 2 * T + t))
                            row = (bnb if t < T else ps[BB + k])[:, (t % T) * D:(t % T + 1) * D]
                            to = {"accum_out": sm(0)[:, bass.ds(i * BB + k, 1)]} if t == 2 * T - 1 else {}
                            dve.scalar_tensor_tensor(h_b, row, nmask[:, bass.ds(i * BB + (k + (t % T) * NB), 1)], h_b,
                                                     ALU.mult, ALU.add, **to).then_inc(s_h4, 1)
                in_batches(dve, batch)

        s_x1 = sem("s_x1")
        s_xs5 = sem("s_xs5")
        s_xT5 = sem("s_xT5")
        s_xTe5 = sem("s_xTe5")
        s_o5 = sem("s_o5")
        s_S5 = sem("s_S5")
        s_sum5 = sem("s_sum5")
        before_products = []

        with nc.Block() as block:
            @block.vector
            def _(dve):
                chain.on(dve)
                link = chain.link
                dve.wait_ge(s_h4, 2 * T * NB)
                n2, norm, z, lo, hi, ser, sel, t0 = (sm(i) for i in range(3, 11))

                def logs():
                    link(dve.tensor_tensor(n2, sm(1), sm(2), ALU.mult))
                    link(dve.tensor_tensor(n2, n2, sm(2), ALU.mult))
                    chain.sqrt(n2, norm)
                    link(dve.tensor_scalar(norm, norm, MIN_NORM, None, ALU.max))
                    link(dve.tensor_scalar(z, norm, 1.0 - 1e-7, None, ALU.min))
                    link(dve.tensor_scalar(lo, z, -1.0, 1.0, ALU.mult, ALU.add))
                    link(dve.tensor_scalar(hi, z, 1.0, None, ALU.add))
                    chain.func(ACT.Ln, lo, lo)
                    chain.func(ACT.Ln, hi, hi)
                layer_norm(dve, link, h43, sq43, chain.sqrt, logs, summed=True)
                dve.sem_inc(s_x1, 1)
                before_products.append(len(chain.jobs))
                link(dve.tensor_tensor(hi, hi, lo, ALU.subtract))
                link(dve.tensor_scalar(hi, hi, 0.5, None, ALU.mult))
                link(dve.tensor_tensor(t0, z, z, ALU.mult))
                link(dve.tensor_scalar(ser, t0, 1.0 / 11, 1.0 / 9, ALU.mult, ALU.add))
                for c in (1.0 / 7, 1.0 / 5, 1.0 / 3, 1.0):
                    link(dve.tensor_tensor(ser, ser, t0, ALU.mult))
                    link(dve.tensor_scalar(ser, ser, c, None, ALU.add))
                link(dve.tensor_tensor(ser, ser, z, ALU.mult))
                link(dve.tensor_scalar(sel, z, 0.25, None, ALU.is_lt))
                link(dve.copy_predicated(hi, sel.bitcast(I32), ser))
                link(dve.reciprocal(norm, norm))
                link(dve.tensor_tensor(hi, hi, norm, ALU.mult))
                x2, xy, den, a = sm(3), sm(4), sm(5), sm(6)

                def batch(i, n):
                    for k in range(n):
                        dve.wait_ge(s_S5, i * BB + (k + 1))
                        at_least(dve, s_sum5, (i * BB + (k + 1 - BB)) * 2)
                        s_b = S[:, bass.ds(i * (BB * D) + k * D, D)]
                        at = bass.ds(i * BB + k, 1)
                        dve.scalar_tensor_tensor(sq4[:, k * D:(k + 1) * D], s_b, 1.0, s_b, ALU.mult, ALU.mult,
                                                 accum_out=x2[:, at]).then_inc(s_sum5, 1)
                        dve.scalar_tensor_tensor(sq4[:, (BB + k) * D:(BB + k + 1) * D], s_b, 1.0, b1b[:, :], ALU.mult, ALU.mult,
                                                 accum_out=xy[:, at]).then_inc(s_sum5, 1)
                in_batches(dve, batch)
                dve.wait_ge(s_sum5, 2 * NB)
                link(dve.tensor_tensor(xy, xy, hi, ALU.mult))
                link(dve.tensor_tensor(x2, x2, hi, ALU.mult))
                link(dve.tensor_tensor(x2, x2, hi, ALU.mult))
                bias3 = b1b[:, :].unsqueeze(1).to_broadcast([P, NB, D])
                link(dve.tensor_scalar(xy, xy, 2.0, 1.0, ALU.mult, ALU.add))
                link(dve.tensor_scalar(a, xy, y2, None, ALU.add))
                link(dve.tensor_scalar(den, x2, y2, None, ALU.mult))
                link(dve.tensor_tensor(den, den, xy, ALU.add))
                link(dve.tensor_scalar(den, den, MIN_NORM, None, ALU.max))
                link(dve.reciprocal(den, den))
                link(dve.tensor_tensor(a, a, den, ALU.mult))
                link(dve.tensor_tensor(a, a, hi, ALU.mult))
                link(dve.tensor_scalar(x2, x2, -1.0, 1.0, ALU.mult, ALU.add))
                link(dve.tensor_tensor(x2, x2, den, ALU.mult))
                link(dve.tensor_tensor(S3, S3, along(a), ALU.mult))
                link(dve.tensor_tensor(sq43, bias3, along(x2), ALU.mult))
                link(dve.tensor_tensor(S3, S3, sq43, ALU.add))
                sum_of_squares(dve, link, S3, sq43, den)
                chain.sqrt(den, a)
                link(dve.tensor_scalar(a, a, MIN_NORM, None, ALU.max))
                link(dve.reciprocal(a, a))
                link(dve.tensor_scalar(a, a, MAX_NORM, 1.0, ALU.mult, ALU.min))
                link(dve.tensor_tensor(S3, S3, along(a), ALU.mult))

            @block.scalar
            def _(act):
                chain.answer(act, 0, before_products[0])
                act.wait_ge(s_x1, 1)

                def batch(i, n):
                    for k in range(n):
                        at_least(act, s_xT5, i * BB + (k + 1 - BB))
                        act.copy(xst4[k], X[:, bass.ds(i * (BB * D) + k * D, D)]).then_inc(s_xs5, 1)
                    for k in range(n):
                        act.wait_ge(s_xT5, i * BB + (k + 1))
                        act.copy(xTs4[k], ps[k][:, 0:P]).then_inc(s_xTe5, 1)
                    for k in range(n):
                        act.wait_ge(s_o5, i * BB + (k + 1))
                        act.copy(S[:, bass.ds(i * (BB * D) + k * D, D)], ps[BB + k][:, 0:D]).then_inc(s_S5, 1)
                in_batches(act, batch)
                chain.answer(act, before_products[0])

            @block.tensor
            def _(pe):
                def batch(i, n):
                    for k in range(n):
                        pe.wait_ge(s_xs5, i * BB + (k + 1))
                        pe.transpose(ps[k][:, 0:P], xst4[k], ident[:, :]).then_inc(s_xT5, 1)
                    for k in range(n):
                        pe.wait_ge(s_xTe5, i * BB + (k + 1))
                        at_least(pe, s_S5, i * BB + (k + 1 - BB))
                        pe.matmul(ps[BB + k][:, 0:D], xTs4[k], w1s[:, :], start=True, stop=True).then_inc(s_o5, 1)
                in_batches(pe, batch)

        kept4, at = cut4(2 * NB * D, NR)
        hotw4, at = cut4(at, P)
        hotT4, at = cut4(at, P)
        msg4, at = cut4(at, MW)
        mrow, at = cut(at, Q * U)
        mrow3 = mrow.rearrange("p (q u) -> p q u", q=Q)
        midx, at = cut(at, Q * U)
        midx3 = midx.bitcast(I32).rearrange("p (q u) -> p q u", q=Q)
        s_ones5 = sem("s_ones5")
        s_keep_w = sem("s_keep_w")
        s_hot_w = sem("s_hot_w")
        s_fld_w = sem("s_fld_w")
        s_turned = sem("s_turned")
        s_turnedc = sem("s_turnedc")
        s_msg = sem("s_msg")
        s_msgc = sem("s_msgc")
        s_row_w = sems("s_row_w", Q)
        msg_rows = sorted_msgs.rearrange("p (t r) -> (p t) r", r=MW)

        def row_written(eng, g0, h):
            at_least(eng, s_row_w[h], g0 * (16 * U // Q))

        with nc.Block() as block:
            @block.vector
            def _(dve):
                dve.memset(msg4[:, :, :, MONE], 1.0).then_inc(s_ones5, 1)

                def step(g0):
                    for h in range(Q):
                        slot_free(dve, s_turned, g0 + h)
                        row_written(dve, g0, h)
                        dve.tensor_copy(kept4[:, h, :, :], R3[:, bass.ds(g0 * U + h * U, U), :]).then_inc(s_keep_w, 1)
                        dve.wait_ge(s_keep_w, g0 * 2 + (2 * h + 1))
                        dve.tensor_scalar(mrow3[:, h, :], kept4[:, h, :, R_DLOC], P - 0.5, float(OUTSIDE),
                                          ALU.is_gt, ALU.mult).then_inc(s_keep_w, 1)
                        for u in range(U):
                            last = dve.tensor_scalar(hotw4[:, h, u, :], iota[:, 0:P], kept4[:, h, u, R_DLOC:R_DLOC + 1],
                                                     kept4[:, h, u, R_WGT:R_WGT + 1], ALU.is_equal, ALU.mult)
                        last.then_inc(s_hot_w, 1)
                        dve.wait_ge(s_keep_w, g0 * 2 + (2 * h + 2))
                        dve.tensor_tensor(midx3[:, h, :], mrow3[:, h, :], kept4[:, h, :, R_POS2], ALU.add)
                        dve.tensor_copy(msg4[:, h, :, MLOC], kept4[:, h, :, R_SLOC]).then_inc(s_fld_w, 1)
                in_groups(dve, step)

            def turned_part(h):
                return ps[h][:, 0:U * P]

            def message_part(h):
                return ps[h][:, U * P:U * P + U * D]

            @block.tensor
            def _(pe):
                def turn(g, g0, h):
                    pe.wait_ge(s_hot_w, g + 1)
                    slot_free(pe, s_msgc, g)
                    for u in range(U):
                        last = pe.transpose(turned_part(h)[:, u * P:(u + 1) * P], hotw4[:, h, u, :], ident[:, :])
                    last.then_inc(s_turned, 1)

                def take(g, h, b):
                    pe.wait_ge(s_turnedc, g + 1)
                    for u in range(U):
                        last = pe.matmul(message_part(h)[:, u * D:(u + 1) * D], hotT4[:, h, u, :],
                                         S[:, bass.ds(b * D, D)], start=True, stop=True)
                    last.then_inc(s_msg, 1)

                two_steps(pe, mybir.EngineType.PE, bucket_of[0], turn, take)

            @block.scalar
            def _(act):
                def turned(g, g0, h):
                    act.wait_ge(s_turned, g + 1)
                    slot_free(act, s_msg, g)
                    act.copy(hotT4[:, h, :, :], turned_part(h).rearrange("p (u f) -> p u f", u=U)).then_inc(s_turnedc, 1)

                def taken(g, h, b):
                    act.wait_ge(s_msg, g + 1)
                    act.wait_ge(s_fld_w, g + 1)
                    act.copy(msg4[:, h, :, 0:D], message_part(h).rearrange("p (u f) -> p u f", u=U)).then_inc(s_msgc, 1)

                two_steps(act, None, None, turned, taken)

            @block.gpsimd
            def _(pool):
                beyond = pool.to_reg(P * MTP - 1)
                pool.wait_ge(s_ones5, 1)

                def step(g0):
                    for h in range(Q):
                        pool.wait_ge(s_msgc, g0 + (h + 1))
                        pool.sem_inc(s_turn, 1)
                        for u in range(U):
                            pool.indirect_dma_start(
                                out=msg_rows, out_offset=bass.IndirectOffsetOnAxis(ap=midx3[:, h, u:u + 1], axis=0),
                                in_=msg4[:, h, u, :], in_offset=None,
                                bounds_check=beyond, oob_is_err=False).then_inc(s_row_w[h], 16)
                in_groups(pool, step)
                for h in range(Q):
                    pool.wait_ge(s_row_w[h], STEPS * 16 * U)

        AW = D + 1
        acc7, at = cut(0, NB * AW)
        rec7, at = cut(at, MQ * MU * MW)
        rec74 = rec7.rearrange("p (q u r) -> p q u r", q=MQ, u=MU)
        hot7, at = cut(at, MQ * MU * P)
        hot74 = hot7.rearrange("p (q u r) -> p q u r", q=MQ, u=MU)
        s_zero7 = sem("s_zero7")
        s_rec7 = sems("s_rec7_", MQ // 2)
        s_off = sem("s_off")
        s_mm7 = sem("s_mm7")
        s_acc7 = sem("s_acc7")
        MLAG = MQ // 2
        VECTOR_SLOTS, POOL_SLOTS, SCALAR_SLOTS = (0, 3, 6), (1, 5), (2, 4, 7)
        hot_by = {}
        for name, slots in (("s_hot_v", VECTOR_SLOTS), ("s_hot_p", POOL_SLOTS), ("s_hot_s", SCALAR_SLOTS)):
            made = sem(name)
            for j, h in enumerate(slots):
                hot_by[h] = (made, len(slots), j + 1)

        def in_order(tiles):
            return iota[:, 0:P].unsqueeze(1).to_broadcast([P, tiles, P])

        def hot_of(col, tiles):
            return col.unsqueeze(2).to_broadcast([P, tiles, P])

        def messages_in(eng, s, h):
            eng.wait_ge(s_rec7[h // 2], s * 16 + 16)
            at_least(eng, s_mm7, s * MQ + (h + 1 - MQ))

        with nc.Block() as block:
            @block.sync
            def _(sp):
                def step(s):
                    for j in range(MQ // 2):
                        at_least(sp, s_mm7, s * MQ + (2 * j + 2 - MQ))
                        sp.dma_start(rec7[:, 2 * j * MU * MW:2 * (j + 1) * MU * MW],
                                     sorted_msgs[:, bass.ds(s * (MQ * MU * MW) + 2 * j * MU * MW, 2 * MU * MW)]
                                     ).then_inc(s_rec7[j], 16)
                in_steps(sp, MSTEPS, step)

            @block.gpsimd
            def _(pool):
                def step(s):
                    for h in POOL_SLOTS:
                        messages_in(pool, s, h)
                        pool.sem_inc(s_turn, 1)
                        for u in range(MU):
                            last = pool.tensor_scalar(hot74[:, h, u, :], iota[:, 0:P], rec74[:, h, u, MLOC:MLOC + 1],
                                                      None, ALU.is_equal)
                        last.then_inc(hot_by[h][0], 1)
                in_steps(pool, MSTEPS, step)

            @block.scalar
            def _(act):
                def step(s):
                    for j, h in enumerate(SCALAR_SLOTS):
                        messages_in(act, s, h)
                        for u in range(MU):
                            last = act.activation(hot74[:, h, u, :], iota[:, 0:P], ACT.Abs,
                                                  bias=rec74[:, h, u, MLOC:MLOC + 1], scale=-1.0)
                        last.then_inc(s_off, 1)
                        act.wait_ge(s_off, s * len(SCALAR_SLOTS) + (j + 1))
                        act.activation(hot74[:, h, :, :], hot74[:, h, :, :], ACT.Relu,
                                       bias=ones[:, 0:1], scale=-1.0).then_inc(hot_by[h][0], 1)
                in_steps(act, MSTEPS, step)

            @block.vector
            def _(dve):
                dve.memset(acc7, 0.0).then_inc(s_zero7, 1)
                dve.wait_ge(s_zero7, 1)

                def add(g, h, b):
                    dve.wait_ge(s_mm7, g + 1)
                    at_least(dve, s_acc7, g)
                    dve.tensor_tensor(acc7[:, bass.ds(b * AW, AW)], ps[h][:, 0:AW], acc7[:, bass.ds(b * AW, AW)],
                                      ALU.add).then_inc(s_acc7, 1)

                def step(s):
                    peeled = isinstance(s, int)
                    buckets = buckets_at(mybir.EngineType.DVE, bucket_of[1], 0 if peeled else s * MQ - MLAG,
                                         MLAG if peeled else MQ)
                    for h in range(MQ):
                        if h in VECTOR_SLOTS:
                            messages_in(dve, s, h)
                            dve.tensor_tensor(hot74[:, h, :, :], in_order(MU), hot_of(rec74[:, h, :, MLOC], MU),
                                              ALU.is_equal).then_inc(hot_by[h][0], 1)
                        if h >= MLAG or not peeled:
                            add(s * MQ + (h - MLAG), (h - MLAG) % MQ, buckets[h - MLAG if peeled else h])
                in_steps(dve, MSTEPS, step)
                buckets = buckets_at(mybir.EngineType.DVE, bucket_of[1], MNG - MLAG, MLAG)
                for h in range(MLAG):
                    add(MNG - MLAG + h, MQ - MLAG + h, buckets[h])

            @block.tensor
            def _(pe):
                def step(s):
                    for h in range(MQ):
                        made, per, nth = hot_by[h]
                        pe.wait_ge(made, s * per + nth)
                        at_least(pe, s_acc7, s * MQ + (h + 1 - MQ))
                        for u in range(MU):
                            last = pe.matmul(ps[h][:, 0:AW], hot74[:, h, u, :], rec74[:, h, u, 0:AW],
                                             start=(u == 0), stop=(u == MU - 1))
                        last.then_inc(s_mm7, 1)
                in_steps(pe, MSTEPS, step)

        top = big_words - 2 * NB * D
        sq8 = cut(top, NB * D)[0]
        h8 = cut(top + NB * D, NB * D)[0]
        sq83, h83 = wide(sq8), wide(h8)
        agg7 = acc7.rearrange("p (b f) -> p b f", b=NB)
        y = sq8
        dinv = small[:, 12 * NB:13 * NB]
        s_st8 = sem("s_st8")
        s_y8 = sem("s_y8")
        with nc.Block() as block:
            @block.vector
            def _(dve):
                chain.on(dve)
                link = chain.link
                raw, norm, th, f, ne = (sm(i) for i in range(3, 8))
                g = agg7[:, :, 0:D]
                sum_of_squares(dve, link, g, sq83, raw)
                chain.sqrt(raw, raw)
                link(dve.tensor_scalar(norm, raw, MIN_NORM, None, ALU.max))
                chain.func(ACT.Tanh, norm, th)
                link(dve.reciprocal(norm, norm))
                link(dve.tensor_tensor(f, th, norm, ALU.mult))
                link(dve.tensor_tensor(ne, f, raw, ALU.mult))
                link(dve.tensor_scalar(ne, ne, MIN_NORM, None, ALU.max))
                link(dve.reciprocal(ne, ne))
                link(dve.tensor_scalar(ne, ne, MAX_NORM, 1.0, ALU.mult, ALU.min))
                link(dve.tensor_tensor(f, f, ne, ALU.mult))
                link(dve.tensor_tensor(h83, g, along(f), ALU.mult))
                link(dve.tensor_tensor(h83, h83, X3, ALU.add))
                link(dve.tensor_scalar(dinv, agg7[:, :, D], 1.0, None, ALU.add))
                chain.sqrt(dinv, dinv)
                link(dve.reciprocal(dinv, dinv))

                def make_y():
                    link(dve.tensor_tensor(sm(3), sm(2), dinv, ALU.mult))
                    link(dve.tensor_tensor(wide(y), h83, along(sm(3)), ALU.mult))
                    dve.sem_inc(s_y8, 1)
                layer_norm(dve, link, h83, sq83, chain.sqrt, make_y)

            @block.scalar
            def _(act):
                chain.answer(act)

            @block.sync
            def _(sp):
                sp.wait_ge(s_y8, 1)
                sp.dma_start(table2.rearrange("(b p) f -> p b f", p=P), wide(y)).then_inc(s_st8, 16)
                sp.wait_ge(s_st8, 16)

        AW9 = D + 1
        acc9, at = cut(0, NB * AW9)
        got94, at = cut4(at, AW9)
        hot94, at = cut4(at, P)
        gidx, at = cut(at, Q * U)
        gidx3 = gidx.bitcast(I32).rearrange("p (q u) -> p q u", q=Q)
        assert at <= top
        s_zero9 = sem("s_zero9")
        s_idx = sem("s_idx")

        def gather_rows(pool, table, to, k):
            def step(g0):
                for h in range(Q):
                    pool.wait_ge(s_idx, g0 + (h + 1 + k * NG))
                    slot_free(pool, s_mm, g0 + h, (1 + k) * NG)
                    pool.sem_inc(s_turn, 1)
                    for u in range(U):
                        pool.indirect_dma_start(
                            out=to[:, h, u, 0:D], out_offset=None, in_=table,
                            in_offset=bass.IndirectOffsetOnAxis(ap=gidx3[:, h, u:u + 1], axis=0)
                        ).then_inc(s_got[h], 16)
            in_groups(pool, step)

        def index_and_hot(dve, hot, k):
            def one_hot(g, g0, h):
                slot_free(dve, s_mm, g, (1 + k) * NG)
                rows = bass.ds(g0 * U + h * U, U)
                dve.tensor_copy(gidx3[:, h, :], R3[:, rows, R_SRCF]).then_inc(s_idx, 1)
                dve.tensor_tensor(hot[:, h, :, :], in_order(U), hot_of(R3[:, rows, R_DLOC], U), ALU.is_equal).then_inc(s_hot, 1)
            return one_hot

        with nc.Block() as block:
            @block.gpsimd
            def _(pool):
                pool.wait_ge(s_zero9, 1)
                gather_rows(pool, table2, got94, 0)

            @block.vector
            def _(dve):
                dve.memset(got94[:, :, :, D], 1.0).then_inc(s_zero9, 1)
                acc93 = acc9.rearrange("p (b f) -> p b f", b=NB)
                dve.tensor_copy(acc93[:, :, 0:D], wide(y)).then_inc(s_zero9, 1)
                dve.memset(acc93[:, :, D:D + 1], 0.0).then_inc(s_zero9, 1)
                dve.wait_ge(s_zero9, 3)

                def parts(b, h):
                    return [(acc9[:, bass.ds(b * AW9, AW9)], ps[h][:, 0:AW9])]

                hot_then_add(dve, bucket_of[0], index_and_hot(dve, hot94, 0), parts, NG)

            @block.tensor
            def _(pe):
                def step(g0):
                    for h in range(Q):
                        pe.wait_ge(s_hot, g0 + (h + 1 + NG))
                        pe.wait_ge(s_got[h], arrived(g0, 16 * U, 1))
                        slot_free(pe, s_acc, g0 + h, NG)
                        for u in range(U):
                            last = pe.matmul(ps[h][:, 0:AW9], hot94[:, h, u, :], got94[:, h, u, :],
                                             start=(u == 0), stop=(u == U - 1))
                        last.then_inc(s_mm, 1)
                in_groups(pe, step)

        agg9 = acc9.rearrange("p (b f) -> p b f", b=NB)
        degn = small[:, 13 * NB:14 * NB]
        s_st10 = sem("s_st10")
        s_x3 = sem("s_x3")
        with nc.Block() as block:
            @block.vector
            def _(dve):
                chain.on(dve)
                link = chain.link
                link(dve.tensor_tensor(h83, agg9[:, :, 0:D], along(dinv), ALU.mult))
                link(dve.tensor_tensor(h83, h83, X3, ALU.add))
                layer_norm(dve, link, h83, sq83, chain.sqrt)
                dve.sem_inc(s_x3, 1)
                link(dve.tensor_scalar(degn, agg9[:, :, D], 1.0, None, ALU.max))
                chain.sqrt(degn, degn)
                link(dve.reciprocal(degn, degn))

            @block.scalar
            def _(act):
                chain.answer(act)

            @block.sync
            def _(sp):
                sp.wait_ge(s_x3, 1)
                sp.dma_start(table3.rearrange("(b p) f -> p b f", p=P), X3).then_inc(s_st10, 16)
                sp.wait_ge(s_st10, 16)

        accN, at = cut(0, NB * P)
        accE, at = cut(at, NB * P)
        got114, at = cut4(at, D)
        hot114, at = cut4(at, P)
        feat4, at = cut4(at, FE)
        gidx, at = cut(at, Q * U)
        gidx3 = gidx.bitcast(I32).rearrange("p (q u) -> p q u", q=Q)
        s_zero11 = sem("s_zero11")
        s_feat_g = sems("s_feat_g", Q)
        s_feat_s = sems("s_feat_s", Q)
        with nc.Block() as block:
            @block.sync
            def _(sp):
                def step(g0):
                    first = registers(mybir.EngineType.SP, given_from, g0, Q, E - GE)
                    given = registers(mybir.EngineType.SP, as_given, g0, Q, 1)
                    for h in range(Q):
                        slot_free(sp, s_mm, g0 + h, 2 * NG)
                        sp.dma_start(feat4[:, h, :, :], attr[bass.ds(first[h], GE), :]
                                     .rearrange("(p u) r -> p u r", u=U), cond=given[h]).then_inc(s_feat_g[h], 16)
                in_groups(sp, step)

            @block.scalar
            def _(act):
                act.wait_ge(s_feats, 16)

                def step(g0):
                    first = registers(mybir.EngineType.Activation, start_of, g0, Q, E)
                    given = registers(mybir.EngineType.Activation, as_given, g0, Q, 1)
                    for h in range(Q):
                        not_given = act.snap(1 - given[h])
                        slot_free(act, s_mm, g0 + h, 2 * NG)
                        act.dma_start(feat4[:, h, :, :], edge_feats[bass.ds(first[h], GE), :]
                                      .rearrange("(p u) r -> p u r", u=U), cond=not_given).then_inc(s_feat_s[h], 16)
                in_groups(act, step)

            @block.gpsimd
            def _(pool):
                gather_rows(pool, table3, got114, 1)

            @block.vector
            def _(dve):
                dve.memset(accN, 0.0).then_inc(s_zero11, 1)
                dve.memset(accE[0:FE, :], 0.0).then_inc(s_zero11, 1)
                dve.wait_ge(s_zero11, 2)

                def parts(b, h):
                    return [(accN[:, bass.ds(b * P, P)], ps[h][:, 0:P]),
                            (accE[0:FE, bass.ds(b * P, P)], ps[h][0:FE, P:2 * P])]

                hot_then_add(dve, bucket_of[0], index_and_hot(dve, hot114, 1), parts, 2 * NG)

            @block.tensor
            def _(pe):
                def step(g0):
                    for h in range(Q):
                        pe.wait_ge(s_hot, g0 + (h + 1 + 2 * NG))
                        pe.wait_ge(s_feat_g[h], arrived(g0))
                        pe.wait_ge(s_feat_s[h], arrived(g0))
                        slot_free(pe, s_acc, g0 + h, 2 * NG)
                        for u in range(U):
                            pe.matmul(ps[h][0:FE, P:2 * P], feat4[:, h, u, :], hot114[:, h, u, :],
                                      start=(u == 0), stop=(u == U - 1))
                        pe.wait_ge(s_got[h], arrived(g0, 16 * U, 2))
                        for u in range(U):
                            last = pe.matmul(ps[h][:, 0:P], got114[:, h, u, :], hot114[:, h, u, :],
                                             start=(u == 0), stop=(u == U - 1))
                        last.then_inc(s_mm, 1)
                in_groups(pe, step)

        h12 = cut(2 * NB * P, NB * D)[0]
        sq12 = cut(3 * NB * P, NB * D)[0]
        h123, sq123 = wide(h12), wide(sq12)
        n_st = [cut(4 * NB * P + 2 * k * P, P)[0] for k in range(BB)]
        e_st = [cut(4 * NB * P + (2 * k + 1) * P, P)[0] for k in range(BB)]
        s_st12 = sem("s_st12")
        s_o12 = sem("s_o12")
        s_h12 = sem("s_h12")
        s_r12 = sem("s_r12")
        s_out = sem("s_out")
        s_x4 = sem("s_x4")
        with nc.Block() as block:
            @block.tensor
            def _(pe):
                def batch(i, n):
                    for k in range(n):
                        pe.wait_ge(s_st12, i * (2 * BB) + (2 * k + 2))
                        at_least(pe, s_h12, i * BB + (k + 1 - BB))
                        pe.matmul(ps[k][:, 0:D], n_st[k], w3s[:, :], start=True, stop=False)
                        pe.matmul(ps[k][:, 0:D], e_st[k][0:FE, :], w3ew[:, :],
                                  start=False, stop=True).then_inc(s_o12, 1)
                in_batches(pe, batch)

            @block.vector
            def _(dve):
                chain.on(dve)
                link = chain.link

                def batch(i, n):
                    for k in range(n):
                        dve.wait_ge(s_o12, i * BB + (k + 1))
                        here = bass.ds(i * (BB * D) + k * D, D)
                        dve.scalar_tensor_tensor(h12[:, here], ps[k][:, 0:D],
                                                 degn[:, bass.ds(i * BB + k, 1)], b3b[:, :],
                                                 ALU.mult, ALU.add).then_inc(s_h12, 1)
                    for k in range(n):
                        here = bass.ds(i * (BB * D) + k * D, D)
                        dve.wait_ge(s_h12, i * BB + (k + 1))
                        dve.scalar_tensor_tensor(h12[:, here], h12[:, here], 0.0, X[:, here], ALU.max, ALU.add,
                                                 accum_out=sm(0)[:, bass.ds(i * BB + k, 1)]).then_inc(s_r12, 1)
                in_batches(dve, batch)
                dve.wait_ge(s_r12, NB)
                layer_norm(dve, link, h123, sq123, chain.sqrt, summed=True)
                dve.sem_inc(s_x4, 1)

            @block.scalar
            def _(act):
                def batch(i, n):
                    for k in range(n):
                        at_least(act, s_o12, i * BB + (k + 1 - BB))
                        act.copy(n_st[k], accN[:, bass.ds(i * (BB * P) + k * P, P)]).then_inc(s_st12, 1)
                        act.copy(e_st[k][0:FE, :], accE[0:FE, bass.ds(i * (BB * P) + k * P, P)]).then_inc(s_st12, 1)
                in_batches(act, batch)
                chain.answer(act)

            @block.sync
            def _(sp):
                sp.wait_ge(s_x4, 1)
                sp.dma_start(out[0:NFULL * P, :].rearrange("(b p) f -> p b f", p=P), X3[:, 0:NFULL, :]).then_inc(s_out, 16)
                sp.dma_start(out[NFULL * P:N, :], X3[0:NREST, NFULL, :]).then_inc(s_out, 16)
                sp.wait_ge(s_out, 32)


INPUTS = ["x", "src", "dst", "edge_attr_64", "edge_type_3", "edge_weight", "node_type_3", "L0_gnn_W_e", "L0_gnn_b_e",
        "L0_gnn_W_n", "L0_gnn_b_n", "L1_gnn_weight", "L1_gnn_bias", "L3_gnn_weight", "L3_gnn_weight_edge", "L3_gnn_bias"]


def kernel(**inputs):
    import numpy as np
    import concourse.bacc as bacc
    from concourse.bass_utils import run_bass_kernel_spmd as run

    nc = bacc.Bacc("TRN2", target_bir_lowering=False, num_devices=1)
    arrays, args = {}, []
    for name in INPUTS:
        a = np.ascontiguousarray(inputs[name])
        arrays[f"in_{name}"] = a
        args.append(nc.dram_tensor(f"in_{name}", a.shape, mybir.dt.from_np(a.dtype), kind="ExternalInput").ap())
    out = nc.dram_tensor("out", (N, D), F32, kind="ExternalOutput").ap()
    build(nc, *args, out)
    return run(nc, [arrays], core_ids=[0]).results[0]["out"]
```
